# Optimizing a Trainium2 kernel written in Bass

```python
import numpy as np
import jax
import jax.numpy as jnp

def _softmax(x, axis=-1):
    return jax.nn.softmax(x, axis=axis)

def _gelu(x):
    return jax.nn.gelu(x, approximate=True)

def _silu(x):
    return jax.nn.silu(x)

def _sigmoid(x):
    return jax.nn.sigmoid(x)

def _layernorm(x, axis=-1, eps=1e-05):
    m = jnp.mean(x, axis=axis, keepdims=True)
    v = jnp.var(x, axis=axis, keepdims=True)
    return (x - m) / jnp.sqrt(v + eps)

def _scatter_add(tgt, idx, src, axis=0):
    return tgt.at[idx].add(src)

def _segment_sum(src, seg, n):
    return jax.ops.segment_sum(src, seg, n)
kernel_name = 'mk_gnn_ffn_d1_gnn_r8_2cc276'

def setup_inputs(seed: int=0):
    np.random.seed(seed)
    _w = jnp.asarray

    def _rec_inputs():
        import jax
        import jax.numpy as jnp
        _gk = jax.random.key(seed)
        x = -0.0003713 + 1 * jax.random.normal(jax.random.fold_in(_gk, 1), (6250, 256), jnp.float32)
        src = jax.random.randint(jax.random.fold_in(_gk, 2), (100000,), 0, 6250, jnp.int32)
        dst = jax.random.randint(jax.random.fold_in(_gk, 3), (100000,), 0, 6250, jnp.int32)
        _o = jnp.argsort(dst, stable=True)
        src = src[_o]
        dst = dst[_o]
        return (x, src, dst)
    x, src, dst = _rec_inputs()

    def _L0_gnn_setup():
        import jax, jax.numpy as jnp
        import numpy as np
        from jax.ops import segment_max, segment_sum
        N_NODES = 6250
        N_EDGES = 100000
        IN_CH = 256
        HEADS = 8
        OUT_CH = 32
        NEG_SLOPE = 0.2
        EPS = 1e-16
        key = jax.random.key(seed)
        k1, k2, k3, k4, k5 = jax.random.split(key, 5)
        x = jax.random.normal(k1, (N_NODES, IN_CH), dtype=jnp.float32)
        edge_index = jax.random.randint(k2, (2, N_EDGES), 0, N_NODES, dtype=jnp.int64)
        W = jax.random.normal(k3, (HEADS * OUT_CH, IN_CH), dtype=jnp.float32) * (1.0 / np.sqrt(IN_CH))
        a_left = jax.random.normal(k4, (HEADS, OUT_CH), dtype=jnp.float32) * (1.0 / np.sqrt(OUT_CH))
        a_right = jax.random.normal(k5, (HEADS, OUT_CH), dtype=jnp.float32) * (1.0 / np.sqrt(OUT_CH))
        return {'x': x, 'edge_index': edge_index, 'W': W, 'a_left': a_left, 'a_right': a_right}
    _L0_gnn_all = _L0_gnn_setup()
    _L0_gnn_in = {k: v for k, v in _L0_gnn_all.items() if k in ('W', 'a_left', 'a_right')}
    del _L0_gnn_all

    def _L0_ffn_setup():
        import jax, jax.numpy as jnp
        import numpy as np
        B, N, D = (16, 512, 256)
        NUM_EXPERTS, TOP_K, HEADS = (4, 2, 4)
        N_EDGES = 131072
        LN_EPS = 1e-05

        def _layernorm(x, g, b):
            mu = x.mean(-1, keepdims=True)
            var = ((x - mu) ** 2).mean(-1, keepdims=True)
            return (x - mu) * jax.lax.rsqrt(var + LN_EPS) * g + b

        def _forward(x, edge_index, W_gat, att_src, att_dst, b_gat, ln_gamma, ln_beta, W1, b1, W2, b2):
            Bc, Nc, Dc = x.shape
            M = Bc * Nc
            x_flat = x.reshape(M, Dc)
            h = (x_flat @ W_gat).reshape(M, HEADS, NUM_EXPERTS)
            loops = jnp.arange(M, dtype=edge_index.dtype)
            src = jnp.concatenate([edge_index[0], loops])
            dst = jnp.concatenate([edge_index[1], loops])
            a_src = (h * att_src).sum(-1)
            a_dst = (h * att_dst).sum(-1)
            e = jax.nn.leaky_relu(a_src[src] + a_dst[dst], negative_slope=0.2)
            e_max = jax.ops.segment_max(e, dst, num_segments=M)
            ee = jnp.exp(e - e_max[dst])
            denom = jax.ops.segment_sum(ee, dst, num_segments=M)
            alpha = ee / (denom[dst] + 1e-16)
            msg = h[src] * alpha[:, :, None]
            agg = jax.ops.segment_sum(msg, dst, num_segments=M).reshape(M, HEADS * NUM_EXPERTS) + b_gat
            scores = _layernorm(agg, ln_gamma, ln_beta).reshape(M, HEADS, NUM_EXPERTS).mean(1)
            scores = scores.reshape(Bc, Nc, NUM_EXPERTS)
            topk_s, topk_i = jax.lax.top_k(scores, TOP_K)
            w = jax.nn.softmax(topk_s, axis=-1)
            out = jnp.zeros_like(x)
            for ei in range(NUM_EXPERTS):
                g = jnp.where(topk_i == ei, w, 0.0).sum(-1)
                hh = jax.nn.gelu(x @ W1[ei] + b1[ei], approximate=False)
                out = out + g[..., None] * (hh @ W2[ei] + b2[ei])
            return out
        key = jax.random.key(seed)
        ks = jax.random.split(key, 8)
        s = 0.05
        return {'x': jax.random.normal(ks[0], (B, N, D), jnp.float32), 'W_gat': jax.random.normal(ks[1], (D, HEADS * NUM_EXPERTS), jnp.float32) * s, 'att_src': jax.random.normal(ks[2], (HEADS, NUM_EXPERTS), jnp.float32) * s, 'att_dst': jax.random.normal(ks[3], (HEADS, NUM_EXPERTS), jnp.float32) * s, 'b_gat': jnp.zeros((HEADS * NUM_EXPERTS,), jnp.float32), 'ln_gamma': jnp.ones((HEADS * NUM_EXPERTS,), jnp.float32), 'ln_beta': jnp.zeros((HEADS * NUM_EXPERTS,), jnp.float32), 'W1': jax.random.normal(ks[4], (NUM_EXPERTS, D, 2 * D), jnp.float32) * s, 'b1': jnp.zeros((NUM_EXPERTS, 2 * D), jnp.float32), 'W2': jax.random.normal(ks[5], (NUM_EXPERTS, 2 * D, D), jnp.float32) * s, 'b2': jnp.zeros((NUM_EXPERTS, D), jnp.float32), 'edge_index': jax.random.randint(ks[6], (2, N_EDGES), 0, B * N, jnp.int32)}
    _L0_ffn_all = _L0_ffn_setup()
    _L0_ffn_in = {k: v for k, v in _L0_ffn_all.items() if k in ('W_gat', 'att_src', 'att_dst', 'b_gat', 'ln_gamma', 'ln_beta', 'W1', 'b1', 'W2', 'b2', 'edge_index')}
    del _L0_ffn_all
    return {'x': x, 'src': src, 'dst': dst, 'L0_gnn_W': _L0_gnn_in['W'], 'L0_gnn_a_left': _L0_gnn_in['a_left'], 'L0_gnn_a_right': _L0_gnn_in['a_right'], 'L0_ffn_W_gat': _L0_ffn_in['W_gat'], 'L0_ffn_att_src': _L0_ffn_in['att_src'], 'L0_ffn_att_dst': _L0_ffn_in['att_dst'], 'L0_ffn_b_gat': _L0_ffn_in['b_gat'], 'L0_ffn_ln_gamma': _L0_ffn_in['ln_gamma'], 'L0_ffn_ln_beta': _L0_ffn_in['ln_beta'], 'L0_ffn_W1': _L0_ffn_in['W1'], 'L0_ffn_b1': _L0_ffn_in['b1'], 'L0_ffn_W2': _L0_ffn_in['W2'], 'L0_ffn_b2': _L0_ffn_in['b2'], 'L0_ffn_edge_index': _L0_ffn_in['edge_index']}

def reference(x, src, dst, L0_gnn_W, L0_gnn_a_left, L0_gnn_a_right, L0_ffn_W_gat, L0_ffn_att_src, L0_ffn_att_dst, L0_ffn_b_gat, L0_ffn_ln_gamma, L0_ffn_ln_beta, L0_ffn_W1, L0_ffn_b1, L0_ffn_W2, L0_ffn_b2, L0_ffn_edge_index):
    import jax
    import jax.numpy as jnp

    def _L0_gnn_ref(x, edge_index, W, a_left, a_right):
        import jax, jax.numpy as jnp
        import numpy as np
        from jax.ops import segment_max, segment_sum
        N_NODES = 6250
        N_EDGES = 100000
        IN_CH = 256
        HEADS = 8
        OUT_CH = 32
        NEG_SLOPE = 0.2
        EPS = 1e-16
        N = x.shape[0]
        H, C = (HEADS, OUT_CH)
        loops = jnp.arange(N, dtype=edge_index.dtype)
        src = jnp.concatenate([edge_index[0], loops])
        dst = jnp.concatenate([edge_index[1], loops])
        Wh = (x @ W.T).reshape(N, H, C)
        e_left = jnp.einsum('nhc,hc->nh', Wh, a_left)
        e_right = jnp.einsum('nhc,hc->nh', Wh, a_right)
        e = e_left[src] + e_right[dst]
        e = jnp.where(e >= 0, e, NEG_SLOPE * e)
        e_max = segment_max(e, dst, num_segments=N)
        e_max = jnp.where(jnp.isfinite(e_max), e_max, 0.0)
        e_exp = jnp.exp(e - e_max[dst])
        denom = segment_sum(e_exp, dst, num_segments=N)
        alpha = e_exp / (denom[dst] + EPS)
        out = segment_sum(Wh[src] * alpha[:, :, None], dst, num_segments=N)
        return out.reshape(N, H * C)

    def _L0_ffn_ref(x, W_gat, att_src, att_dst, b_gat, ln_gamma, ln_beta, W1, b1, W2, b2, edge_index):
        import jax, jax.numpy as jnp
        import numpy as np
        B, N, D = (16, 512, 256)
        NUM_EXPERTS, TOP_K, HEADS = (4, 2, 4)
        N_EDGES = 131072
        LN_EPS = 1e-05

        def _layernorm(x, g, b):
            mu = x.mean(-1, keepdims=True)
            var = ((x - mu) ** 2).mean(-1, keepdims=True)
            return (x - mu) * jax.lax.rsqrt(var + LN_EPS) * g + b

        def _forward(x, edge_index, W_gat, att_src, att_dst, b_gat, ln_gamma, ln_beta, W1, b1, W2, b2):
            Bc, Nc, Dc = x.shape
            M = Bc * Nc
            x_flat = x.reshape(M, Dc)
            h = (x_flat @ W_gat).reshape(M, HEADS, NUM_EXPERTS)
            loops = jnp.arange(M, dtype=edge_index.dtype)
            src = jnp.concatenate([edge_index[0], loops])
            dst = jnp.concatenate([edge_index[1], loops])
            a_src = (h * att_src).sum(-1)
            a_dst = (h * att_dst).sum(-1)
            e = jax.nn.leaky_relu(a_src[src] + a_dst[dst], negative_slope=0.2)
            e_max = jax.ops.segment_max(e, dst, num_segments=M)
            ee = jnp.exp(e - e_max[dst])
            denom = jax.ops.segment_sum(ee, dst, num_segments=M)
            alpha = ee / (denom[dst] + 1e-16)
            msg = h[src] * alpha[:, :, None]
            agg = jax.ops.segment_sum(msg, dst, num_segments=M).reshape(M, HEADS * NUM_EXPERTS) + b_gat
            scores = _layernorm(agg, ln_gamma, ln_beta).reshape(M, HEADS, NUM_EXPERTS).mean(1)
            scores = scores.reshape(Bc, Nc, NUM_EXPERTS)
            topk_s, topk_i = jax.lax.top_k(scores, TOP_K)
            w = jax.nn.softmax(topk_s, axis=-1)
            out = jnp.zeros_like(x)
            for ei in range(NUM_EXPERTS):
                g = jnp.where(topk_i == ei, w, 0.0).sum(-1)
                hh = jax.nn.gelu(x @ W1[ei] + b1[ei], approximate=False)
                out = out + g[..., None] * (hh @ W2[ei] + b2[ei])
            return out
        return _forward(x, edge_index, W_gat, att_src, att_dst, b_gat, ln_gamma, ln_beta, W1, b1, W2, b2)
    edge_index = jnp.stack([src, dst])
    x = x + _L0_gnn_ref(_layernorm(x, axis=-1), edge_index, L0_gnn_W, L0_gnn_a_left, L0_gnn_a_right)
    x = x + _L0_ffn_ref(_layernorm(x, axis=-1)[None], L0_ffn_W_gat, L0_ffn_att_src, L0_ffn_att_dst, L0_ffn_b_gat, L0_ffn_ln_gamma, L0_ffn_ln_beta, L0_ffn_W1, L0_ffn_b1, L0_ffn_W2, L0_ffn_b2, L0_ffn_edge_index)[0]
    return x

_drawn_inputs = setup_inputs


def setup_inputs(seed=0):
    import zlib

    import numpy as np

    out = dict(_drawn_inputs(seed))
    spreads = {'L0_ffn_b_gat': (0.0, 0.1),
     'L0_ffn_ln_gamma': (1.0, 0.2),
     'L0_ffn_ln_beta': (0.0, 0.1),
     'L0_ffn_b1': (0.0, 0.1),
     'L0_ffn_b2': (0.0, 0.1)}
    factors = {}
    for name, (base, spread) in spreads.items():
        noise = np.random.default_rng([zlib.crc32(name.encode()), seed]).standard_normal(out[name].shape)
        drawn = base * np.exp(spread * noise) if base else spread * noise
        out[name] = jnp.asarray(drawn.astype(out[name].dtype))
    for name, factor in factors.items():
        out[name] = (out[name] * factor).astype(out[name].dtype)
    return out
```

```python
import concourse.bass as bass
from concourse import mybir
from contextlib import ExitStack

P = 128
N_NODES, D = 6250, 256
TILES = -(-N_NODES // P)
LAST_ROWS = N_NODES - (TILES - 1) * P
NODES_PAD = TILES * P
SLOT = 256
CHUNKS = SLOT // P
SPI = 8
HALF = SPI // 2
G_HEADS, G_CH = 8, 32
F_HEADS, F_CH = 4, 4
EXPERTS, HID = 4, 512
FB = HID // P
G_EDGES, F_EDGES = 100000, 131072
G_CHUNK_ROWS = -(-G_EDGES // SLOT)
G_ITERS = -(-(G_CHUNK_ROWS + TILES - 1) // SPI)
G_SLOTS = G_ITERS * SPI
G_PAD_ROWS = G_SLOTS - (TILES - 1)
G_PAD = G_PAD_ROWS * SLOT
F_ITERS = (F_EDGES + TILES * (SLOT - 1)) // SLOT // SPI
F_SLOTS = F_ITERS * SPI
assert F_SLOTS >= (F_EDGES + TILES * (SLOT - 1)) // SLOT
ALL_SLOTS = G_SLOTS + F_SLOTS
G_BLOCKS, F_BLOCKS = -(-G_SLOTS // P), -(-F_SLOTS // P)
EPP = F_EDGES // P
SC_HALF = -(-EPP // (2 * G_ITERS))
SC_COLS = 2 * SC_HALF * G_ITERS
LIST_LEN = F_BLOCKS * P * SLOT
TRASH = LIST_LEN
LIST_ALL = LIST_LEN + SC_COLS * P
SRC_BITS = 13
SRC_SPAN = 1 << SRC_BITS
FAR = 8000
BIG = 2.0 ** 100
SLOPE = 0.2
DEN_EPS = 1e-16
LN_EPS = 1e-5


class Gat:
    def __init__(self, heads, ch, first_iter, iters):
        self.H, self.C = heads, ch
        self.HC = heads * ch
        self.A = heads * (ch + 1)
        self.EL = self.HC
        self.SPL = self.HC + heads
        self.W = self.SPL + (3 * heads + 1) // 2
        self.i0, self.i1 = first_iter, first_iter + iters
        self.HB = min(heads, 4)


GNN = Gat(G_HEADS, G_CH, 0, G_ITERS)
FFN = Gat(F_HEADS, F_CH, G_ITERS, F_ITERS)


def build(nc, x, src, dst, g_w, a_left, a_right, w_gat, att_src, att_dst, b_gat, ln_gamma, ln_beta,
          w1, b1, w2, b2, edge_index, out, dbg=None):
    f32, bf16, i32 = mybir.dt.float32, mybir.dt.bfloat16, mybir.dt.int32
    ALU, ACT, AX = mybir.AluOpType, mybir.ActivationFunctionType, mybir.AxisListType
    ctx = ExitStack()
    with ctx:
        def sb(name, shape, dt=f32):
            return ctx.enter_context(nc.sbuf_tensor(name, shape, dt))

        def pb(name, shape, dt=f32):
            return ctx.enter_context(nc.psum_tensor(name, shape, dt))

        def sem(name):
            return ctx.enter_context(nc.semaphore(name))

        def dram(name, shape, dt):
            return nc.dram_tensor(name, shape, dt, kind="Internal").ap()

        g_table = dram("g_table", (NODES_PAD, GNN.W), f32)
        f_table = dram("f_table", (NODES_PAD, FFN.W), f32)
        src_rows = dram("src_rows", (G_PAD_ROWS, SLOT), i32)
        dst_rows = dram("dst_rows", (G_PAD_ROWS, SLOT), i32)
        f_list = dram("f_list", (LIST_ALL, 1), i32)

        X = sb("X", [P, TILES, D])
        ACC = sb("ACC", [P, TILES, G_HEADS, G_CH + 1])
        EM = sb("EM", [P, TILES, 2 * G_HEADS])
        ACC2 = sb("ACC2", [P, TILES, F_HEADS, F_CH + 1])
        EM2 = sb("EM2", [P, TILES, 2 * F_HEADS])
        TROW = sb("TROW", [1, ALL_SLOTS], i32)
        ROW = sb("ROW", [P, P])
        ROWI = sb("ROWI", [P, P], i32)
        COL = sb("COL", [P, 1])
        COLI = sb("COLI", [P, 1], i32)
        IDF = sb("IDF", [P, P])
        IDB = sb("IDB", [P, P], bf16)
        ONES = sb("ONES", [P, P])
        UPPER = sb("UPPER", [P, P])
        SEL = sb("SEL", [3 * G_HEADS, G_HEADS, P], bf16)
        SEL2 = sb("SEL2", [3 * F_HEADS, F_HEADS, P], bf16)
        IDXB = sb("IDXB", [P, 2, HALF, CHUNKS], i32)
        POSB = sb("POSB", [P, 2, SC_HALF], i32)
        RECB = sb("RECB", [P, 2, SC_HALF], i32)
        TICK = sb("TICK", [P, 4])
        U1 = sb("U1", [P, G_HEADS])
        U2 = sb("U2", [P, G_HEADS])
        U3 = sb("U3", [P, G_HEADS])
        TB = sb("TB", [P, 2, 2 * G_HEADS])
        DLT = sb("DLT", [P, 2, G_HEADS])
        AL = sb("AL", [P, 4, G_HEADS])
        L1 = sb("L1", [P, CHUNKS, G_HEADS])
        L2 = sb("L2", [P, CHUNKS, G_HEADS])
        L3 = sb("L3", [P, CHUNKS, G_HEADS])
        LG = sb("LG", [P, 2, CHUNKS, G_HEADS])
        TMPA = sb("TMPA", [P, GNN.A])
        STAT = sb("STAT", [P, TILES, 6])
        MEAN = sb("MEAN", [P, TILES])
        VAR = sb("VAR", [P, TILES])
        RSTD = sb("RSTD", [P, TILES])
        ELR = sb("ELR", [P, TILES, 2 * G_HEADS])
        TCOLS = sb("TCOLS", [P, TILES * FFN.W])
        ET = TCOLS[:, 0:TILES * (GNN.W - GNN.HC)].rearrange("p (t w) -> p t w", t=TILES)
        FT = TCOLS[:, :].rearrange("p (t w) -> p t w", t=TILES)
        WREG = sb("WREG", [P, 2 * D + 2 * (D + 2 * G_HEADS)])
        WSB = WREG[:, 0:2 * D].rearrange("p (b d) -> p b d", b=2)
        WA = WREG[:, 2 * D:].rearrange("p (b d) -> p b d", b=2)
        S4 = WREG[:, 0:4 * TILES * 4].rearrange("p (a t e) -> p a t e", a=4, t=TILES)
        ACOL = sb("ACOL", [P, 2, 2])
        ADIAG = sb("ADIAG", [P, 2, 2 * G_HEADS])
        WGAT = sb("WGAT", [P, 2, F_HEADS * F_CH])
        HF = sb("HF", [P, TILES, F_HEADS * F_CH])
        ROWS16 = sb("ROWS16", [P, 5, F_HEADS * F_CH])
        B1R = sb("B1R", [EXPERTS * FB, P])
        B1C = sb("B1C", [P, EXPERTS * FB])
        G4 = sb("G4", [P, TILES, EXPERTS])
        S16A = sb("S16A", [P, TILES, 16])
        S16B = sb("S16B", [P, TILES, 16])
        S1 = sb("S1", [P, 4, TILES])
        LI = sb("LI", [P, 2, SLOT], i32)
        LF = sb("LF", [P, 2, SLOT])
        CNT = sb("CNT", [P, TILES])
        CNT2 = sb("CNT2", [P, TILES])
        Q = sb("Q", [P, TILES])
        QI = sb("QI", [P, TILES], i32)
        THR = sb("THR", [P, TILES])
        BASE = sb("BASE", [P, TILES])
        SLOT0 = sb("SLOT0", [P, TILES + 1])
        NSL = sb("NSL", [P, TILES])
        ZERO = sb("ZERO", [P, TILES])
        TCOL = sb("TCOL", [P, G_BLOCKS + F_BLOCKS])
        CCOL = sb("CCOL", [P, G_BLOCKS])
        CIDX = sb("CIDX", [P, G_BLOCKS], i32)
        SCOL = sb("SCOL", [P, 1])
        JUNK = sb("JUNK", [P, 64])

        sizes = [2 * ALL_SLOTS, 2 * ALL_SLOTS, SC_COLS, SC_COLS, SPI * CHUNKS * GNN.W, 4 * SLOT, SLOT, 2 * SLOT, SLOT,
                 2 * CHUNKS * GNN.A]
        LOOP = sb("LOOP", [P, sum(sizes)])
        at = [sum(sizes[:k]) for k in range(len(sizes) + 1)]
        part = [LOOP[:, at[k]:at[k + 1]] for k in range(len(sizes))]
        IDX = part[0].bitcast(i32).rearrange("p (g k) -> p g k", k=CHUNKS)
        DL = part[1].rearrange("p (g k) -> p g k", k=CHUNKS)
        POS = part[2].bitcast(i32)
        REC = part[3].bitcast(i32)
        R = part[4].rearrange("p (s k w) -> p s k w", s=SPI, k=CHUNKS)
        SF = part[5].rearrange("p (s k n) -> p s k n", s=4, k=CHUNKS)
        NE = part[6].bitcast(bf16).rearrange("p (s k n) -> p s k n", s=2, k=CHUNKS)
        ST = part[7].rearrange("p (s k n) -> p s k n", s=2, k=CHUNKS)
        ELT = part[8].bitcast(bf16)[0:3 * G_HEADS].rearrange("p (s k n) -> p s k n", s=2, k=CHUNKS)
        MSG = part[9].rearrange("p (s k a) -> p s k a", s=2, k=CHUNKS)
        XN = part[5][:, 0:2 * D].rearrange("p (r d) -> p r d", r=2)
        XT = part[5][:, 2 * D:4 * D].rearrange("p (r k n) -> p r k n", r=2, k=2)
        STG = part[9][:, 0:2 * (D + 2 * G_HEADS)].rearrange("p (r d) -> p r d", r=2)
        w_at = [0, EXPERTS * 2 * HID, EXPERTS * FB * D, FB * 4 * P, 4 * D, EXPERTS * D]
        w_at = [sum(w_at[:k + 1]) for k in range(len(w_at))]
        assert w_at[-1] <= at[-1]
        W1S = LOOP[:, w_at[0]:w_at[1]].rearrange("p (e k n) -> p e k n", e=EXPERTS, k=2)
        W2S = LOOP[:, w_at[1]:w_at[2]].rearrange("p (e f n) -> p e f n", e=EXPERTS, f=FB)
        HH = LOOP[:, w_at[2]:w_at[3]].rearrange("p (f n) -> p f n", f=FB)
        OUTS = LOOP[:, w_at[3]:w_at[4]].rearrange("p (j n) -> p j n", n=D)
        B2R = LOOP[:, w_at[4]:w_at[5]].rearrange("p (e n) -> p e n", e=EXPERTS)

        assert 8 * EPP <= (TILES - 1) * D
        xflat = X[:, :, :].rearrange("p t d -> p (t d)")

        def edges_at(k):
            return xflat[:, k * EPP:(k + 1) * EPP]
        fdst, fsrc, ftmi = (edges_at(k).bitcast(i32) for k in (0, 1, 7))
        ftile, fmask, fscan, fpos, ftmp = (edges_at(k) for k in (2, 3, 4, 5, 6))
        HR, HW = 125, G_EDGES // 125
        gdst = part[4][:, 0:HW].bitcast(i32)
        gdstf = part[4][:, HW:2 * HW]
        gjunk = part[4][:, 2 * HW:3 * HW]
        FILL = part[4][:, 3 * HW:3 * HW + LIST_LEN // P // 2].bitcast(i32)

        XP = pb("XP", [P, 4, 512])
        TR = [pb(f"TR{r}", [P, 512]) for r in range(2)]
        GP = pb("GP", [P, 512])
        OP = pb("OP", [P, 512])

        s_x = sem("s_x"); s_w = sem("s_w"); s_pad = sem("s_pad"); s_padt = sem("s_padt")
        s_ge = sem("s_ge"); s_fe = sem("s_fe"); s_rows = sem("s_rows"); s_fill = sem("s_fill"); s_fillt = sem("s_fillt")
        s_fw = sem("s_fw"); s_ew = sem("s_ew"); s_c = sem("s_c"); s_iota = sem("s_iota")
        dv = sem("dv")
        s_wt = sem("s_wt"); s_pe = sem("s_pe"); s_act = sem("s_act")
        s_cidx = sem("s_cidx"); s_lrow = sem("s_lrow"); s_flist = sem("s_flist"); s_lf = sem("s_lf"); s_ltr = sem("s_ltr"); s_lcp = sem("s_lcp")
        s_xn = sem("s_xn"); s_pt = sem("s_pt"); s_xt = sem("s_xt"); s_pj = sem("s_pj"); s_ev = sem("s_ev"); s_stg = sem("s_stg")
        s_stat = sem("s_stat"); s_hist = sem("s_hist"); s_rk = sem("s_rk")
        s_tdma = [sem(f"s_tdma{r}") for r in range(2)]
        s_td2 = sem("s_td2"); s_ready = sem("s_ready")
        s_stage = [sem(f"s_stage{h}") for h in range(2)]
        s_sc = [sem(f"s_sc{h}") for h in range(2)]
        s_row = [sem(f"s_row{s}") for s in range(SPI)]
        s_tick = sem("s_tick")
        s_sf = sem("s_sf"); s_ne = sem("s_ne"); s_tr = sem("s_tr"); s_elt = sem("s_elt"); s_stc = sem("s_stc")
        s_mask = sem("s_mask"); s_red = sem("s_red"); s_b2 = sem("s_b2"); s_b3 = sem("s_b3"); s_b4 = sem("s_b4")
        s_er = sem("s_er"); s_dlt = sem("s_dlt"); s_mset = sem("s_mset"); s_alpha = sem("s_alpha")
        s_gat = sem("s_gat"); s_c1 = sem("s_c1"); s_c2 = sem("s_c2"); s_c3 = sem("s_c3"); s_lg = sem("s_lg")
        s_wexp = sem("s_wexp"); s_msg = sem("s_msg"); s_out = sem("s_out"); s_e1 = sem("s_e1"); s_acc = sem("s_acc")
        s_h1 = sem("s_h1"); s_hh = sem("s_hh"); s_y = sem("s_y"); s_o1 = sem("s_o1"); s_o2 = sem("s_o2")
        s_st = sem("s_st"); s_var = sem("s_var"); s_sd = sem("s_sd"); s_x2 = sem("s_x2"); s_fpos = sem("s_fpos")
        s_bias = [sem(f"s_bias{e}") for e in range(EXPERTS)]
        s_add = [sem(f"s_add{e}") for e in range(EXPERTS)]

        block = ctx.enter_context(nc.Block())

        def bank(n, cols):
            return XP[:, n, 0:cols]

        x_full = x[0:(TILES - 1) * P, :].rearrange("(t p) d -> p t d", p=P)
        GAT_T = {0: (ACC, EM, SEL, g_table), 1: (ACC2, EM2, SEL2, f_table)}

        @block.sync
        def _(sp):
            with nc.allow_non_contiguous_dma("small rows"):
                XL = 8
                for j in range(0, TILES - 1, XL):
                    sp.dma_start(X[:, j:j + XL, :], x_full[:, j:j + XL, :]).then_inc(s_x, 16)
                sp.wait_ge(s_c, 1)
                sp.dma_start(X[0:LAST_ROWS, TILES - 1, :], x[(TILES - 1) * P:N_NODES, :]).then_inc(s_x, 16)
                sp.dma_start(gdst[0:HR, :], dst.rearrange("(p n) -> p n", p=HR)).then_inc(s_ge, 16)
                sp.dma_start(WSB[:, :, :], g_w.rearrange("(b p) d -> p b d", p=P)).then_inc(s_w, 16)
                for b in range(2):
                    for c, a in enumerate((a_left, a_right)):
                        sp.dma_start(ACOL[:, b, c:c + 1],
                                     a.rearrange("h (c one) -> (h c) one", one=1)[b * P:(b + 1) * P, :]).then_inc(s_w, 16)
                for rows, a in ((src_rows, src), (dst_rows, dst)):
                    flat = rows.rearrange("a b -> (a b)")
                    sp.dma_start(flat[0:G_EDGES].rearrange("(a b) -> a b", a=16),
                                 a.rearrange("(a b) -> a b", a=16)).then_inc(s_pad, 16)
                sp.wait_ge(s_padt, 2)
                npad = (G_PAD - G_EDGES) // 32
                for k, rows in enumerate((src_rows, dst_rows)):
                    flat = rows.rearrange("a b -> (a b)")
                    sp.dma_start(flat[G_EDGES:G_PAD].rearrange("(a b) -> a b", a=32),
                                 LI[0:32, k, 0:npad]).then_inc(s_pad, 16)
                sp.wait_ge(s_fillt, 1)
                for k in range(2):
                    sp.dma_start(f_list[k * LIST_LEN // 2:(k + 1) * LIST_LEN // 2, 0].rearrange("(p n) -> p n", p=P),
                                 FILL).then_inc(s_fill, 16)
                sp.dma_start(WGAT[:, :, :], w_gat.rearrange("(k p) n -> p k n", p=P)).then_inc(s_fw, 16)
                for j, a in enumerate((att_src.rearrange("h c -> (h c)"), att_dst.rearrange("h c -> (h c)"),
                                       b_gat, ln_gamma, ln_beta)):
                    sp.dma_start(ROWS16[:, j, :], a.partition_broadcast(P)).then_inc(s_fw, 16)
                sp.dma_start(B1R[:, :], b1.rearrange("e (f p) -> (e f) p", p=P)).then_inc(s_fw, 16)

                def table_rows(i, r):
                    sp.wait_ge(s_stg, 2 * i + r + 1)
                    sp.dma_start(g_table[bass.ds(256 * i + P * r, P), 0:D], STG[:, r, 0:D]).then_inc(s_tdma[r], 16)
                with sp.Fori(0, TILES // 2) as i:
                    for r in range(2):
                        table_rows(i, r)
                table_rows(TILES // 2, 0)
                sp.wait_ge(s_xn, TILES)
                e2 = edge_index.rearrange("a (p n) -> a p n", p=P)
                sp.dma_start(fdst, e2[1]).then_inc(s_fe, 16)
                sp.dma_start(fsrc, e2[0]).then_inc(s_fe, 16)
                sp.wait_ge(s_td2, 1)
                sp.dma_start(g_table.rearrange("(t p) w -> p t w", p=P)[:, :, D:GNN.W], ET[:, :, :]).then_inc(s_ready, 16)

                def stage(gat, i, h):
                    if gat is GNN:
                        if not (isinstance(i, int) and i == 0):
                            sp.wait_ge(s_sc[h], 16 * SC_HALF * i)
                        sp.dma_start(POSB[:, h, :], POS[:, bass.ds((2 * i + h) * SC_HALF, SC_HALF)]).then_inc(s_stage[h], 16)
                        sp.dma_start(RECB[:, h, :], REC[:, bass.ds((2 * i + h) * SC_HALF, SC_HALF)]).then_inc(s_stage[h], 16)
                    if not (isinstance(i, int) and i == 0):
                        for s in range(h * HALF, (h + 1) * HALF):
                            sp.wait_ge(s_row[s], 32 * i)
                    sp.dma_start(IDXB[:, h, :, :], IDX[:, bass.ds(SPI * i + HALF * h, HALF), :]).then_inc(s_stage[h], 16)

                sp.wait_ge(s_lcp, 1)
                for j in range(0, TILES - 1, XL):
                    sp.dma_start(X[:, j:j + XL, :], x_full[:, j:j + XL, :]).then_inc(s_x2, 16)
                for gat in (GNN, FFN):
                    if gat is FFN:
                        sp.wait_ge(s_sc[0], 16 * SC_HALF * G_ITERS)
                        sp.wait_ge(s_sc[1], 16 * SC_HALF * G_ITERS)
                        for b in range(F_BLOCKS):
                            if b:
                                sp.wait_ge(s_lf, G_BLOCKS + b)
                            sp.dma_start(LI[:, 0, :], f_list[b * P * SLOT:(b + 1) * P * SLOT, 0]
                                         .rearrange("(p n) -> p n", p=P)).then_inc(s_flist, 16)
                        sp.wait_ge(s_td2, 2)
                        sp.dma_start(f_table.rearrange("(t p) w -> p t w", p=P), FT[:, :, :]).then_inc(s_ready, 16)
                        sp.wait_ge(s_lcp, 2)
                    for h in range(2):
                        stage(gat, gat.i0, h)
                    with sp.Fori(gat.i0 + 1, gat.i1) as i:
                        for h in range(2):
                            stage(gat, i, h)

                sp.wait_ge(s_acc, ALL_SLOTS)
                for e in range(EXPERTS):
                    sp.dma_start(W1S[:, e, :, :], w1[e].rearrange("(k p) n -> p k n", p=P)).then_inc(s_ew, 16)
                    sp.dma_start(W2S[:, e, :, :], w2[e].rearrange("(f p) n -> p f n", p=P)).then_inc(s_ew, 16)
                sp.dma_start(B2R, b2.partition_broadcast(P)).then_inc(s_ew, 16)
                with sp.Fori(0, TILES // 4) as i:
                    sp.wait_ge(s_add[EXPERTS - 1], 4 * i + 4)
                    sp.dma_start(out[bass.ds(i * 4 * P, 4 * P), :].rearrange("(j p) d -> p j d", p=P), OUTS).then_inc(s_st, 16)
                sp.wait_ge(s_add[EXPERTS - 1], TILES)
                sp.dma_start(out[(TILES - 1) * P:N_NODES, :], OUTS[0:LAST_ROWS, 0, :]).then_inc(s_st, 16)
                sp.wait_ge(s_st, 16 * (TILES // 4 + 1))

        @block.gpsimd
        def _(pool):
            pool.iota(ROWI[:, :], pattern=[[1, P]], base=0, channel_multiplier=0).then_inc(s_iota, 1)
            pool.iota(COLI[:, :], pattern=[[0, 1]], base=0, channel_multiplier=1).then_inc(s_iota, 1)
            pool.iota(POS[:, EPP:SC_COLS], pattern=[[1, SC_COLS - EPP]], base=TRASH + F_EDGES,
                      channel_multiplier=SC_COLS - EPP).then_inc(s_iota, 1)
            pool.memset(REC[:, EPP:SC_COLS], 0).then_inc(s_iota, 1)
            pool.memset(X[:, TILES - 1, :], 0.0).then_inc(s_c, 1)
            pool.memset(TICK[:, :], 0.0).then_inc(s_tick, 1)
            pool.memset(LI[:, 0, 0:SLOT], 0).then_inc(s_padt, 1)
            pool.memset(LI[:, 1, 0:SLOT], FAR).then_inc(s_padt, 1)
            pool.memset(FILL, P * SRC_SPAN).then_inc(s_fillt, 1)
            pool.wait_ge(s_pad, 64)
            pool.wait_ge(s_cidx, 1)
            for b in range(G_BLOCKS):
                if b:
                    pool.wait_ge(s_lf, b)
                for k, rows in enumerate((src_rows, dst_rows)):
                    pool.indirect_dma_start(out=LI[:, k, :], out_offset=None, in_=rows,
                                            in_offset=bass.IndirectOffsetOnAxis(ap=CIDX[:, b:b + 1], axis=0)).then_inc(s_lrow, 16)

            def half(gat, i, h):
                table = g_table if gat is GNN else f_table
                n = 2 * i + h
                pool.wait_ge(s_tick, n + 1)
                pool.wait_ge(s_stage[h], 48 * i + 48 if gat is GNN else 48 * G_ITERS + 16 * (i - G_ITERS) + 16)
                if not (isinstance(i, int) and i == gat.i0):
                    pool.wait_ge(s_msg, SPI * (i - 1) + HALF * h + HALF)
                pool.tensor_tensor(TICK[:, 0:1], TICK[:, 1:2], TICK[:, 2:3], ALU.add).then_inc(s_tick, 1)
                sc = list(range(SC_HALF)) if gat is GNN else []
                for s in range(HALF):
                    for k in range(CHUNKS):
                        pool.indirect_dma_start(out=R[:, h * HALF + s, k, 0:gat.W], out_offset=None, in_=table,
                                                in_offset=bass.IndirectOffsetOnAxis(ap=IDXB[:, h, s, k:k + 1], axis=0)
                                                ).then_inc(s_row[h * HALF + s], 16)
                        for c in sc[:2 if len(sc) > HALF * CHUNKS - (s * CHUNKS + k) - 1 else 1]:
                            sc.remove(c)
                            pool.indirect_dma_start(out=f_list, out_offset=bass.IndirectOffsetOnAxis(ap=POSB[:, h, c:c + 1], axis=0),
                                                    in_=RECB[:, h, c:c + 1], in_offset=None).then_inc(s_sc[h], 16)
                for c in sc:
                    pool.indirect_dma_start(out=f_list, out_offset=bass.IndirectOffsetOnAxis(ap=POSB[:, h, c:c + 1], axis=0),
                                            in_=RECB[:, h, c:c + 1], in_offset=None).then_inc(s_sc[h], 16)

            pool.wait_ge(s_xn, TILES)
            pool.iota(ftmi, pattern=[[1, EPP]], base=TRASH, channel_multiplier=EPP).then_inc(s_iota, 1)
            pool.wait_ge(s_fill, 32)
            for k, gat in enumerate((GNN, FFN)):
                if gat is GNN:
                    pool.wait_ge(s_tdma[0], 16 * (TILES // 2 + 1))
                    pool.wait_ge(s_tdma[1], 16 * (TILES // 2))
                pool.wait_ge(s_ready, 16 * (k + 1))
                for h in range(2):
                    half(gat, gat.i0, h)
                with pool.Fori(gat.i0 + 1, gat.i1) as i:
                    for h in range(2):
                        half(gat, i, h)

        @block.scalar
        def _(act):
            def list_copies(first, blocks):
                for b in range(blocks):
                    n = first + b
                    g0 = (0 if first == 0 else G_SLOTS) + P * b
                    w = min(P, (G_SLOTS if first == 0 else ALL_SLOTS) - g0)
                    act.wait_ge(s_ltr, n + 1)
                    for k in range(CHUNKS):
                        act.activation(IDX[:, g0:g0 + w, k], TR[0][:, k * P:k * P + w], ACT.Copy)
                        act.activation(DL[:, g0:g0 + w, k], TR[1][:, k * P:k * P + w], ACT.Copy)
                    act.activation(TROW[0:1, g0:g0 + w], GP[0:1, 0:w], ACT.Copy).then_inc(s_act, 1)

            def rstd(k):
                act.wait_ge(s_var, k + 1)
                act.activation(RSTD[:, :], VAR[:, :], ACT.Sqrt).then_inc(s_sd, 1)

            def project(phase, i, r):
                tau = (TILES if phase else 0) + 2 * i + r
                first = isinstance(tau, int) and tau < 2
                act.wait_ge(s_pt, tau + 1)
                act.activation(XT[:, r, :, :], TR[r][:, 0:2 * P].rearrange("p (k n) -> p k n", k=2), ACT.Copy).then_inc(s_xt, 1)
                if phase == 0:
                    act.wait_ge(s_pj, tau + 1)
                    if not first:
                        act.wait_ge(s_tdma[r], 16 * i)
                        act.wait_ge(s_ev, tau - 1)
                    act.activation(STG[:, r, :], (GP, OP)[r][:, 0:D + 2 * G_HEADS], ACT.Copy).then_inc(s_stg, 1)

            def steps(gat, it, first, last):
                H, C, n0 = gat.H, gat.C, it * SPI
                for s in range(-1 if first else 0, SPI + (2 if last else 0)):
                    if not (last and s >= SPI - 1):
                        g = n0 + s + 1
                        q = (s + 1) % 2
                        act.wait_ge(s_tr, g + 1)
                        if not (first and gat is GNN and s < 1):
                            act.wait_ge(s_mask, g - 1)
                        act.activation(ELT[0:3 * H, q, :, :],
                                       TR[q][0:3 * H, 256:256 + P].bitcast(bf16).rearrange("p (k n) -> p k n", k=CHUNKS),
                                       ACT.Copy).then_inc(s_elt, 1)
                        if not (first and gat is GNN and s < 1):
                            act.wait_ge(s_gat, g - 1)
                        act.activation(ST[:, q, :, :], TR[q][:, 0:2 * P].rearrange("p (k n) -> p k n", k=CHUNKS),
                                       ACT.Copy).then_inc(s_stc, 1)
                    if s >= 0 and not (last and s >= SPI):
                        g = n0 + s
                        act.wait_ge(s_dlt, g + 1)
                        if not (first and gat is GNN and s < 4):
                            act.wait_ge(s_acc, g - 3)
                        act.activation(AL[:, s % 4, 0:H], DLT[:, s % 2, 0:H], ACT.Exp).then_inc(s_alpha, 1)
                        act.wait_ge(s_lg, g + 1)
                        if not (first and gat is GNN and s < 2):
                            act.wait_ge(s_out, g - 1)
                        act.activation(MSG[:, s % 2, :, 0:gat.A].rearrange("p k (h c) -> p k h c", c=C + 1)[:, :, :, C],
                                       LG[:, s % 2, :, 0:H], ACT.Exp).then_inc(s_wexp, 1)

            act.wait_ge(s_wt, 1)
            for b in range(2):
                act.activation(WA[:, b, 0:D], bank(b, D), ACT.Copy)
            for b in range(2):
                act.activation(WA[:, b, D:D + 16], XP[:, b, D:D + 16], ACT.Copy).then_inc(s_act, 1)
            rstd(0)
            for r in range(2):
                project(0, 0, r)
            with act.Fori(1, TILES // 2) as i:
                for r in range(2):
                    project(0, i, r)
            project(0, TILES // 2, 0)
            list_copies(0, G_BLOCKS)
            steps(GNN, 0, True, False)
            with act.Fori(1, G_ITERS - 1) as i:
                steps(GNN, i, False, False)
            steps(GNN, G_ITERS - 1, False, True)
            list_copies(G_BLOCKS, F_BLOCKS)
            rstd(1)
            for r in range(2):
                project(1, 0, r)
            with act.Fori(1, TILES // 2) as i:
                for r in range(2):
                    project(1, i, r)
            project(1, TILES // 2, 0)
            steps(FFN, FFN.i0, True, False)
            with act.Fori(FFN.i0 + 1, FFN.i1 - 1) as i:
                steps(FFN, i, False, False)
            steps(FFN, FFN.i1 - 1, False, True)
            rstd(2)
            act.wait_ge(s_var, 4)
            act.activation(S4[:, 1, :, :], S4[:, 0, :, :], ACT.Exp).then_inc(s_sd, 1)
            act.wait_ge(s_wt, 2)
            act.activation(B1C[:, :], GP[:, 0:EXPERTS * FB], ACT.Copy).then_inc(s_act, 1)
            act.wait_ge(s_act, 2 + G_BLOCKS + F_BLOCKS + 1)

            def hidden(i, cols):
                for e in range(EXPERTS):
                    for f in range(FB):
                        m = (i * EXPERTS + e) * FB + f
                        act.wait_ge(s_h1, m + 1)
                        if f == 0 and not (isinstance(i, int) and i == 0 and e == 0):
                            act.wait_ge(s_y, i * EXPERTS + e)
                        act.activation(HH[:, f, 0:cols], XP[:, f, 0:cols], ACT.Gelu,
                                       bias=B1C[:, e * FB + f:e * FB + f + 1]).then_inc(s_hh, 1)
            hidden(0, 512)
            with act.Fori(1, TILES // 4) as i:
                hidden(i, 512)
            hidden(TILES // 4, P)

        @block.tensor
        def _(pe):
            pe.wait_ge(s_w, 80)
            pe.wait_ge(s_rows, 1)
            for kb in range(2):
                for ob in range(2):
                    pe.transpose(XP[:, kb, ob * P:(ob + 1) * P], WSB[:, ob, kb * P:(kb + 1) * P], IDF[:, :])
                for ob in range(2):
                    last = pe.matmul(XP[:, kb, D:D + 16], WSB[:, ob, kb * P:(kb + 1) * P], ADIAG[:, ob, :],
                                     start=(ob == 0), stop=(ob == 1), skip_group_check=True)
            last.then_inc(s_wt, 1)
            pe.wait_ge(s_rows, 2)
            pe.matmul(XP[:, 2, 0:TILES], ONES[0:HR, :], CNT[0:HR, :], start=True, stop=True).then_inc(s_rk, 1)

            def lists(first, blocks):
                for b in range(blocks):
                    n = first + b
                    pe.wait_ge(s_lf, n + 1)
                    if n:
                        pe.wait_ge(s_act, 2 + n)
                    for k in range(CHUNKS):
                        pe.transpose(TR[0][:, k * P:(k + 1) * P], LF[:, 0, k * P:(k + 1) * P], IDF[:, :])
                        pe.transpose(TR[1][:, k * P:(k + 1) * P], LF[:, 1, k * P:(k + 1) * P], IDF[:, :])
                    pe.transpose(GP[0:1, 0:P], TCOL[:, n:n + 1], IDF[:, :]).then_inc(s_ltr, 1)

            def project(phase, i, r):
                tau = (TILES if phase else 0) + 2 * i + r
                first = isinstance(tau, int) and tau < 2
                pe.wait_ge(s_xn, tau + 1)
                if not first:
                    pe.wait_ge(s_xt, tau - 1)
                for k in range(2):
                    last = pe.transpose(TR[r][:, k * P:(k + 1) * P], XN[:, r, k * P:(k + 1) * P], IDF[:, :])
                last.then_inc(s_pt, 1)
                pe.wait_ge(s_xt, tau + 1)
                if not first:
                    pe.wait_ge(s_stg if phase == 0 else s_ev, tau - 1)
                w = WA if phase == 0 else WGAT
                cols = D + 16 if phase == 0 else 16
                for k in range(2):
                    last = pe.matmul((GP, OP)[r][:, 0:cols], XT[:, r, k, :], w[:, k, :], start=(k == 0), stop=(k == 1))
                last.then_inc(s_pj, 1)

            def steps(gat, it, first, last_):
                H, C, HB, n0 = gat.H, gat.C, gat.HB, it * SPI
                SELG = SEL if gat is GNN else SEL2
                NB = H // HB
                def p1(s):
                    g = n0 + s
                    q = s % 2
                    sl = s % SPI
                    pe.wait_ge(s_sf, g + 1)
                    pe.wait_ge(s_row[sl], it * 32 + 32 * (1 + s // SPI))
                    if not (first and gat is GNN and s < 2):
                        pe.wait_ge(s_stc, g - 1)
                        pe.wait_ge(s_elt, g - 1)
                    for k in range(CHUNKS):
                        pe.transpose(TR[q][0:3 * H, 256 + k * 64:256 + (k + 1) * 64].bitcast(bf16),
                                     R[:, sl, k, gat.SPL:gat.SPL + 3 * H // 2].bitcast(bf16), IDB[:, :])
                    for k in range(CHUNKS):
                        last = pe.transpose(TR[q][:, k * P:(k + 1) * P], SF[:, s % 4, k, :], IDF[:, :])
                    last.then_inc(s_tr, 1)

                def p2(s):
                    g = n0 + s
                    q = s % 2
                    pe.wait_ge(s_ne, g + 1)
                    pe.wait_ge(s_elt, g + 1)
                    if not (first and gat is GNN and s < 1):
                        pe.wait_ge(s_red, g)
                    for k in range(CHUNKS):
                        for b in range(NB):
                            o = XP[:, k * NB + b, :].rearrange("p (h n) -> p h n", h=HB)
                            pe.matmul(o, NE[:, q, k, :], IDB[:, :].unsqueeze(1).to_broadcast([P, HB, P]),
                                      start=True, stop=False)
                            for h in range(HB):
                                last = pe.matmul(o[:, h, :], SELG[0:3 * H, b * HB + h, :], ELT[0:3 * H, q, k, :],
                                                 start=False, stop=(h == HB - 1))
                    last.then_inc(s_mask, 1)

                def p3(s):
                    g = n0 + s
                    q = s % 2
                    pe.wait_ge(s_b4, g + 1)
                    pe.wait_ge(s_er, g + 1)
                    pe.wait_ge(s_stc, g + 1)
                    if not (first and gat is GNN and s < 1):
                        pe.wait_ge(s_c3, g)
                    for k in range(CHUNKS):
                        last = pe.matmul(GP[:, k * 2 * H:(k + 1) * 2 * H], ST[:, q, k, :], TB[:, q, 0:2 * H],
                                         start=True, stop=True, skip_group_check=True)
                    last.then_inc(s_gat, 1)

                def p4(s):
                    g = n0 + s
                    pe.wait_ge(s_msg, g + 1)
                    if not (first and gat is GNN and s < 1):
                        pe.wait_ge(s_acc, g)
                    for k in range(CHUNKS):
                        last = pe.matmul(OP[:, 0:gat.A], SF[:, s % 4, k, :], MSG[:, s % 2, k, 0:gat.A],
                                         start=(k == 0), stop=(k == CHUNKS - 1))
                    last.then_inc(s_out, 1)

                if first:
                    p1(0)
                    p2(0)
                for s in range(SPI + (1 if last_ else 0)):
                    nxt = not (last_ and s >= SPI - 1)
                    if nxt:
                        p1(s + 1)
                    if s < SPI:
                        p3(s)
                    if nxt:
                        p2(s + 1)
                    if not (first and s == 0):
                        p4(s - 1)

            for r in range(2):
                project(0, 0, r)
            with pe.Fori(1, TILES // 2) as i:
                for r in range(2):
                    project(0, i, r)
            project(0, TILES // 2, 0)
            lists(0, G_BLOCKS)
            pe.wait_ge(s_rows, 3)
            pe.matmul(XP[:, 2, 0:TILES], ONES[:, :], CNT2[:, :], start=True, stop=True)
            pe.matmul(XP[:, 3, 0:TILES], UPPER[:, :], CNT2[:, :], start=True, stop=True).then_inc(s_rk, 1)
            steps(GNN, 0, True, False)
            with pe.Fori(1, G_ITERS - 1) as i:
                steps(GNN, i, False, False)
            steps(GNN, G_ITERS - 1, False, True)
            lists(G_BLOCKS, F_BLOCKS)
            for r in range(2):
                project(1, 0, r)
            with pe.Fori(1, TILES // 2) as i:
                for r in range(2):
                    project(1, i, r)
            project(1, TILES // 2, 0)
            steps(FFN, FFN.i0, True, False)
            with pe.Fori(FFN.i0 + 1, FFN.i1 - 1) as i:
                steps(FFN, i, False, False)
            steps(FFN, FFN.i1 - 1, False, True)

            pe.wait_ge(s_fw, 16 * 7)
            pe.wait_ge(s_acc, ALL_SLOTS)
            pe.transpose(GP[:, 0:EXPERTS * FB], B1R[:, :], IDF[0:16, 0:16]).then_inc(s_wt, 1)
            pe.wait_ge(s_ew, 16 * 9)
            XTA = ACC[:, :, :, :].rearrange("p t h c -> p (t h c)")[:, 0:2 * NODES_PAD].rearrange("p (k n) -> p k n", k=2)

            def expert(i, cols):
                start0 = isinstance(i, int) and i == 0
                for e in range(EXPERTS):
                    for f in range(FB):
                        m = (i * EXPERTS + e) * FB + f
                        if not (start0 and e == 0):
                            pe.wait_ge(s_hh, m - FB + 1)
                        for k in range(2):
                            last = pe.matmul(XP[:, f, 0:cols], W1S[:, e, k, f * P:(f + 1) * P],
                                             XTA[:, k, bass.ds(i * 4 * P, cols)], start=(k == 0), stop=(k == 1))
                        last.then_inc(s_h1, 1)
                    pe.wait_ge(s_hh, (i * EXPERTS + e + 1) * FB)
                    if e:
                        pe.wait_ge(s_add[e - 1], 4 * i + cols // P)
                    elif not start0:
                        pe.wait_ge(s_add[EXPERTS - 1], 4 * i)
                    for j in range(cols // P):
                        for f in range(FB):
                            last = pe.matmul((TR[0], TR[1], GP, OP)[j][:, 0:D], HH[:, f, j * P:(j + 1) * P], W2S[:, e, f, :],
                                             start=(f == 0), stop=(f == FB - 1))
                    last.then_inc(s_y, 1)
            pe.wait_ge(s_act, 2 + G_BLOCKS + F_BLOCKS + 1)
            expert(0, 512)
            with pe.Fori(1, TILES // 4) as i:
                expert(i, 512)
            expert(TILES // 4, P)

        @block.vector
        def _(dve):
            chain = [0]

            def link(ins):
                chain[0] += 1
                ins.then_inc(dv, 1)
                dve.wait_ge(dv, chain[0])

            def layer_stats(k):
                with dve.Fori(0, TILES) as t:
                    dve.bn_stats(STAT[:, t, :], X[:, t, :]).then_inc(s_stat, 1)
                dve.wait_ge(s_stat, TILES * (k + 1))
                link(dve.tensor_tensor(MEAN[:, :], STAT[:, :, 1], STAT[:, :, 4], ALU.add))
                link(dve.tensor_scalar(MEAN[:, :], MEAN[:, :], 0.5, None, ALU.mult))
                link(dve.tensor_tensor(VAR[:, :], STAT[:, :, 1], STAT[:, :, 4], ALU.subtract))
                link(dve.tensor_tensor(VAR[:, :], VAR[:, :], VAR[:, :], ALU.mult))
                link(dve.tensor_scalar(VAR[:, :], VAR[:, :], 0.25, LN_EPS, ALU.mult, ALU.add))
                link(dve.tensor_tensor(RSTD[:, :], STAT[:, :, 2], STAT[:, :, 5], ALU.add))
                link(dve.tensor_scalar(RSTD[:, :], RSTD[:, :], 1.0 / D, None, ALU.mult))
                link(dve.tensor_tensor(VAR[:, :], VAR[:, :], RSTD[:, :], ALU.add))
                dve.sem_inc(s_var, 1)
                dve.wait_ge(s_sd, k + 1)
                link(dve.reciprocal(RSTD[:, :], RSTD[:, :]))

            def project(phase, i, r):
                t = 2 * i + r
                tau = (TILES if phase else 0) + t
                first = isinstance(tau, int) and tau < 2
                if not first:
                    dve.wait_ge(s_pt, tau - 1)
                dve.tensor_scalar(XN[:, r, :], X[:, t, :] if isinstance(t, int) else X[:, bass.ds(t, 1), :].squeeze(1),
                                  MEAN[:, bass.ds(t, 1)], RSTD[:, bass.ds(t, 1)], ALU.subtract, ALU.mult).then_inc(s_xn, 1)

            def project_out(phase, i, r):
                t = 2 * i + r
                tau = (TILES if phase else 0) + t
                ps = (GP, OP)[r]
                if phase == 0:
                    dve.wait_ge(s_stg, tau + 1)
                    dve.tensor_scalar(ACC[:, bass.ds(t, 1), :, 0:G_CH].squeeze(1),
                                      STG[:, r, 0:D].rearrange("p (h c) -> p h c", h=G_HEADS), 1.0, None, ALU.mult)
                    dve.tensor_scalar(ELR[:, bass.ds(t, 1), :].squeeze(1), STG[:, r, D:D + 2 * G_HEADS], 1.0, None, ALU.mult).then_inc(s_ev, 1)
                else:
                    dve.wait_ge(s_pj, tau + 1)
                    dve.tensor_scalar(XTA[:, :, bass.ds(t * P, P)], XT[:, r, :, :], 1.0, None, ALU.mult)
                    dve.tensor_scalar(HF[:, bass.ds(t, 1), :].squeeze(1), ps[:, 0:16], 1.0, None, ALU.mult).then_inc(s_ev, 1)

            def projection(phase):
                for r in range(2):
                    project(phase, 0, r)
                for r in range(2):
                    project_out(phase, 0, r)
                with dve.Fori(1, TILES // 2) as i:
                    for r in range(2):
                        project(phase, i, r)
                    for r in range(2):
                        project_out(phase, i, r)
                project(phase, TILES // 2, 0)
                project_out(phase, TILES // 2, 0)
                dve.wait_ge(s_ev, TILES * (phase + 1))

            def logits(el, er, et, em, H):
                spl = et[:, :, H:H + (3 * H + 1) // 2].bitcast(bf16)
                t1, t2 = S16A[:, :, 0:H], S16B[:, :, 0:H]
                dve.tensor_copy(et[:, :, 0:H], el)
                link(dve.tensor_copy(spl[:, :, 0:H], el))
                link(dve.tensor_tensor(t1, el, spl[:, :, 0:H], ALU.subtract))
                link(dve.tensor_copy(spl[:, :, H:2 * H], t1))
                link(dve.tensor_tensor(t2, t1, spl[:, :, H:2 * H], ALU.subtract))
                link(dve.tensor_copy(spl[:, :, 2 * H:3 * H], t2))
                dve.tensor_copy(em[:, :, 0:H], er)
                link(dve.tensor_tensor(t1, el, er, ALU.add))
                link(dve.scalar_tensor_tensor(em[:, :, H:2 * H], t1, SLOPE, t1, ALU.mult, ALU.max))

            def slot_tiles(first, blocks, qcols):
                for b in range(blocks):
                    link(dve.tensor_scalar(SCOL[:, :], COL[:, :], float(P * b), None, ALU.add))
                    link(dve.tensor_scalar(JUNK[:, 0:TILES - 1], qcols, SCOL[:, 0:1], None, ALU.is_le, ALU.add,
                                           accum_out=TCOL[:, first + b:first + b + 1]))
                    if first == 0:
                        link(dve.tensor_tensor(CCOL[:, b:b + 1], SCOL[:, :], TCOL[:, b:b + 1], ALU.subtract))
                        link(dve.tensor_scalar(CIDX[:, b:b + 1], CCOL[:, b:b + 1], float(G_PAD_ROWS - 1), None, ALU.min))

            XTA = ACC[:, :, :, :].rearrange("p t h c -> p (t h c)")[:, 0:2 * NODES_PAD].rearrange("p (k n) -> p k n", k=2)

            dve.wait_ge(s_iota, 4)
            dve.memset(ONES[:, :], 1.0)
            dve.memset(CNT[:, :], 0.0)
            dve.memset(ZERO[:, :], 0.0)
            dve.memset(ACC[:, :, :, G_CH:G_CH + 1], 1.0)
            dve.memset(ACC2[:, :, :, F_CH:F_CH + 1], 1.0)
            dve.tensor_copy(COL[:, :], COLI[:, :])
            link(dve.tensor_copy(ROW[:, :], ROWI[:, :]))
            link(dve.tensor_scalar(IDF[:, :], ROW[:, :], COL[:, 0:1], None, ALU.is_equal))
            dve.tensor_copy(IDB[:, :], IDF[:, :])
            dve.tensor_scalar(UPPER[:, :], ROW[:, :], COL[:, 0:1], None, ALU.is_gt)
            dve.tensor_scalar(THR[:, :], ROW[:, 0:TILES], float(P), None, ALU.mult)
            for sel, H in ((SEL, G_HEADS), (SEL2, F_HEADS)):
                link(dve.tensor_reduce(JUNK[0:3 * H, 0:H], IDF[0:3 * H, 0:3 * H].rearrange("p (j h) -> p h j", h=H), AX.X, ALU.add))
                link(dve.tensor_copy(sel[:, :, :], JUNK[0:3 * H, 0:H].unsqueeze(2).to_broadcast([3 * H, H, P])))
            dve.wait_ge(s_w, 80)
            dve.memset(ADIAG[:, :, :], 0.0)
            HPB = P // G_CH
            link(dve.tensor_reduce(JUNK[:, 0:HPB], IDF[:, :].rearrange("p (h c) -> p h c", c=G_CH), AX.X, ALU.add))
            for b in range(2):
                for c in range(2):
                    o = c * G_HEADS + b * HPB
                    link(dve.tensor_scalar(ADIAG[:, b, o:o + HPB], JUNK[:, 0:HPB], ACOL[:, b, c:c + 1], None, ALU.mult))
            dve.sem_inc(s_rows, 1)

            dve.wait_ge(s_ge, 16)
            link(dve.tensor_copy(gdstf[0:HR, :], gdst[0:HR, :]))
            with dve.Fori(1, TILES) as t:
                dve.tensor_scalar(gjunk[0:HR, :], gdstf[0:HR, :], THR[0:HR, bass.ds(t, 1)], None, ALU.is_lt, ALU.add,
                                  accum_out=CNT[0:HR, bass.ds(t, 1)]).then_inc(s_hist, 1)
                dve.wait_ge(s_hist, t)
            dve.wait_ge(s_hist, TILES - 1)
            dve.sem_inc(s_rows, 1)

            dve.wait_ge(s_x, 16 * (-(-(TILES - 1) // 8) + 1))
            layer_stats(0)
            projection(0)
            logits(ELR[:, :, 0:8], ELR[:, :, 8:16], ET, EM, G_HEADS)
            dve.sem_inc(s_td2, 1)

            dve.wait_ge(s_rk, 1)
            link(dve.tensor_copy(QI[:, :], XP[:, 2, 0:TILES]))
            link(dve.tensor_scalar(QI[:, :], QI[:, :], 8, None, ALU.arith_shift_right))
            link(dve.tensor_copy(Q[:, :], QI[:, :]))
            link(dve.tensor_tensor(Q[:, :], Q[:, :], ROW[:, 0:TILES], ALU.add))
            slot_tiles(0, G_BLOCKS, Q[:, 1:TILES])
            dve.sem_inc(s_cidx, 1)
            for b in range(G_BLOCKS):
                dve.wait_ge(s_lrow, 32 * (b + 1))
                if b:
                    dve.wait_ge(s_ltr, b)
                link(dve.tensor_scalar(SCOL[:, :], TCOL[:, b:b + 1], float(P), None, ALU.mult))
                dve.tensor_copy(LF[:, 0, :], LI[:, 0, :])
                link(dve.tensor_copy(LF[:, 1, :], LI[:, 1, :]))
                dve.tensor_scalar(LF[:, 1, :], LF[:, 1, :], SCOL[:, 0:1], None, ALU.subtract).then_inc(s_lf, 1)

            dve.wait_ge(s_fe, 32)
            dve.wait_ge(s_iota, 5)
            dve.tensor_copy(fpos, ftmi)
            link(dve.tensor_scalar(REC[:, 0:EPP], fdst, 7, None, ALU.arith_shift_right))
            link(dve.tensor_copy(ftile, REC[:, 0:EPP]))
            link(dve.tensor_scalar(REC[:, 0:EPP], fdst, P - 1, None, ALU.bitwise_and))
            link(dve.tensor_copy(ftmp, REC[:, 0:EPP]))
            link(dve.tensor_copy(fscan, fsrc))
            link(dve.tensor_scalar(fscan, fscan, float(N_NODES - 1), None, ALU.min))
            link(dve.scalar_tensor_tensor(REC[:, 0:EPP], ftmp, float(SRC_SPAN), fscan, ALU.mult, ALU.add))
            with dve.Fori(0, TILES) as t:
                dve.tensor_scalar(fmask, ftile, ROW[:, bass.ds(t, 1)], None, ALU.is_equal, ALU.add,
                                  accum_out=CNT2[:, bass.ds(t, 1)]).then_inc(s_hist, 1)
                dve.wait_ge(s_hist, t + TILES)
            dve.wait_ge(s_hist, 2 * TILES - 1)
            dve.sem_inc(s_rows, 1)
            dve.wait_ge(s_rk, 2)
            link(dve.tensor_scalar(NSL[:, :], XP[:, 2, 0:TILES], float(SLOT - 1), None, ALU.add))
            link(dve.tensor_copy(QI[:, :], NSL[:, :]))
            link(dve.tensor_scalar(QI[:, :], QI[:, :], 8, None, ALU.arith_shift_right))
            link(dve.tensor_copy(NSL[:, :], QI[:, :]))
            link(dve.memset(ZERO[:, :], 0.0))
            link(dve.memset(SLOT0[:, 0:1], 0.0))
            link(dve.tensor_tensor_scan(SLOT0[:, 1:TILES + 1], NSL[:, :], ZERO[:, :], 0.0, ALU.add, ALU.add))
            link(dve.scalar_tensor_tensor(BASE[:, :], SLOT0[:, 0:TILES], float(SLOT), XP[:, 3, 0:TILES], ALU.mult, ALU.add))
            link(dve.tensor_scalar(BASE[:, :], BASE[:, :], -1.0, None, ALU.add))
            with dve.Fori(0, TILES) as t:
                dve.tensor_scalar(fmask, ftile, ROW[:, bass.ds(t, 1)], None, ALU.is_equal).then_inc(s_fpos, 1)
                dve.wait_ge(s_fpos, 5 * t + 1)
                dve.tensor_tensor_scan(fscan, fmask, ZERO[:, 0:1].to_broadcast([P, EPP]), BASE[:, bass.ds(t, 1)],
                                       ALU.add, ALU.add).then_inc(s_fpos, 1)
                dve.wait_ge(s_fpos, 5 * t + 2)
                dve.tensor_tensor(fscan, fscan, ftmi, ALU.subtract).then_inc(s_fpos, 1)
                dve.wait_ge(s_fpos, 5 * t + 3)
                dve.tensor_tensor(ftmp, fscan, fmask, ALU.mult).then_inc(s_fpos, 1)
                dve.wait_ge(s_fpos, 5 * t + 4)
                dve.tensor_tensor(fpos, fpos, ftmp, ALU.add).then_inc(s_fpos, 1)
            dve.wait_ge(s_fpos, 5 * TILES)
            link(dve.tensor_copy(POS[:, 0:EPP], fpos))
            slot_tiles(G_BLOCKS, F_BLOCKS, SLOT0[:, 1:TILES])
            dve.wait_ge(s_act, 2 + G_BLOCKS)
            dve.sem_inc(s_lcp, 1)

            def load_tiles(first_index, count):
                return [dve.value_load(TROW[0:1, bass.ds(first_index + j, 1)], min_val=0, max_val=TILES - 1)
                        for j in range(count)]

            def steps(gat, it, first, last_):
                H, C, n0 = gat.H, gat.C, it * SPI
                acc, em = (ACC, EM) if gat is GNN else (ACC2, EM2)
                begin = 0 if first else -2
                tiles = load_tiles(n0 + begin, SPI - begin)

                def tile_of(s):
                    return tiles[s - begin]

                def a(s):
                    g = n0 + s
                    sf = SF[:, s % 4, :, :]
                    dve.tensor_tensor(sf, ROW[:, :].unsqueeze(1).to_broadcast([P, CHUNKS, P]),
                                      DL[:, bass.ds(g, 1), :].squeeze(1).unsqueeze(2).to_broadcast([P, CHUNKS, P]),
                                      ALU.is_equal).then_inc(s_sf, 1)
                    dve.wait_ge(s_sf, g + 1)
                    dve.tensor_scalar(NE[:, s % 2, :, :], sf, 1.0, BIG, ALU.subtract, ALU.mult).then_inc(s_ne, 1)

                def b(s):
                    g = n0 + s
                    q = s % 2
                    t = tile_of(s)
                    er = em[:, bass.ds(t, 1), 0:H].squeeze(1)
                    mx = em[:, bass.ds(t, 1), H:2 * H].squeeze(1)
                    dve.wait_ge(s_mask, g + 1)
                    dve.tensor_reduce(U1[:, 0:H], XP[:, 0:CHUNKS * H // gat.HB, :]
                                      .rearrange("p b n -> p (b n)").rearrange("p (k h n) -> p h k n", k=CHUNKS, h=H),
                                      AX.XY, ALU.max).then_inc(s_red, 1)
                    dve.tensor_scalar(TB[:, q, 0:H], er, 1.0, None, ALU.mult).then_inc(s_er, 1)
                    dve.wait_ge(s_red, g + 1)
                    dve.tensor_tensor(U2[:, 0:H], U1[:, 0:H], er, ALU.add).then_inc(s_b2, 1)
                    dve.wait_ge(s_b2, g + 1)
                    dve.scalar_tensor_tensor(U3[:, 0:H], U2[:, 0:H], SLOPE, U2[:, 0:H], ALU.mult, ALU.max).then_inc(s_b3, 1)
                    dve.wait_ge(s_b3, g + 1)
                    if not (first and gat is GNN and s == 0):
                        dve.wait_ge(s_mset, g)
                    dve.tensor_tensor(TB[:, q, H:2 * H], U3[:, 0:H], mx, ALU.max).then_inc(s_b4, 1)
                    dve.wait_ge(s_b4, g + 1)
                    dve.tensor_tensor(DLT[:, q, 0:H], mx, TB[:, q, H:2 * H], ALU.subtract).then_inc(s_dlt, 1)
                    dve.wait_ge(s_dlt, g + 1)
                    dve.tensor_scalar(mx, TB[:, q, H:2 * H], 1.0, None, ALU.mult).then_inc(s_mset, 1)

                def c(s):
                    g = n0 + s
                    gp = GP[:, 0:CHUNKS * 2 * H].rearrange("p (k n) -> p k n", k=CHUNKS)
                    rel = R[:, s % SPI, :, gat.EL:gat.EL + H]
                    dve.wait_ge(s_gat, g + 1)
                    dve.tensor_tensor(L1[:, :, 0:H], rel, gp[:, :, 0:H], ALU.add).then_inc(s_c1, 1)
                    dve.wait_ge(s_c1, g + 1)
                    dve.scalar_tensor_tensor(L2[:, :, 0:H], L1[:, :, 0:H], SLOPE, L1[:, :, 0:H], ALU.mult, ALU.max).then_inc(s_c2, 1)
                    dve.wait_ge(s_c2, g + 1)
                    dve.tensor_tensor(L3[:, :, 0:H], L2[:, :, 0:H], gp[:, :, H:2 * H], ALU.subtract).then_inc(s_c3, 1)
                    dve.wait_ge(s_c3, g + 1)
                    dve.tensor_scalar(LG[:, s % 2, :, 0:H], L3[:, :, 0:H], 0.0, None, ALU.min).then_inc(s_lg, 1)

                def d(s):
                    g = n0 + s
                    sl = s % SPI
                    m = MSG[:, s % 2, :, 0:gat.A].rearrange("p k (h c) -> p k h c", c=C + 1)
                    dve.wait_ge(s_wexp, g + 1)
                    dve.tensor_tensor(m[:, :, :, 0:C], R[:, sl, :, 0:gat.HC].rearrange("p k (h c) -> p k h c", c=C),
                                      m[:, :, :, C:C + 1].to_broadcast([P, CHUNKS, H, C]), ALU.mult).then_inc(s_msg, 1)

                def e(s):
                    g = n0 + s
                    t = tile_of(s)
                    ac = acc[:, bass.ds(t, 1), :, :].squeeze(1)
                    tmp = TMPA[:, 0:gat.A].rearrange("p (h c) -> p h c", c=C + 1)
                    dve.wait_ge(s_alpha, g + 1)
                    if not (first and gat is GNN and s == 0):
                        dve.wait_ge(s_acc, g)
                    dve.tensor_tensor(tmp, ac, AL[:, s % 4, 0:H].unsqueeze(2).to_broadcast([P, H, C + 1]), ALU.mult).then_inc(s_e1, 1)
                    dve.wait_ge(s_e1, g + 1)
                    dve.wait_ge(s_out, g + 1)
                    dve.tensor_tensor(ac, tmp, OP[:, 0:gat.A].rearrange("p (h c) -> p h c", c=C + 1), ALU.add).then_inc(s_acc, 1)

                if first:
                    a(0)
                for s in range(SPI + (2 if last_ else 0)):
                    if not (last_ and s >= SPI - 1):
                        a(s + 1)
                    if s < SPI:
                        b(s)
                    if s - 1 < SPI and not (first and s < 1):
                        d(s - 1)
                    if s < SPI:
                        c(s)
                    if not (first and s < 2):
                        e(s - 2)

            def loop(gat):
                steps(gat, gat.i0, True, False)
                with dve.Fori(gat.i0 + 1, gat.i1 - 1) as i:
                    steps(gat, i, False, False)
                steps(gat, gat.i1 - 1, False, True)

            loop(GNN)

            dve.wait_ge(s_x2, 16 * (TILES - 1) // 8)
            dve.wait_ge(s_acc, G_SLOTS)
            den = ELR[:, :, 0:8]
            link(dve.tensor_scalar(den, ACC[:, :, :, G_CH], DEN_EPS, None, ALU.add))
            link(dve.reciprocal(den, den))
            accv = ACC[:, :, :, 0:G_CH]
            link(dve.tensor_tensor(accv, accv, den.unsqueeze(3).to_broadcast([P, TILES, G_HEADS, G_CH]), ALU.mult))
            link(dve.tensor_tensor(X[:, :, :].rearrange("p t (h c) -> p t h c", h=G_HEADS), accv,
                                   X[:, :, :].rearrange("p t (h c) -> p t h c", h=G_HEADS), ALU.add))
            for b in range(F_BLOCKS):
                n = G_BLOCKS + b
                dve.wait_ge(s_flist, 16 * (b + 1))
                if b:
                    dve.wait_ge(s_ltr, n)
                link(dve.tensor_scalar(LI[:, 1, :], LI[:, 0, :], SRC_BITS, None, ALU.arith_shift_right))
                link(dve.tensor_copy(LF[:, 1, :], LI[:, 1, :]))
                link(dve.tensor_scalar(LI[:, 1, :], LI[:, 0, :], SRC_SPAN - 1, None, ALU.bitwise_and))
                dve.tensor_copy(LF[:, 0, :], LI[:, 1, :]).then_inc(s_lf, 1)
            dve.wait_ge(s_act, 2 + G_BLOCKS + F_BLOCKS)
            dve.sem_inc(s_lcp, 1)

            layer_stats(1)
            dve.wait_ge(s_fw, 16 * 7)
            projection(1)
            h44 = HF[:, :, :].rearrange("p t (h c) -> p t h c", c=F_CH)
            for j, o in ((0, 0), (1, 4)):
                link(dve.tensor_tensor(S16A[:, :, :], HF[:, :, :], ROWS16[:, j, :].unsqueeze(1).to_broadcast([P, TILES, 16]), ALU.mult))
                link(dve.tensor_reduce(ELR[:, :, o:o + 4], S16A[:, :, :].rearrange("p t (h c) -> p t h c", c=F_CH), AX.X, ALU.add))
            dve.tensor_copy(ACC2[:, :, :, 0:F_CH], h44)
            dve.tensor_copy(FT[:, :, 0:16], HF[:, :, :])
            logits(ELR[:, :, 0:4], ELR[:, :, 4:8], FT[:, :, 16:FFN.W], EM2, F_HEADS)
            dve.sem_inc(s_td2, 1)
            loop(FFN)

            dve.wait_ge(s_acc, ALL_SLOTS)
            den = ELR[:, :, 0:4]
            link(dve.tensor_scalar(den, ACC2[:, :, :, F_CH], DEN_EPS, None, ALU.add))
            link(dve.reciprocal(den, den))

            def row16(j):
                return ROWS16[:, j, :].unsqueeze(1).to_broadcast([P, TILES, 16])

            def col(v, n=16):
                return v.unsqueeze(2).to_broadcast([P, TILES, n])
            A16 = S16A[:, :, :]
            B16 = S16B[:, :, :]
            link(dve.tensor_tensor(A16.rearrange("p t (h c) -> p t h c", c=F_CH), ACC2[:, :, :, 0:F_CH],
                                   den.unsqueeze(3).to_broadcast([P, TILES, F_HEADS, F_CH]), ALU.mult))
            link(dve.tensor_tensor(A16, A16, row16(2), ALU.add))
            link(dve.tensor_reduce(S1[:, 0, :], A16, AX.X, ALU.add))
            link(dve.tensor_scalar(S1[:, 0, :], S1[:, 0, :], 1.0 / 16, None, ALU.mult))
            link(dve.tensor_tensor(A16, A16, col(S1[:, 0, :]), ALU.subtract))
            link(dve.tensor_tensor(B16, A16, A16, ALU.mult))
            link(dve.tensor_reduce(S1[:, 1, :], B16, AX.X, ALU.add))
            dve.tensor_scalar(VAR[:, :], S1[:, 1, :], 1.0 / 16, LN_EPS, ALU.mult, ALU.add).then_inc(s_var, 1)
            dve.wait_ge(s_sd, 3)
            link(dve.reciprocal(RSTD[:, :], RSTD[:, :]))
            link(dve.tensor_tensor(A16, A16, col(RSTD[:, :]), ALU.mult))
            link(dve.tensor_tensor(A16, A16, row16(3), ALU.mult))
            link(dve.tensor_tensor(A16, A16, row16(4), ALU.add))
            sc = S4[:, 3, :, :]
            link(dve.tensor_reduce(sc, A16.rearrange("p t (h c) -> p t c h", c=F_CH), AX.X, ALU.add))
            link(dve.tensor_scalar(sc, sc, 1.0 / F_HEADS, None, ALU.mult))
            rank = S4[:, 2, :, :]
            link(dve.memset(rank, 0.0))
            for e in range(EXPERTS):
                for o in range(EXPERTS):
                    if o != e:
                        link(dve.tensor_tensor(S1[:, 2, :], sc[:, :, o], sc[:, :, e], ALU.is_ge if o < e else ALU.is_gt))
                        link(dve.tensor_tensor(rank[:, :, e], rank[:, :, e], S1[:, 2, :], ALU.add))
            link(dve.tensor_scalar(rank, rank, 2.0, None, ALU.is_lt))
            link(dve.tensor_reduce(S1[:, 0, :], sc, AX.X, ALU.max))
            dve.tensor_tensor(S4[:, 0, :, :], sc, col(S1[:, 0, :], 4), ALU.subtract).then_inc(s_var, 1)
            dve.wait_ge(s_sd, 4)
            link(dve.tensor_tensor(G4[:, :, :], S4[:, 1, :, :], rank, ALU.mult))
            link(dve.tensor_reduce(S1[:, 1, :], G4[:, :, :], AX.X, ALU.add))
            link(dve.reciprocal(S1[:, 1, :], S1[:, 1, :]))
            link(dve.tensor_tensor(G4[:, :, :], G4[:, :, :], col(S1[:, 1, :], 4), ALU.mult))

            def combine(i, nt):
                if not (isinstance(i, int) and i == 0):
                    dve.wait_ge(s_st, 16 * i)
                for e in range(EXPERTS):
                    if e:
                        dve.wait_ge(s_bias[e - 1], 4 * i + nt)
                    for j in range(nt):
                        t = 4 * i + j
                        dve.scalar_tensor_tensor(OUTS[:, j, :], B2R[:, e, :], G4[:, bass.ds(t, 1), e:e + 1].squeeze(1),
                                                 OUTS[:, j, :] if e else X[:, bass.ds(t, 1), :].squeeze(1),
                                                 ALU.mult, ALU.add).then_inc(s_bias[e], 1)
                for e in range(EXPERTS):
                    dve.wait_ge(s_y, i * EXPERTS + e + 1)
                    dve.wait_ge(s_add[e - 1] if e else s_bias[EXPERTS - 1], 4 * i + nt)
                    for j in range(nt):
                        t = 4 * i + j
                        dve.scalar_tensor_tensor(OUTS[:, j, :], (TR[0], TR[1], GP, OP)[j][:, 0:D],
                                                 G4[:, bass.ds(t, 1), e:e + 1].squeeze(1), OUTS[:, j, :],
                                                 ALU.mult, ALU.add).then_inc(s_add[e], 1)
            dve.wait_ge(s_ew, 16 * 9)
            combine(0, 4)
            with dve.Fori(1, TILES // 4) as i:
                combine(i, 4)
            combine(TILES // 4, 1)


_INS = ['x', 'src', 'dst', 'L0_gnn_W', 'L0_gnn_a_left', 'L0_gnn_a_right', 'L0_ffn_W_gat', 'L0_ffn_att_src',
        'L0_ffn_att_dst', 'L0_ffn_b_gat', 'L0_ffn_ln_gamma', 'L0_ffn_ln_beta', 'L0_ffn_W1', 'L0_ffn_b1',
        'L0_ffn_W2', 'L0_ffn_b2', 'L0_ffn_edge_index']


def kernel(**inputs):
    import numpy as _np
    import concourse.bacc as _bacc
    from concourse import mybir as _mybir
    from concourse.bass_utils import run_bass_kernel_spmd as _run

    nc = _bacc.Bacc("TRN2", target_bir_lowering=False, num_devices=1)
    arrays, args = {}, []
    for name in _INS:
        a = _np.ascontiguousarray(inputs[name])
        arrays[f"in_{name}"] = a
        args.append(nc.dram_tensor(f"in_{name}", a.shape, _mybir.dt.from_np(a.dtype), kind="ExternalInput").ap())
    out = nc.dram_tensor("out_0", (N_NODES, D), _mybir.dt.float32, kind="ExternalOutput").ap()
    build(nc, *args, out)
    r = _run(nc, [arrays], core_ids=[0])
    return r.results[0]["out_0"]
```

```python
import concourse.bass as bass
from concourse import mybir
from contextlib import ExitStack

P = 128
N_NODES, D = 6250, 256
TILES = -(-N_NODES // P)
LAST_ROWS = N_NODES - (TILES - 1) * P
NODES_PAD = TILES * P
SLOT = 256
CHUNKS = SLOT // P
SPI = 8
HALF = SPI // 2
G_HEADS, G_CH = 8, 32
F_HEADS, F_CH = 4, 4
EXPERTS, HID = 4, 512
FB = HID // P
G_EDGES, F_EDGES = 100000, 131072
G_CHUNK_ROWS = -(-G_EDGES // SLOT)
G_ITERS = -(-(G_CHUNK_ROWS + TILES - 1) // SPI)
G_SLOTS = G_ITERS * SPI
G_PAD_ROWS = G_SLOTS - (TILES - 1)
G_PAD = G_PAD_ROWS * SLOT
F_ITERS = (F_EDGES + TILES * (SLOT - 1)) // SLOT // SPI
F_SLOTS = F_ITERS * SPI
assert F_SLOTS >= (F_EDGES + TILES * (SLOT - 1)) // SLOT
ALL_SLOTS = G_SLOTS + F_SLOTS
G_BLOCKS, F_BLOCKS = -(-G_SLOTS // P), -(-F_SLOTS // P)
EPP = F_EDGES // P
SC_HALF = -(-EPP // (2 * G_ITERS))
SC_COLS = 2 * SC_HALF * G_ITERS
LIST_LEN = F_BLOCKS * P * SLOT
TRASH = LIST_LEN
LIST_ALL = LIST_LEN + SC_COLS * P
SRC_BITS = 13
SRC_SPAN = 1 << SRC_BITS
FAR = 8000
BIG = 2.0 ** 100
SLOPE = 0.2
DEN_EPS = 1e-16
LN_EPS = 1e-5


class Gat:
    def __init__(self, heads, ch, first_iter, iters):
        self.H, self.C = heads, ch
        self.HC = heads * ch
        self.A = heads * (ch + 1)
        self.EL = self.HC
        self.SPL = self.HC + heads
        self.W = self.SPL + (3 * heads + 1) // 2
        self.i0, self.i1 = first_iter, first_iter + iters
        self.HB = min(heads, 4)


GNN = Gat(G_HEADS, G_CH, 0, G_ITERS)
FFN = Gat(F_HEADS, F_CH, G_ITERS, F_ITERS)


def build(nc, x, src, dst, g_w, a_left, a_right, w_gat, att_src, att_dst, b_gat, ln_gamma, ln_beta,
          w1, b1, w2, b2, edge_index, out, dbg=None):
    f32, bf16, i32 = mybir.dt.float32, mybir.dt.bfloat16, mybir.dt.int32
    ALU, ACT, AX = mybir.AluOpType, mybir.ActivationFunctionType, mybir.AxisListType
    ctx = ExitStack()
    with ctx:
        def sb(name, shape, dt=f32):
            return ctx.enter_context(nc.sbuf_tensor(name, shape, dt))

        def pb(name, shape, dt=f32):
            return ctx.enter_context(nc.psum_tensor(name, shape, dt))

        def sem(name):
            return ctx.enter_context(nc.semaphore(name))

        def dram(name, shape, dt):
            return nc.dram_tensor(name, shape, dt, kind="Internal").ap()

        g_table = dram("g_table", (NODES_PAD, GNN.W), f32)
        f_table = dram("f_table", (NODES_PAD, FFN.W), f32)
        src_rows = dram("src_rows", (G_PAD_ROWS, SLOT), i32)
        dst_rows = dram("dst_rows", (G_PAD_ROWS, SLOT), i32)
        f_list = dram("f_list", (LIST_ALL, 1), i32)

        X = sb("X", [P, TILES, D])
        ACC = sb("ACC", [P, TILES, G_HEADS, G_CH + 1])
        EM = sb("EM", [P, TILES, 2 * G_HEADS])
        ACC2 = sb("ACC2", [P, TILES, F_HEADS, F_CH + 1])
        EM2 = sb("EM2", [P, TILES, 2 * F_HEADS])
        TROW = sb("TROW", [1, ALL_SLOTS], i32)
        ROW = sb("ROW", [P, P])
        ROWI = sb("ROWI", [P, P], i32)
        COL = sb("COL", [P, 1])
        COLI = sb("COLI", [P, 1], i32)
        IDF = sb("IDF", [P, P])
        IDB = sb("IDB", [P, P], bf16)
        ONES = sb("ONES", [P, P])
        UPPER = sb("UPPER", [P, P])
        SEL = sb("SEL", [3 * G_HEADS, G_HEADS, P], bf16)
        SEL2 = sb("SEL2", [3 * F_HEADS, F_HEADS, P], bf16)
        IDXB = sb("IDXB", [P, 2, HALF, CHUNKS], i32)
        POSB = sb("POSB", [P, 2, SC_HALF], i32)
        RECB = sb("RECB", [P, 2, SC_HALF], i32)
        DLB = sb("DLB", [P, 2, HALF, CHUNKS])
        TICK = sb("TICK", [P, 4])
        U1 = sb("U1", [P, G_HEADS])
        U2 = sb("U2", [P, G_HEADS])
        U3 = sb("U3", [P, G_HEADS])
        TB = sb("TB", [P, 2, 2 * G_HEADS])
        DLT = sb("DLT", [P, 2, G_HEADS])
        AL = sb("AL", [P, 4, G_HEADS])
        L1 = sb("L1", [P, CHUNKS, G_HEADS])
        L2 = sb("L2", [P, CHUNKS, G_HEADS])
        L3 = sb("L3", [P, CHUNKS, G_HEADS])
        LG = sb("LG", [P, 2, CHUNKS, G_HEADS])
        TMPA = sb("TMPA", [P, GNN.A])
        STAT = sb("STAT", [P, TILES, 6])
        MEAN = sb("MEAN", [P, TILES])
        VAR = sb("VAR", [P, TILES])
        RSTD = sb("RSTD", [P, TILES])
        ELR = sb("ELR", [P, TILES, 2 * G_HEADS])
        TCOLS = sb("TCOLS", [P, TILES * FFN.W])
        ET = TCOLS[:, 0:TILES * (GNN.W - GNN.HC)].rearrange("p (t w) -> p t w", t=TILES)
        FT = TCOLS[:, :].rearrange("p (t w) -> p t w", t=TILES)
        WREG = sb("WREG", [P, 2 * D + 2 * (D + 2 * G_HEADS)])
        WSB = WREG[:, 0:2 * D].rearrange("p (b d) -> p b d", b=2)
        WA = WREG[:, 2 * D:].rearrange("p (b d) -> p b d", b=2)
        S4 = WREG[:, 0:4 * TILES * 4].rearrange("p (a t e) -> p a t e", a=4, t=TILES)
        ACOL = sb("ACOL", [P, 2, 2])
        ADIAG = sb("ADIAG", [P, 2, 2 * G_HEADS])
        WGAT = sb("WGAT", [P, 2, F_HEADS * F_CH])
        HF = sb("HF", [P, TILES, F_HEADS * F_CH])
        ROWS16 = sb("ROWS16", [P, 5, F_HEADS * F_CH])
        B1R = sb("B1R", [EXPERTS * FB, P])
        B1C = sb("B1C", [P, EXPERTS * FB])
        G4 = sb("G4", [P, TILES, EXPERTS])
        S16A = sb("S16A", [P, TILES, 16])
        S16B = sb("S16B", [P, TILES, 16])
        S1 = sb("S1", [P, 4, TILES])
        LI = sb("LI", [P, 2, SLOT], i32)
        LF = sb("LF", [P, 2, SLOT])
        CNT = sb("CNT", [P, TILES])
        CNT2 = sb("CNT2", [P, TILES])
        Q = sb("Q", [P, TILES])
        QI = sb("QI", [P, TILES], i32)
        THR = sb("THR", [P, TILES])
        BASE = sb("BASE", [P, TILES])
        SLOT0 = sb("SLOT0", [P, TILES + 1])
        NSL = sb("NSL", [P, TILES])
        ZERO = sb("ZERO", [P, TILES])
        TCOL = sb("TCOL", [P, G_BLOCKS + F_BLOCKS])
        CCOL = sb("CCOL", [P, G_BLOCKS])
        CIDX = sb("CIDX", [P, G_BLOCKS], i32)
        SCOL = sb("SCOL", [P, 1])
        JUNK = sb("JUNK", [P, 64])

        sizes = [2 * ALL_SLOTS, 2 * ALL_SLOTS, SC_COLS, SC_COLS, SPI * CHUNKS * GNN.W, 4 * SLOT, SLOT, 4 * SLOT, SLOT,
                 2 * CHUNKS * GNN.A]
        LOOP = sb("LOOP", [P, sum(sizes)])
        at = [sum(sizes[:k]) for k in range(len(sizes) + 1)]
        part = [LOOP[:, at[k]:at[k + 1]] for k in range(len(sizes))]
        IDX = part[0].bitcast(i32).rearrange("p (g k) -> p g k", k=CHUNKS)
        DL = part[1].rearrange("p (g k) -> p g k", k=CHUNKS)
        POS = part[2].bitcast(i32)
        REC = part[3].bitcast(i32)
        R = part[4].rearrange("p (s k w) -> p s k w", s=SPI, k=CHUNKS)
        SF = part[5].rearrange("p (s k n) -> p s k n", s=4, k=CHUNKS)
        NE = part[6].bitcast(bf16).rearrange("p (s k n) -> p s k n", s=2, k=CHUNKS)
        ST = part[7].rearrange("p (s k n) -> p s k n", s=4, k=CHUNKS)
        ELT = part[8].bitcast(bf16)[0:3 * G_HEADS].rearrange("p (s k n) -> p s k n", s=2, k=CHUNKS)
        MSG = part[9].rearrange("p (s k a) -> p s k a", s=2, k=CHUNKS)
        HP = HALF * G_HEADS
        DT = S16A[:, :, :].rearrange("p t c -> p (t c)")[0:HP, 0:SLOT]
        NF = S16A[:, :, :].rearrange("p t c -> p (t c)")[0:HP, SLOT:2 * SLOT + 1]
        PEN = S16B[:, :, :].rearrange("p t c -> p (t c)")[0:HP, 0:SLOT + 1]
        SCN = S16B[:, :, :].rearrange("p t c -> p (t c)")[0:HP, SLOT + 1:2 * SLOT + 1]
        LAST = ELR[:, :, :].rearrange("p t c -> p (t c)")[0:HP, 0:SLOT]
        UB = HF[:, :, :].rearrange("p t c -> p (t c)")[:, 0:2 * CHUNKS * HALF * 2 * G_HEADS] \
            .rearrange("p (q k s v) -> p q k s v", q=2, k=CHUNKS, s=HALF)
        EH, DH = (HF[:, :, :].rearrange("p t c -> p (t c)")[:, 256 + 64 * j:320 + 64 * j]
                  .rearrange("p (k s h) -> p k s h", k=CHUNKS, s=HALF) for j in range(2))
        XN = part[5][:, 0:2 * D].rearrange("p (r d) -> p r d", r=2)
        XT = part[5][:, 2 * D:4 * D].rearrange("p (r k n) -> p r k n", r=2, k=2)
        STG = part[9][:, 0:2 * (D + 2 * G_HEADS)].rearrange("p (r d) -> p r d", r=2)
        w_at = [0, EXPERTS * 2 * HID, EXPERTS * FB * D, FB * 4 * P, 4 * D, EXPERTS * D]
        w_at = [sum(w_at[:k + 1]) for k in range(len(w_at))]
        assert w_at[-1] <= at[-1]
        W1S = LOOP[:, w_at[0]:w_at[1]].rearrange("p (e k n) -> p e k n", e=EXPERTS, k=2)
        W2S = LOOP[:, w_at[1]:w_at[2]].rearrange("p (e f n) -> p e f n", e=EXPERTS, f=FB)
        HH = LOOP[:, w_at[2]:w_at[3]].rearrange("p (f n) -> p f n", f=FB)
        OUTS = LOOP[:, w_at[3]:w_at[4]].rearrange("p (j n) -> p j n", n=D)
        B2R = LOOP[:, w_at[4]:w_at[5]].rearrange("p (e n) -> p e n", e=EXPERTS)

        assert 8 * EPP <= (TILES - 1) * D
        xflat = X[:, :, :].rearrange("p t d -> p (t d)")

        def edges_at(k):
            return xflat[:, k * EPP:(k + 1) * EPP]
        fdst, fsrc, ftmi = (edges_at(k).bitcast(i32) for k in (0, 1, 7))
        ftile, fmask, fscan, fpos, ftmp = (edges_at(k) for k in (2, 3, 4, 5, 6))
        HR, HW = 125, G_EDGES // 125
        gdst = part[4][:, 0:HW].bitcast(i32)
        gdstf = part[4][:, HW:2 * HW]
        gjunk = part[4][:, 2 * HW:3 * HW]
        FILL = part[4][:, 3 * HW:3 * HW + LIST_LEN // P // 2].bitcast(i32)

        XP = pb("XP", [P, 4, 512])
        TR = [pb(f"TR{r}", [P, 512]) for r in range(2)]
        GP = pb("GP", [P, 512])
        OP = pb("OP", [P, 512])

        s_x = sem("s_x"); s_w = sem("s_w"); s_pad = sem("s_pad"); s_padt = sem("s_padt")
        s_ge = sem("s_ge"); s_fe = sem("s_fe"); s_rows = sem("s_rows"); s_fill = sem("s_fill"); s_fillt = sem("s_fillt")
        s_fw = sem("s_fw"); s_ew = sem("s_ew"); s_c = sem("s_c"); s_iota = sem("s_iota")
        dv = sem("dv")
        s_wt = sem("s_wt"); s_pe = sem("s_pe"); s_act = sem("s_act")
        s_cidx = sem("s_cidx"); s_lrow = sem("s_lrow"); s_flist = sem("s_flist"); s_lf = sem("s_lf"); s_ltr = sem("s_ltr"); s_lcp = sem("s_lcp")
        s_xn = sem("s_xn"); s_pt = sem("s_pt"); s_xt = sem("s_xt"); s_pj = sem("s_pj"); s_ev = sem("s_ev"); s_stg = sem("s_stg")
        s_stat = sem("s_stat"); s_hist = sem("s_hist"); s_rk = sem("s_rk")
        s_tdma = [sem(f"s_tdma{r}") for r in range(2)]
        s_td2 = sem("s_td2"); s_ready = sem("s_ready")
        s_stage = [sem(f"s_stage{h}") for h in range(2)]
        s_sc = [sem(f"s_sc{h}") for h in range(2)]
        s_row = [sem(f"s_row{s}") for s in range(SPI)]
        s_tick = sem("s_tick")
        s_sf = sem("s_sf"); s_ne = sem("s_ne"); s_tr = sem("s_tr"); s_elt = sem("s_elt"); s_stc = sem("s_stc")
        s_mask = sem("s_mask"); s_red = sem("s_red"); s_b2 = sem("s_b2"); s_b3 = sem("s_b3"); s_b4 = sem("s_b4")
        s_er = sem("s_er"); s_dlt = sem("s_dlt"); s_mset = sem("s_mset"); s_alpha = sem("s_alpha")
        s_gat = sem("s_gat"); s_c1 = sem("s_c1"); s_c2 = sem("s_c2"); s_c3 = sem("s_c3"); s_lg = sem("s_lg")
        s_wexp = sem("s_wexp"); s_msg = sem("s_msg"); s_out = sem("s_out"); s_e1 = sem("s_e1"); s_acc = sem("s_acc")
        s_h1 = sem("s_h1"); s_hh = sem("s_hh"); s_y = sem("s_y"); s_o1 = sem("s_o1"); s_o2 = sem("s_o2")
        s_t1 = sem("s_t1"); s_dlb = [sem(f"s_dlb{h}") for h in range(2)]; s_b1 = sem("s_b1"); s_eh = sem("s_eh"); s_dt = sem("s_dt"); s_nf = sem("s_nf"); s_pen = sem("s_pen"); s_scan = sem("s_scan")
        s_last = sem("s_last"); s_t2 = sem("s_t2"); s_ub = sem("s_ub"); s_u = sem("s_u")
        s_st = sem("s_st"); s_var = sem("s_var"); s_sd = sem("s_sd"); s_x2 = sem("s_x2"); s_fpos = sem("s_fpos")
        s_bias = [sem(f"s_bias{e}") for e in range(EXPERTS)]
        s_add = [sem(f"s_add{e}") for e in range(EXPERTS)]

        block = ctx.enter_context(nc.Block())

        def wait(eng, semaphore, value):
            if not (isinstance(value, int) and value < 1):
                eng.wait_ge(semaphore, value)

        def span(first, last):
            return range(-2 if first else 0, SPI + (2 if last else 0))

        def staged(gat, i):
            return 64 * i + 64 if gat is GNN else 64 * G_ITERS + 32 * (i - G_ITERS) + 32

        def has(slot, first, last):
            return not (first and slot < 0) and not (last and slot >= SPI)

        def bank(n, cols):
            return XP[:, n, 0:cols]

        x_full = x[0:(TILES - 1) * P, :].rearrange("(t p) d -> p t d", p=P)
        GAT_T = {0: (ACC, EM, SEL, g_table), 1: (ACC2, EM2, SEL2, f_table)}

        @block.sync
        def _(sp):
            with nc.allow_non_contiguous_dma("small rows"):
                XL = 8
                for j in range(0, TILES - 1, XL):
                    sp.dma_start(X[:, j:j + XL, :], x_full[:, j:j + XL, :]).then_inc(s_x, 16)
                sp.wait_ge(s_c, 1)
                sp.dma_start(X[0:LAST_ROWS, TILES - 1, :], x[(TILES - 1) * P:N_NODES, :]).then_inc(s_x, 16)
                sp.dma_start(gdst[0:HR, :], dst.rearrange("(p n) -> p n", p=HR)).then_inc(s_ge, 16)
                sp.dma_start(WSB[:, :, :], g_w.rearrange("(b p) d -> p b d", p=P)).then_inc(s_w, 16)
                for b in range(2):
                    for c, a in enumerate((a_left, a_right)):
                        sp.dma_start(ACOL[:, b, c:c + 1],
                                     a.rearrange("h (c one) -> (h c) one", one=1)[b * P:(b + 1) * P, :]).then_inc(s_w, 16)
                for rows, a in ((src_rows, src), (dst_rows, dst)):
                    flat = rows.rearrange("a b -> (a b)")
                    sp.dma_start(flat[0:G_EDGES].rearrange("(a b) -> a b", a=16),
                                 a.rearrange("(a b) -> a b", a=16)).then_inc(s_pad, 16)
                sp.wait_ge(s_padt, 2)
                npad = (G_PAD - G_EDGES) // 32
                for k, rows in enumerate((src_rows, dst_rows)):
                    flat = rows.rearrange("a b -> (a b)")
                    sp.dma_start(flat[G_EDGES:G_PAD].rearrange("(a b) -> a b", a=32),
                                 LI[0:32, k, 0:npad]).then_inc(s_pad, 16)
                sp.wait_ge(s_fillt, 1)
                for k in range(2):
                    sp.dma_start(f_list[k * LIST_LEN // 2:(k + 1) * LIST_LEN // 2, 0].rearrange("(p n) -> p n", p=P),
                                 FILL).then_inc(s_fill, 16)
                sp.dma_start(WGAT[:, :, :], w_gat.rearrange("(k p) n -> p k n", p=P)).then_inc(s_fw, 16)
                for j, a in enumerate((att_src.rearrange("h c -> (h c)"), att_dst.rearrange("h c -> (h c)"),
                                       b_gat, ln_gamma, ln_beta)):
                    sp.dma_start(ROWS16[:, j, :], a.partition_broadcast(P)).then_inc(s_fw, 16)
                sp.dma_start(B1R[:, :], b1.rearrange("e (f p) -> (e f) p", p=P)).then_inc(s_fw, 16)

                def table_rows(i, r):
                    sp.wait_ge(s_stg, 2 * i + r + 1)
                    sp.dma_start(g_table[bass.ds(256 * i + P * r, P), 0:D], STG[:, r, 0:D]).then_inc(s_tdma[r], 16)
                with sp.Fori(0, TILES // 2) as i:
                    for r in range(2):
                        table_rows(i, r)
                table_rows(TILES // 2, 0)
                sp.wait_ge(s_xn, TILES)
                e2 = edge_index.rearrange("a (p n) -> a p n", p=P)
                sp.dma_start(fdst, e2[1]).then_inc(s_fe, 16)
                sp.dma_start(fsrc, e2[0]).then_inc(s_fe, 16)
                sp.wait_ge(s_td2, 1)
                sp.dma_start(g_table.rearrange("(t p) w -> p t w", p=P)[:, :, D:GNN.W], ET[:, :, :]).then_inc(s_ready, 16)

                def stage(gat, i, h):
                    if gat is GNN:
                        if not (isinstance(i, int) and i == 0):
                            sp.wait_ge(s_sc[h], 16 * SC_HALF * i)
                        sp.dma_start(POSB[:, h, :], POS[:, bass.ds((2 * i + h) * SC_HALF, SC_HALF)]).then_inc(s_stage[h], 16)
                        sp.dma_start(RECB[:, h, :], REC[:, bass.ds((2 * i + h) * SC_HALF, SC_HALF)]).then_inc(s_stage[h], 16)
                    if not (isinstance(i, int) and i == 0):
                        for s in range(h * HALF, (h + 1) * HALF):
                            sp.wait_ge(s_row[s], 32 * i)
                        sp.wait_ge(s_dlb[h], 32 * i)
                    sp.dma_start(IDXB[:, h, :, :], IDX[:, bass.ds(SPI * i + HALF * h, HALF), :]).then_inc(s_stage[h], 16)
                    sp.dma_start(DLB[:, h, :, :], DL[:, bass.ds(SPI * i + HALF * h, HALF), :]).then_inc(s_stage[h], 16)

                sp.wait_ge(s_lcp, 1)
                for j in range(0, TILES - 1, XL):
                    sp.dma_start(X[:, j:j + XL, :], x_full[:, j:j + XL, :]).then_inc(s_x2, 16)
                for gat in (GNN, FFN):
                    if gat is FFN:
                        sp.wait_ge(s_sc[0], 16 * SC_HALF * G_ITERS)
                        sp.wait_ge(s_sc[1], 16 * SC_HALF * G_ITERS)
                        for b in range(F_BLOCKS):
                            if b:
                                sp.wait_ge(s_lf, G_BLOCKS + b)
                            sp.dma_start(LI[:, 0, :], f_list[b * P * SLOT:(b + 1) * P * SLOT, 0]
                                         .rearrange("(p n) -> p n", p=P)).then_inc(s_flist, 16)
                        sp.wait_ge(s_td2, 2)
                        sp.dma_start(f_table.rearrange("(t p) w -> p t w", p=P), FT[:, :, :]).then_inc(s_ready, 16)
                        sp.wait_ge(s_lcp, 2)
                    for h in range(2):
                        stage(gat, gat.i0, h)
                    with sp.Fori(gat.i0 + 1, gat.i1) as i:
                        for h in range(2):
                            stage(gat, i, h)

                sp.wait_ge(s_acc, ALL_SLOTS)
                for e in range(EXPERTS):
                    sp.dma_start(W1S[:, e, :, :], w1[e].rearrange("(k p) n -> p k n", p=P)).then_inc(s_ew, 16)
                    sp.dma_start(W2S[:, e, :, :], w2[e].rearrange("(f p) n -> p f n", p=P)).then_inc(s_ew, 16)
                sp.dma_start(B2R, b2.partition_broadcast(P)).then_inc(s_ew, 16)
                with sp.Fori(0, TILES // 4) as i:
                    sp.wait_ge(s_add[EXPERTS - 1], 4 * i + 4)
                    sp.dma_start(out[bass.ds(i * 4 * P, 4 * P), :].rearrange("(j p) d -> p j d", p=P), OUTS).then_inc(s_st, 16)
                sp.wait_ge(s_add[EXPERTS - 1], TILES)
                sp.dma_start(out[(TILES - 1) * P:N_NODES, :], OUTS[0:LAST_ROWS, 0, :]).then_inc(s_st, 16)
                sp.wait_ge(s_st, 16 * (TILES // 4 + 1))

        @block.gpsimd
        def _(pool):
            pool.iota(ROWI[:, :], pattern=[[1, P]], base=0, channel_multiplier=0).then_inc(s_iota, 1)
            pool.iota(COLI[:, :], pattern=[[0, 1]], base=0, channel_multiplier=1).then_inc(s_iota, 1)
            pool.iota(POS[:, EPP:SC_COLS], pattern=[[1, SC_COLS - EPP]], base=TRASH + F_EDGES,
                      channel_multiplier=SC_COLS - EPP).then_inc(s_iota, 1)
            pool.memset(REC[:, EPP:SC_COLS], 0).then_inc(s_iota, 1)
            pool.memset(X[:, TILES - 1, :], 0.0).then_inc(s_c, 1)
            pool.memset(TICK[:, :], 0.0).then_inc(s_tick, 1)
            pool.memset(LI[:, 0, 0:SLOT], 0).then_inc(s_padt, 1)
            pool.memset(LI[:, 1, 0:SLOT], FAR).then_inc(s_padt, 1)
            pool.memset(FILL, P * SRC_SPAN).then_inc(s_fillt, 1)
            pool.wait_ge(s_pad, 64)
            pool.wait_ge(s_cidx, 1)
            for b in range(G_BLOCKS):
                if b:
                    pool.wait_ge(s_lf, b)
                for k, rows in enumerate((src_rows, dst_rows)):
                    pool.indirect_dma_start(out=LI[:, k, :], out_offset=None, in_=rows,
                                            in_offset=bass.IndirectOffsetOnAxis(ap=CIDX[:, b:b + 1], axis=0)).then_inc(s_lrow, 16)

            def half(gat, i, h):
                table = g_table if gat is GNN else f_table
                for pair in range(2):
                    first = pair * HALF // 2
                    pool.wait_ge(s_tick, 4 * i + 2 * h + pair + 1)
                    if pair == 0:
                        pool.wait_ge(s_stage[h], staged(gat, i))
                    if not (isinstance(i, int) and i == gat.i0):
                        pool.wait_ge(s_msg, SPI * (i - 1) + HALF * h + first + HALF // 2)
                    pool.tensor_tensor(TICK[:, 0:1], TICK[:, 1:2], TICK[:, 2:3], ALU.add).then_inc(s_tick, 1)
                    for s in range(first, first + HALF // 2):
                        for k in range(CHUNKS):
                            pool.indirect_dma_start(out=R[:, h * HALF + s, k, 0:gat.W], out_offset=None, in_=table,
                                                    in_offset=bass.IndirectOffsetOnAxis(ap=IDXB[:, h, s, k:k + 1], axis=0)
                                                    ).then_inc(s_row[h * HALF + s], 16)
                    for c in range(pair * SC_HALF // 2, (pair + 1) * SC_HALF // 2 if gat is GNN else 0):
                        pool.indirect_dma_start(out=f_list, out_offset=bass.IndirectOffsetOnAxis(ap=POSB[:, h, c:c + 1], axis=0),
                                                in_=RECB[:, h, c:c + 1], in_offset=None).then_inc(s_sc[h], 16)

            pool.wait_ge(s_xn, TILES)
            pool.iota(ftmi, pattern=[[1, EPP]], base=TRASH, channel_multiplier=EPP).then_inc(s_iota, 1)
            pool.wait_ge(s_fill, 32)
            for k, gat in enumerate((GNN, FFN)):
                if gat is GNN:
                    pool.wait_ge(s_tdma[0], 16 * (TILES // 2 + 1))
                    pool.wait_ge(s_tdma[1], 16 * (TILES // 2))
                pool.wait_ge(s_ready, 16 * (k + 1))
                for h in range(2):
                    half(gat, gat.i0, h)
                with pool.Fori(gat.i0 + 1, gat.i1) as i:
                    for h in range(2):
                        half(gat, i, h)

        @block.scalar
        def _(act):
            def list_copies(first, blocks):
                for b in range(blocks):
                    n = first + b
                    g0 = (0 if first == 0 else G_SLOTS) + P * b
                    w = min(P, (G_SLOTS if first == 0 else ALL_SLOTS) - g0)
                    act.wait_ge(s_ltr, n + 1)
                    for k in range(CHUNKS):
                        act.activation(IDX[:, g0:g0 + w, k], TR[0][:, k * P:k * P + w], ACT.Copy)
                        act.activation(DL[:, g0:g0 + w, k], TR[1][:, k * P:k * P + w], ACT.Copy)
                    act.activation(TROW[0:1, g0:g0 + w], GP[0:1, 0:w], ACT.Copy).then_inc(s_act, 1)

            def rstd(k):
                act.wait_ge(s_var, k + 1)
                act.activation(RSTD[:, :], VAR[:, :], ACT.Sqrt).then_inc(s_sd, 1)

            def project(phase, i, r):
                tau = (TILES if phase else 0) + 2 * i + r
                first = isinstance(tau, int) and tau < 2
                act.wait_ge(s_pt, tau + 1)
                act.activation(XT[:, r, :, :], TR[r][:, 0:2 * P].rearrange("p (k n) -> p k n", k=2), ACT.Copy).then_inc(s_xt, 1)
                if phase == 0:
                    act.wait_ge(s_pj, tau + 1)
                    if not first:
                        act.wait_ge(s_tdma[r], 16 * i)
                        act.wait_ge(s_ev, tau - 1)
                    act.activation(STG[:, r, :], (GP, OP)[r][:, 0:D + 2 * G_HEADS], ACT.Copy).then_inc(s_stg, 1)

            def steps(gat, it, first, last):
                H, C, n0 = gat.H, gat.C, it * SPI
                for s in span(first, last):
                    g = n0 + s
                    if gat is GNN and s % HALF == HALF - 1 and has(s + 1, first, last):
                        n = 2 * it + (s + 1) // HALF
                        act.wait_ge(s_t1, n + 1)
                        wait(act, s_nf, n)
                        act.activation(DT, XP[0:HP, 0, SLOT:2 * SLOT], ACT.Copy).then_inc(s_dt, 1)
                    if has(s - 1, first, last):
                        act.wait_ge(s_lg, g)
                        wait(act, s_out, g - 2)
                        act.activation(MSG[:, (s - 1) % 2, :, 0:gat.A].rearrange("p k (h c) -> p k h c", c=C + 1)[:, :, :, C],
                                       LG[:, (s - 1) % 2, :, 0:H], ACT.Exp).then_inc(s_wexp, 1)
                    if gat is GNN and s % HALF == HALF - 1 and has(s + 1, first, last):
                        n = 2 * it + (s + 1) // HALF
                        act.wait_ge(s_t2, n + 1)
                        wait(act, s_u, 4 * (n - 1))
                        act.activation(UB[:, (s + 1) // HALF % 2, :, :, :],
                                       XP[:, 1, 0:P].rearrange("p (k s v) -> p k s v", k=CHUNKS, s=HALF),
                                       ACT.Copy).then_inc(s_ub, 1)
                    if has(s + 2, first, last):
                        q = s % 2
                        if gat is FFN:
                            act.wait_ge(s_sf, g + 3)
                            if not (first and s < 0):
                                act.wait_ge(s_mask, g + 1 - G_SLOTS)
                            act.activation(NE[:, q, :, :], SF[:, (s + 2) % 4, :, :], ACT.Copy, bias=-BIG, scale=BIG).then_inc(s_ne, 1)
                        act.wait_ge(s_tr, g + 3)
                        if gat is FFN:
                            act.activation(ELT[0:3 * H, q, :, :],
                                           TR[q][0:3 * H, 256:256 + P].bitcast(bf16).rearrange("p (k n) -> p k n", k=CHUNKS),
                                           ACT.Copy).then_inc(s_elt, 1)
                        wait(act, s_gat, g - 1)
                        if gat is GNN:
                            act.activation(ST[:, (s + 2) % 4, :, :], TR[q][:, 0:2 * P].rearrange("p (k n) -> p k n", k=CHUNKS),
                                           ACT.Copy).then_inc(s_stc, 1)
                        else:
                            act.activation(ST[:, (s + 2) % 4, :, :], TR[q][:, 0:P].bitcast(bf16).rearrange("p (k n) -> p k n", k=CHUNKS),
                                           ACT.Copy, bias=1.0, scale=1.0 / BIG).then_inc(s_stc, 1)
                    if has(s, first, last):
                        act.wait_ge(s_dlt, g + 1)
                        wait(act, s_acc, g - 3)
                        act.activation(AL[:, s % 4, 0:H], DLT[:, s % 2, 0:H], ACT.Exp).then_inc(s_alpha, 1)
                    if gat is GNN and s % HALF == HALF - 2 and has(s + 2, first, last):
                        n, h = 2 * it + (s + 2) // HALF, (s + 2) // HALF % 2
                        wait(act, s_t1, n)
                        for sl in range(h * HALF, h * HALF + HALF):
                            act.wait_ge(s_row[sl], it * 32 + 32 * (1 + (s + 2) // SPI))
                        act.activation(EH, R[:, h * HALF:(h + 1) * HALF, :, gat.EL:gat.EL + H].rearrange("p s k h -> p k s h"),
                                       ACT.Copy)
                        act.wait_ge(s_stage[h], staged(gat, it + (s + 2) // SPI))
                        act.activation(DH, DLB[:, h, :, :].rearrange("p s k -> p k s").unsqueeze(3).to_broadcast([P, CHUNKS, HALF, H]),
                                       ACT.Copy).then_inc(s_eh, 1)

            act.wait_ge(s_wt, 1)
            for b in range(2):
                act.activation(WA[:, b, 0:D], bank(b, D), ACT.Copy)
            for b in range(2):
                act.activation(WA[:, b, D:D + 16], XP[:, b, D:D + 16], ACT.Copy).then_inc(s_act, 1)
            rstd(0)
            for r in range(2):
                project(0, 0, r)
            with act.Fori(1, TILES // 2) as i:
                for r in range(2):
                    project(0, i, r)
            project(0, TILES // 2, 0)
            list_copies(0, G_BLOCKS)
            steps(GNN, 0, True, False)
            with act.Fori(1, G_ITERS - 1) as i:
                steps(GNN, i, False, False)
            steps(GNN, G_ITERS - 1, False, True)
            list_copies(G_BLOCKS, F_BLOCKS)
            rstd(1)
            for r in range(2):
                project(1, 0, r)
            with act.Fori(1, TILES // 2) as i:
                for r in range(2):
                    project(1, i, r)
            project(1, TILES // 2, 0)
            steps(FFN, FFN.i0, True, False)
            with act.Fori(FFN.i0 + 1, FFN.i1 - 1) as i:
                steps(FFN, i, False, False)
            steps(FFN, FFN.i1 - 1, False, True)
            rstd(2)
            act.wait_ge(s_var, 4)
            act.activation(S4[:, 1, :, :], S4[:, 0, :, :], ACT.Exp).then_inc(s_sd, 1)
            act.wait_ge(s_wt, 2)
            act.activation(B1C[:, :], GP[:, 0:EXPERTS * FB], ACT.Copy).then_inc(s_act, 1)
            act.wait_ge(s_act, 2 + G_BLOCKS + F_BLOCKS + 1)

            def hidden(i, cols):
                for e in range(EXPERTS):
                    for f in range(FB):
                        m = (i * EXPERTS + e) * FB + f
                        act.wait_ge(s_h1, m + 1)
                        if f == 0 and not (isinstance(i, int) and i == 0 and e == 0):
                            act.wait_ge(s_y, i * EXPERTS + e)
                        act.activation(HH[:, f, 0:cols], XP[:, f, 0:cols], ACT.Gelu,
                                       bias=B1C[:, e * FB + f:e * FB + f + 1]).then_inc(s_hh, 1)
            hidden(0, 512)
            with act.Fori(1, TILES // 4) as i:
                hidden(i, 512)
            hidden(TILES // 4, P)

        @block.tensor
        def _(pe):
            pe.wait_ge(s_w, 80)
            pe.wait_ge(s_rows, 1)
            for kb in range(2):
                for ob in range(2):
                    pe.transpose(XP[:, kb, ob * P:(ob + 1) * P], WSB[:, ob, kb * P:(kb + 1) * P], IDF[:, :])
                for ob in range(2):
                    last = pe.matmul(XP[:, kb, D:D + 16], WSB[:, ob, kb * P:(kb + 1) * P], ADIAG[:, ob, :],
                                     start=(ob == 0), stop=(ob == 1), skip_group_check=True)
            last.then_inc(s_wt, 1)
            pe.wait_ge(s_rows, 2)
            pe.matmul(XP[:, 2, 0:TILES], ONES[0:HR, :], CNT[0:HR, :], start=True, stop=True).then_inc(s_rk, 1)

            def lists(first, blocks):
                for b in range(blocks):
                    n = first + b
                    pe.wait_ge(s_lf, n + 1)
                    if n:
                        pe.wait_ge(s_act, 2 + n)
                    for k in range(CHUNKS):
                        pe.transpose(TR[0][:, k * P:(k + 1) * P], LF[:, 0, k * P:(k + 1) * P], IDF[:, :])
                        pe.transpose(TR[1][:, k * P:(k + 1) * P], LF[:, 1, k * P:(k + 1) * P], IDF[:, :])
                    pe.transpose(GP[0:1, 0:P], TCOL[:, n:n + 1], IDF[:, :]).then_inc(s_ltr, 1)

            def project(phase, i, r):
                tau = (TILES if phase else 0) + 2 * i + r
                first = isinstance(tau, int) and tau < 2
                pe.wait_ge(s_xn, tau + 1)
                if not first:
                    pe.wait_ge(s_xt, tau - 1)
                for k in range(2):
                    last = pe.transpose(TR[r][:, k * P:(k + 1) * P], XN[:, r, k * P:(k + 1) * P], IDF[:, :])
                last.then_inc(s_pt, 1)
                pe.wait_ge(s_xt, tau + 1)
                if not first:
                    pe.wait_ge(s_stg if phase == 0 else s_ev, tau - 1)
                w = WA if phase == 0 else WGAT
                cols = D + 16 if phase == 0 else 16
                for k in range(2):
                    last = pe.matmul((GP, OP)[r][:, 0:cols], XT[:, r, k, :], w[:, k, :], start=(k == 0), stop=(k == 1))
                last.then_inc(s_pj, 1)

            def steps(gat, it, first, last_):
                H, C, HB, n0 = gat.H, gat.C, gat.HB, it * SPI

                def selection_t(s):
                    g, q = n0 + s, s % 2
                    pe.wait_ge(s_sf, g + 1)
                    if s % HALF == HALF - 1:
                        pe.sem_inc(s_dlb[s // HALF % 2], 32)
                    wait(pe, s_stc, g - 1)
                    if gat is FFN:
                        if not (first and s < 2):
                            pe.wait_ge(s_elt, g - 1 - G_SLOTS)
                        pe.wait_ge(s_row[s % SPI], it * 32 + 32 * (1 + s // SPI))
                        for k in range(CHUNKS):
                            pe.transpose(TR[q][0:3 * H, 256 + k * 64:256 + (k + 1) * 64].bitcast(bf16),
                                         R[:, s % SPI, k, gat.SPL:gat.SPL + 3 * H // 2].bitcast(bf16), IDB[:, :])
                        pe.wait_ge(s_ne, g + 1 - G_SLOTS)
                    for k in range(CHUNKS):
                        if gat is GNN:
                            last = pe.transpose(TR[q][:, k * P:(k + 1) * P], SF[:, s % 4, k, :], IDF[:, :])
                        else:
                            last = pe.transpose(TR[q][:, k * 64:(k + 1) * 64].bitcast(bf16), NE[:, q, k, :], IDB[:, :])
                    last.then_inc(s_tr, 1)

                def masked_logits(s):
                    g, q = n0 + s, s % 2
                    pe.wait_ge(s_ne, g + 1 - G_SLOTS)
                    pe.wait_ge(s_elt, g + 1 - G_SLOTS)
                    if not (first and s < 2):
                        pe.wait_ge(s_red, g - 1 - G_SLOTS)
                    for k in range(CHUNKS):
                        o = XP[:, 2 * q + k, :].rearrange("p (h n) -> p h n", h=HB)
                        pe.matmul(o, NE[:, q, k, :], IDB[:, :].unsqueeze(1).to_broadcast([P, HB, P]),
                                  start=True, stop=False)
                        for h in range(HB):
                            last = pe.matmul(o[:, h, :], SEL2[0:3 * H, h, :], ELT[0:3 * H, q, k, :],
                                             start=False, stop=(h == HB - 1))
                    last.then_inc(s_mask, 1)

                def rows_of_logits(s):
                    n, h = 2 * it + s // HALF, s // HALF % 2
                    pe.wait_ge(s_eh, n + 1)
                    wait(pe, s_scan, n)
                    wait(pe, s_dt, n)
                    for k in range(CHUNKS):
                        pe.transpose(XP[0:HP, 0, k * P:(k + 1) * P], EH[:, k, :, :].rearrange("p s h -> p (s h)"), IDF[:, :])
                    for k in range(CHUNKS):
                        last = pe.transpose(XP[0:HP, 0, SLOT + k * P:SLOT + (k + 1) * P],
                                            DH[:, k, :, :].rearrange("p s h -> p (s h)"), IDF[:, :])
                    last.then_inc(s_t1, 1)

                def maxima_back(s):
                    n = 2 * it + s // HALF
                    pe.wait_ge(s_last, n + 1)
                    wait(pe, s_ub, n)
                    for k in range(CHUNKS):
                        o = XP[:, 1, k * 64:(k + 1) * 64].rearrange("p (s v) -> p s v", s=HALF)
                        pe.matmul(o[:, :, 0:H], LAST[:, k * P:(k + 1) * P], IDF[0:HP, 0:HP], start=True, stop=True, skip_group_check=True)
                        last = pe.matmul(o[:, :, H:2 * H], PEN[:, 1 + k * P:1 + (k + 1) * P], IDF[0:HP, 0:HP], start=True, stop=True, skip_group_check=True)
                    last.then_inc(s_t2, 1)

                def maxima(s):
                    g = n0 + s
                    pe.wait_ge(s_ub, 2 * it + s // HALF + 1)
                    pe.wait_ge(s_sf, g + 1)
                    wait(pe, s_b2, g - 1)
                    for k in range(CHUNKS):
                        last = pe.matmul(XP[:, 2 + s % 2, 0:2 * H], SF[:, s % 4, k, :], UB[:, s // HALF % 2, k, s % HALF, :],
                                         start=(k == 0), stop=(k == CHUNKS - 1))
                    last.then_inc(s_u, 1)

                def at_edges(s):
                    g, q = n0 + s, s % 2
                    pe.wait_ge(s_b4, g + 1)
                    pe.wait_ge(s_er, g + 1)
                    pe.wait_ge(s_stc, g + 1)
                    wait(pe, s_c3, g)
                    for k in range(CHUNKS):
                        last = pe.matmul(GP[:, k * 2 * H:(k + 1) * 2 * H], ST[:, s % 4, k, :], TB[:, q, 0:2 * H],
                                         start=True, stop=True, skip_group_check=True)
                    last.then_inc(s_gat, 1)

                def sums(s):
                    g = n0 + s
                    pe.wait_ge(s_msg, g + 1)
                    wait(pe, s_acc, g)
                    for k in range(CHUNKS):
                        last = pe.matmul(OP[:, 0:gat.A], SF[:, s % 4, k, :], MSG[:, s % 2, k, 0:gat.A],
                                         start=(k == 0), stop=(k == CHUNKS - 1))
                    last.then_inc(s_out, 1)

                for s in span(first, last_):
                    if gat is FFN and has(s + 1, first, last_):
                        masked_logits(s + 1)
                    if has(s, first, last_):
                        at_edges(s)
                    if gat is GNN and s % HALF == HALF - 1 and has(s + 1, first, last_):
                        maxima_back(s + 1)
                    if gat is GNN and has(s + 1, first, last_):
                        maxima(s + 1)
                    if has(s + 2, first, last_):
                        selection_t(s + 2)
                    if gat is GNN and s % HALF == HALF - 2 and has(s + 2, first, last_):
                        rows_of_logits(s + 2)
                    if has(s - 1, first, last_):
                        sums(s - 1)

            for r in range(2):
                project(0, 0, r)
            with pe.Fori(1, TILES // 2) as i:
                for r in range(2):
                    project(0, i, r)
            project(0, TILES // 2, 0)
            lists(0, G_BLOCKS)
            pe.wait_ge(s_rows, 3)
            pe.matmul(XP[:, 2, 0:TILES], ONES[:, :], CNT2[:, :], start=True, stop=True)
            pe.matmul(XP[:, 3, 0:TILES], UPPER[:, :], CNT2[:, :], start=True, stop=True).then_inc(s_rk, 1)
            steps(GNN, 0, True, False)
            with pe.Fori(1, G_ITERS - 1) as i:
                steps(GNN, i, False, False)
            steps(GNN, G_ITERS - 1, False, True)
            lists(G_BLOCKS, F_BLOCKS)
            for r in range(2):
                project(1, 0, r)
            with pe.Fori(1, TILES // 2) as i:
                for r in range(2):
                    project(1, i, r)
            project(1, TILES // 2, 0)
            steps(FFN, FFN.i0, True, False)
            with pe.Fori(FFN.i0 + 1, FFN.i1 - 1) as i:
                steps(FFN, i, False, False)
            steps(FFN, FFN.i1 - 1, False, True)

            pe.wait_ge(s_fw, 16 * 7)
            pe.wait_ge(s_acc, ALL_SLOTS)
            pe.transpose(GP[:, 0:EXPERTS * FB], B1R[:, :], IDF[0:16, 0:16]).then_inc(s_wt, 1)
            pe.wait_ge(s_ew, 16 * 9)
            XTA = ACC[:, :, :, :].rearrange("p t h c -> p (t h c)")[:, 0:2 * NODES_PAD].rearrange("p (k n) -> p k n", k=2)

            def expert(i, cols):
                start0 = isinstance(i, int) and i == 0
                for e in range(EXPERTS):
                    for f in range(FB):
                        m = (i * EXPERTS + e) * FB + f
                        if not (start0 and e == 0):
                            pe.wait_ge(s_hh, m - FB + 1)
                        for k in range(2):
                            last = pe.matmul(XP[:, f, 0:cols], W1S[:, e, k, f * P:(f + 1) * P],
                                             XTA[:, k, bass.ds(i * 4 * P, cols)], start=(k == 0), stop=(k == 1))
                        last.then_inc(s_h1, 1)
                    pe.wait_ge(s_hh, (i * EXPERTS + e + 1) * FB)
                    if e:
                        pe.wait_ge(s_add[e - 1], 4 * i + cols // P)
                    elif not start0:
                        pe.wait_ge(s_add[EXPERTS - 1], 4 * i)
                    for j in range(cols // P):
                        for f in range(FB):
                            last = pe.matmul((TR[0], TR[1], GP, OP)[j][:, 0:D], HH[:, f, j * P:(j + 1) * P], W2S[:, e, f, :],
                                             start=(f == 0), stop=(f == FB - 1))
                    last.then_inc(s_y, 1)
            pe.wait_ge(s_act, 2 + G_BLOCKS + F_BLOCKS + 1)
            expert(0, 512)
            with pe.Fori(1, TILES // 4) as i:
                expert(i, 512)
            expert(TILES // 4, P)

        @block.vector
        def _(dve):
            chain = [0]

            def link(ins):
                chain[0] += 1
                ins.then_inc(dv, 1)
                dve.wait_ge(dv, chain[0])

            def layer_stats(k):
                with dve.Fori(0, TILES) as t:
                    dve.bn_stats(STAT[:, t, :], X[:, t, :]).then_inc(s_stat, 1)
                dve.wait_ge(s_stat, TILES * (k + 1))
                link(dve.tensor_tensor(MEAN[:, :], STAT[:, :, 1], STAT[:, :, 4], ALU.add))
                link(dve.tensor_scalar(MEAN[:, :], MEAN[:, :], 0.5, None, ALU.mult))
                link(dve.tensor_tensor(VAR[:, :], STAT[:, :, 1], STAT[:, :, 4], ALU.subtract))
                link(dve.tensor_tensor(VAR[:, :], VAR[:, :], VAR[:, :], ALU.mult))
                link(dve.tensor_scalar(VAR[:, :], VAR[:, :], 0.25, LN_EPS, ALU.mult, ALU.add))
                link(dve.tensor_tensor(RSTD[:, :], STAT[:, :, 2], STAT[:, :, 5], ALU.add))
                link(dve.tensor_scalar(RSTD[:, :], RSTD[:, :], 1.0 / D, None, ALU.mult))
                link(dve.tensor_tensor(VAR[:, :], VAR[:, :], RSTD[:, :], ALU.add))
                dve.sem_inc(s_var, 1)
                dve.wait_ge(s_sd, k + 1)
                link(dve.reciprocal(RSTD[:, :], RSTD[:, :]))

            def project(phase, i, r):
                t = 2 * i + r
                tau = (TILES if phase else 0) + t
                first = isinstance(tau, int) and tau < 2
                if not first:
                    dve.wait_ge(s_pt, tau - 1)
                dve.tensor_scalar(XN[:, r, :], X[:, t, :] if isinstance(t, int) else X[:, bass.ds(t, 1), :].squeeze(1),
                                  MEAN[:, bass.ds(t, 1)], RSTD[:, bass.ds(t, 1)], ALU.subtract, ALU.mult).then_inc(s_xn, 1)

            def project_out(phase, i, r):
                t = 2 * i + r
                tau = (TILES if phase else 0) + t
                ps = (GP, OP)[r]
                if phase == 0:
                    dve.wait_ge(s_stg, tau + 1)
                    dve.tensor_scalar(ACC[:, bass.ds(t, 1), :, 0:G_CH].squeeze(1),
                                      STG[:, r, 0:D].rearrange("p (h c) -> p h c", h=G_HEADS), 1.0, None, ALU.mult)
                    dve.tensor_scalar(ELR[:, bass.ds(t, 1), :].squeeze(1), STG[:, r, D:D + 2 * G_HEADS], 1.0, None, ALU.mult).then_inc(s_ev, 1)
                else:
                    dve.wait_ge(s_pj, tau + 1)
                    dve.tensor_scalar(XTA[:, :, bass.ds(t * P, P)], XT[:, r, :, :], 1.0, None, ALU.mult)
                    dve.tensor_scalar(HF[:, bass.ds(t, 1), :].squeeze(1), ps[:, 0:16], 1.0, None, ALU.mult).then_inc(s_ev, 1)

            def projection(phase):
                for r in range(2):
                    project(phase, 0, r)
                for r in range(2):
                    project_out(phase, 0, r)
                with dve.Fori(1, TILES // 2) as i:
                    for r in range(2):
                        project(phase, i, r)
                    for r in range(2):
                        project_out(phase, i, r)
                project(phase, TILES // 2, 0)
                project_out(phase, TILES // 2, 0)
                dve.wait_ge(s_ev, TILES * (phase + 1))

            def logits(el, er, et, em, H):
                spl = et[:, :, H:H + (3 * H + 1) // 2].bitcast(bf16)
                t1, t2 = S16A[:, :, 0:H], S16B[:, :, 0:H]
                dve.tensor_copy(et[:, :, 0:H], el)
                link(dve.tensor_copy(spl[:, :, 0:H], el))
                link(dve.tensor_tensor(t1, el, spl[:, :, 0:H], ALU.subtract))
                link(dve.tensor_copy(spl[:, :, H:2 * H], t1))
                link(dve.tensor_tensor(t2, t1, spl[:, :, H:2 * H], ALU.subtract))
                link(dve.tensor_copy(spl[:, :, 2 * H:3 * H], t2))
                dve.tensor_copy(em[:, :, 0:H], er)
                link(dve.tensor_tensor(t1, el, er, ALU.add))
                link(dve.scalar_tensor_tensor(em[:, :, H:2 * H], t1, SLOPE, t1, ALU.mult, ALU.max))

            def slot_tiles(first, blocks, qcols):
                for b in range(blocks):
                    link(dve.tensor_scalar(SCOL[:, :], COL[:, :], float(P * b), None, ALU.add))
                    link(dve.tensor_scalar(JUNK[:, 0:TILES - 1], qcols, SCOL[:, 0:1], None, ALU.is_le, ALU.add,
                                           accum_out=TCOL[:, first + b:first + b + 1]))
                    if first == 0:
                        link(dve.tensor_tensor(CCOL[:, b:b + 1], SCOL[:, :], TCOL[:, b:b + 1], ALU.subtract))
                        link(dve.tensor_scalar(CIDX[:, b:b + 1], CCOL[:, b:b + 1], float(G_PAD_ROWS - 1), None, ALU.min))

            XTA = ACC[:, :, :, :].rearrange("p t h c -> p (t h c)")[:, 0:2 * NODES_PAD].rearrange("p (k n) -> p k n", k=2)

            dve.wait_ge(s_iota, 4)
            dve.memset(ONES[:, :], 1.0)
            dve.memset(CNT[:, :], 0.0)
            dve.memset(ZERO[:, :], 0.0)
            dve.memset(ACC[:, :, :, G_CH:G_CH + 1], 1.0)
            dve.memset(ACC2[:, :, :, F_CH:F_CH + 1], 1.0)
            dve.tensor_copy(COL[:, :], COLI[:, :])
            link(dve.tensor_copy(ROW[:, :], ROWI[:, :]))
            link(dve.tensor_scalar(IDF[:, :], ROW[:, :], COL[:, 0:1], None, ALU.is_equal))
            dve.tensor_copy(IDB[:, :], IDF[:, :])
            dve.tensor_scalar(UPPER[:, :], ROW[:, :], COL[:, 0:1], None, ALU.is_gt)
            dve.tensor_scalar(THR[:, :], ROW[:, 0:TILES], float(P), None, ALU.mult)
            for sel, H in ((SEL, G_HEADS), (SEL2, F_HEADS)):
                link(dve.tensor_reduce(JUNK[0:3 * H, 0:H], IDF[0:3 * H, 0:3 * H].rearrange("p (j h) -> p h j", h=H), AX.X, ALU.add))
                link(dve.tensor_copy(sel[:, :, :], JUNK[0:3 * H, 0:H].unsqueeze(2).to_broadcast([3 * H, H, P])))
            dve.wait_ge(s_w, 80)
            dve.memset(ADIAG[:, :, :], 0.0)
            HPB = P // G_CH
            link(dve.tensor_reduce(JUNK[:, 0:HPB], IDF[:, :].rearrange("p (h c) -> p h c", c=G_CH), AX.X, ALU.add))
            for b in range(2):
                for c in range(2):
                    o = c * G_HEADS + b * HPB
                    link(dve.tensor_scalar(ADIAG[:, b, o:o + HPB], JUNK[:, 0:HPB], ACOL[:, b, c:c + 1], None, ALU.mult))
            dve.sem_inc(s_rows, 1)

            dve.wait_ge(s_ge, 16)
            link(dve.tensor_copy(gdstf[0:HR, :], gdst[0:HR, :]))
            with dve.Fori(1, TILES) as t:
                dve.tensor_scalar(gjunk[0:HR, :], gdstf[0:HR, :], THR[0:HR, bass.ds(t, 1)], None, ALU.is_lt, ALU.add,
                                  accum_out=CNT[0:HR, bass.ds(t, 1)]).then_inc(s_hist, 1)
                dve.wait_ge(s_hist, t)
            dve.wait_ge(s_hist, TILES - 1)
            dve.sem_inc(s_rows, 1)

            dve.wait_ge(s_x, 16 * (-(-(TILES - 1) // 8) + 1))
            layer_stats(0)
            projection(0)
            logits(ELR[:, :, 0:8], ELR[:, :, 8:16], ET, EM, G_HEADS)
            dve.sem_inc(s_td2, 1)

            dve.wait_ge(s_rk, 1)
            link(dve.tensor_copy(QI[:, :], XP[:, 2, 0:TILES]))
            link(dve.tensor_scalar(QI[:, :], QI[:, :], 8, None, ALU.arith_shift_right))
            link(dve.tensor_copy(Q[:, :], QI[:, :]))
            link(dve.tensor_tensor(Q[:, :], Q[:, :], ROW[:, 0:TILES], ALU.add))
            slot_tiles(0, G_BLOCKS, Q[:, 1:TILES])
            dve.sem_inc(s_cidx, 1)
            for b in range(G_BLOCKS):
                dve.wait_ge(s_lrow, 32 * (b + 1))
                if b:
                    dve.wait_ge(s_ltr, b)
                link(dve.tensor_scalar(SCOL[:, :], TCOL[:, b:b + 1], float(P), None, ALU.mult))
                dve.tensor_copy(LF[:, 0, :], LI[:, 0, :])
                link(dve.tensor_copy(LF[:, 1, :], LI[:, 1, :]))
                dve.tensor_scalar(LF[:, 1, :], LF[:, 1, :], SCOL[:, 0:1], None, ALU.subtract).then_inc(s_lf, 1)

            dve.wait_ge(s_fe, 32)
            dve.wait_ge(s_iota, 5)
            dve.tensor_copy(fpos, ftmi)
            link(dve.tensor_scalar(REC[:, 0:EPP], fdst, 7, None, ALU.arith_shift_right))
            link(dve.tensor_copy(ftile, REC[:, 0:EPP]))
            link(dve.tensor_scalar(REC[:, 0:EPP], fdst, P - 1, None, ALU.bitwise_and))
            link(dve.tensor_copy(ftmp, REC[:, 0:EPP]))
            link(dve.tensor_copy(fscan, fsrc))
            link(dve.tensor_scalar(fscan, fscan, float(N_NODES - 1), None, ALU.min))
            link(dve.scalar_tensor_tensor(REC[:, 0:EPP], ftmp, float(SRC_SPAN), fscan, ALU.mult, ALU.add))
            with dve.Fori(0, TILES) as t:
                dve.tensor_scalar(fmask, ftile, ROW[:, bass.ds(t, 1)], None, ALU.is_equal, ALU.add,
                                  accum_out=CNT2[:, bass.ds(t, 1)]).then_inc(s_hist, 1)
                dve.wait_ge(s_hist, t + TILES)
            dve.wait_ge(s_hist, 2 * TILES - 1)
            dve.sem_inc(s_rows, 1)
            dve.wait_ge(s_rk, 2)
            link(dve.tensor_scalar(NSL[:, :], XP[:, 2, 0:TILES], float(SLOT - 1), None, ALU.add))
            link(dve.tensor_copy(QI[:, :], NSL[:, :]))
            link(dve.tensor_scalar(QI[:, :], QI[:, :], 8, None, ALU.arith_shift_right))
            link(dve.tensor_copy(NSL[:, :], QI[:, :]))
            link(dve.memset(ZERO[:, :], 0.0))
            link(dve.memset(SLOT0[:, 0:1], 0.0))
            link(dve.tensor_tensor_scan(SLOT0[:, 1:TILES + 1], NSL[:, :], ZERO[:, :], 0.0, ALU.add, ALU.add))
            link(dve.scalar_tensor_tensor(BASE[:, :], SLOT0[:, 0:TILES], float(SLOT), XP[:, 3, 0:TILES], ALU.mult, ALU.add))
            link(dve.tensor_scalar(BASE[:, :], BASE[:, :], -1.0, None, ALU.add))
            with dve.Fori(0, TILES) as t:
                dve.tensor_scalar(fmask, ftile, ROW[:, bass.ds(t, 1)], None, ALU.is_equal).then_inc(s_fpos, 1)
                dve.wait_ge(s_fpos, 5 * t + 1)
                dve.tensor_tensor_scan(fscan, fmask, ZERO[:, 0:1].to_broadcast([P, EPP]), BASE[:, bass.ds(t, 1)],
                                       ALU.add, ALU.add).then_inc(s_fpos, 1)
                dve.wait_ge(s_fpos, 5 * t + 2)
                dve.tensor_tensor(fscan, fscan, ftmi, ALU.subtract).then_inc(s_fpos, 1)
                dve.wait_ge(s_fpos, 5 * t + 3)
                dve.tensor_tensor(ftmp, fscan, fmask, ALU.mult).then_inc(s_fpos, 1)
                dve.wait_ge(s_fpos, 5 * t + 4)
                dve.tensor_tensor(fpos, fpos, ftmp, ALU.add).then_inc(s_fpos, 1)
            dve.wait_ge(s_fpos, 5 * TILES)
            link(dve.tensor_copy(POS[:, 0:EPP], fpos))
            slot_tiles(G_BLOCKS, F_BLOCKS, SLOT0[:, 1:TILES])
            dve.wait_ge(s_act, 2 + G_BLOCKS)
            dve.sem_inc(s_lcp, 1)

            def tile_of(slot):
                return dve.value_load(TROW[0:1, bass.ds(slot, 1)], min_val=0, max_val=TILES - 1)

            def steps(gat, it, first, last_):
                H, C, n0 = gat.H, gat.C, it * SPI
                acc, em = (ACC, EM) if gat is GNN else (ACC2, EM2)
                tiles = {s: tile_of(n0 + s) for s in range(0 if first else -2, 1)}

                def er(s):
                    return em[:, bass.ds(tiles[s], 1), 0:H].squeeze(1)

                def top(s):
                    return em[:, bass.ds(tiles[s], 1), H:2 * H].squeeze(1)

                def sums_of(s):
                    return acc[:, bass.ds(tiles[s], 1), :, :].squeeze(1)

                tmp = TMPA[:, 0:gat.A].rearrange("p (h c) -> p h c", c=C + 1)
                gp = GP[:, 0:CHUNKS * 2 * H].rearrange("p (k n) -> p k n", k=CHUNKS)
                base = 0 if gat is GNN else G_SLOTS

                def scan(s, stage):
                    n = 2 * it + (s + 1) // HALF
                    if gat is FFN or s % HALF != HALF - 1 or not has(s + 1, first, last_):
                        return
                    if stage == 0:
                        dve.wait_ge(s_dt, n + 1)
                        wait(dve, s_t2, n)
                        dve.tensor_tensor(NF[:, 1:SLOT], DT[:, 1:SLOT], DT[:, 0:SLOT - 1], ALU.not_equal).then_inc(s_nf, 1)
                    elif stage == 1:
                        dve.wait_ge(s_nf, n + 1)
                        dve.tensor_scalar(PEN, NF, -BIG, None, ALU.mult).then_inc(s_pen, 1)
                    elif stage == 2:
                        dve.wait_ge(s_pen, n + 1)
                        dve.tensor_tensor_scan(SCN, PEN[:, 0:SLOT], XP[0:HP, 0, 0:SLOT], -BIG, ALU.add, ALU.max).then_inc(s_scan, 1)
                    else:
                        dve.wait_ge(s_scan, n + 1)
                        dve.tensor_tensor(LAST, SCN, NF[:, 1:SLOT + 1], ALU.mult).then_inc(s_last, 1)

                for s in span(first, last_):
                    g, q = n0 + s, s % 2
                    has_a, has_b = has(s + 2, first, last_), has(s, first, last_)
                    has_c, has_e = has(s - 1, first, last_), has(s - 2, first, last_)
                    r = (s - 1) % 2
                    if has_b and gat is FFN:
                        dve.wait_ge(s_mask, g + 1 - base)
                        dve.tensor_reduce(U1[:, 0:H], XP[:, 2 * q:2 * q + CHUNKS, :].rearrange("p k (h n) -> p h k n", h=H),
                                          AX.XY, ALU.max).then_inc(s_red, 1)
                    if has_b:
                        dve.tensor_scalar(TB[:, q, 0:H], er(s), 1.0, None, ALU.mult).then_inc(s_er, 1)
                    if has_e:
                        dve.wait_ge(s_alpha, g - 1)
                        wait(dve, s_acc, g - 2)
                        dve.tensor_tensor(tmp, sums_of(s - 2), AL[:, (s - 2) % 4, 0:H].unsqueeze(2).to_broadcast([P, H, C + 1]),
                                          ALU.mult).then_inc(s_e1, 1)
                    if has_c:
                        dve.wait_ge(s_gat, g)
                        dve.tensor_tensor(L1[:, :, 0:H], R[:, (s - 1) % SPI, :, gat.EL:gat.EL + H], gp[:, :, 0:H],
                                          ALU.add).then_inc(s_c1, 1)
                    if has_b and gat is GNN:
                        dve.wait_ge(s_u, g + 1)
                        wait(dve, s_b2, g)
                        dve.scalar_tensor_tensor(U1[:, 0:H], XP[:, 2 + q, H:2 * H], BIG, er(s),
                                                 ALU.add, ALU.subtract).then_inc(s_b1, 1)
                    scan(s, 0)
                    if has_c:
                        dve.wait_ge(s_c1, g)
                        dve.scalar_tensor_tensor(L2[:, :, 0:H], L1[:, :, 0:H], SLOPE, L1[:, :, 0:H], ALU.mult, ALU.max).then_inc(s_c2, 1)
                    if has_b:
                        if gat is GNN:
                            dve.wait_ge(s_b1, g + 1)
                            dve.tensor_tensor(U2[:, 0:H], XP[:, 2 + q, 0:H], U1[:, 0:H], ALU.subtract).then_inc(s_b2, 1)
                        else:
                            dve.wait_ge(s_red, g + 1 - base)
                            dve.tensor_tensor(U2[:, 0:H], er(s), U1[:, 0:H], ALU.add).then_inc(s_b2, 1)
                    scan(s, 1)
                    if has_c:
                        dve.wait_ge(s_c2, g)
                        dve.tensor_tensor(L3[:, :, 0:H], L2[:, :, 0:H], gp[:, :, H:2 * H], ALU.subtract).then_inc(s_c3, 1)
                    if has_b:
                        dve.wait_ge(s_b2, g + 1)
                        dve.scalar_tensor_tensor(U3[:, 0:H], U2[:, 0:H], SLOPE, U2[:, 0:H], ALU.mult, ALU.max).then_inc(s_b3, 1)
                    if has_c:
                        dve.wait_ge(s_c3, g)
                        dve.tensor_scalar(LG[:, r, :, 0:H], L3[:, :, 0:H], 0.0, None, ALU.min).then_inc(s_lg, 1)
                    scan(s, 2)
                    if has_b:
                        dve.wait_ge(s_b3, g + 1)
                        wait(dve, s_mset, g)
                        dve.tensor_tensor(TB[:, q, H:2 * H], U3[:, 0:H], top(s), ALU.max).then_inc(s_b4, 1)
                    scan(s, 3)
                    if has_a:
                        if (s + 2) % HALF == 0:
                            dve.wait_ge(s_stage[(s + 2) // HALF % 2], staged(gat, it + (s + 2) // SPI))
                        wait(dve, s_out, g - 1)
                        dve.tensor_tensor(SF[:, (s + 2) % 4, :, :], ROW[:, :].unsqueeze(1).to_broadcast([P, CHUNKS, P]),
                                          DLB[:, (s + 2) // HALF % 2, (s + 2) % HALF, :].unsqueeze(2).to_broadcast([P, CHUNKS, P]),
                                          ALU.is_equal).then_inc(s_sf, 1)
                    if has_e:
                        dve.wait_ge(s_e1, g - 1)
                        dve.wait_ge(s_out, g - 1)
                        dve.tensor_tensor(sums_of(s - 2), tmp, OP[:, 0:gat.A].rearrange("p (h c) -> p h c", c=C + 1),
                                          ALU.add).then_inc(s_acc, 1)
                    if has_b:
                        dve.wait_ge(s_b4, g + 1)
                        dve.tensor_tensor(DLT[:, q, 0:H], top(s), TB[:, q, H:2 * H], ALU.subtract).then_inc(s_dlt, 1)
                    if has_c:
                        m = MSG[:, r, :, 0:gat.A].rearrange("p k (h c) -> p k h c", c=C + 1)
                        dve.wait_ge(s_wexp, g)
                        dve.tensor_tensor(m[:, :, :, 0:C], R[:, (s - 1) % SPI, :, 0:gat.HC].rearrange("p k (h c) -> p k h c", c=C),
                                          m[:, :, :, C:C + 1].to_broadcast([P, CHUNKS, H, C]), ALU.mult).then_inc(s_msg, 1)
                    if has_b:
                        dve.wait_ge(s_dlt, g + 1)
                        dve.tensor_scalar(top(s), TB[:, q, H:2 * H], 1.0, None, ALU.mult).then_inc(s_mset, 1)
                    if 0 <= s < SPI - 1:
                        tiles[s + 1] = tile_of(n0 + s + 1)

            def loop(gat):
                steps(gat, gat.i0, True, False)
                with dve.Fori(gat.i0 + 1, gat.i1 - 1) as i:
                    steps(gat, i, False, False)
                steps(gat, gat.i1 - 1, False, True)

            dve.memset(NF[:, 0:1], 1.0)
            link(dve.memset(NF[:, SLOT:SLOT + 1], 1.0))
            loop(GNN)

            dve.wait_ge(s_x2, 16 * (TILES - 1) // 8)
            dve.wait_ge(s_acc, G_SLOTS)
            den = ELR[:, :, 0:8]
            link(dve.tensor_scalar(den, ACC[:, :, :, G_CH], DEN_EPS, None, ALU.add))
            link(dve.reciprocal(den, den))
            accv = ACC[:, :, :, 0:G_CH]
            link(dve.tensor_tensor(accv, accv, den.unsqueeze(3).to_broadcast([P, TILES, G_HEADS, G_CH]), ALU.mult))
            link(dve.tensor_tensor(X[:, :, :].rearrange("p t (h c) -> p t h c", h=G_HEADS), accv,
                                   X[:, :, :].rearrange("p t (h c) -> p t h c", h=G_HEADS), ALU.add))
            for b in range(F_BLOCKS):
                n = G_BLOCKS + b
                dve.wait_ge(s_flist, 16 * (b + 1))
                if b:
                    dve.wait_ge(s_ltr, n)
                link(dve.tensor_scalar(LI[:, 1, :], LI[:, 0, :], SRC_BITS, None, ALU.arith_shift_right))
                link(dve.tensor_copy(LF[:, 1, :], LI[:, 1, :]))
                link(dve.tensor_scalar(LI[:, 1, :], LI[:, 0, :], SRC_SPAN - 1, None, ALU.bitwise_and))
                dve.tensor_copy(LF[:, 0, :], LI[:, 1, :]).then_inc(s_lf, 1)
            dve.wait_ge(s_act, 2 + G_BLOCKS + F_BLOCKS)
            dve.sem_inc(s_lcp, 1)

            layer_stats(1)
            dve.wait_ge(s_fw, 16 * 7)
            projection(1)
            h44 = HF[:, :, :].rearrange("p t (h c) -> p t h c", c=F_CH)
            for j, o in ((0, 0), (1, 4)):
                link(dve.tensor_tensor(S16A[:, :, :], HF[:, :, :], ROWS16[:, j, :].unsqueeze(1).to_broadcast([P, TILES, 16]), ALU.mult))
                link(dve.tensor_reduce(ELR[:, :, o:o + 4], S16A[:, :, :].rearrange("p t (h c) -> p t h c", c=F_CH), AX.X, ALU.add))
            dve.tensor_copy(ACC2[:, :, :, 0:F_CH], h44)
            dve.tensor_copy(FT[:, :, 0:16], HF[:, :, :])
            logits(ELR[:, :, 0:4], ELR[:, :, 4:8], FT[:, :, 16:FFN.W], EM2, F_HEADS)
            dve.sem_inc(s_td2, 1)
            loop(FFN)

            dve.wait_ge(s_acc, ALL_SLOTS)
            den = ELR[:, :, 0:4]
            link(dve.tensor_scalar(den, ACC2[:, :, :, F_CH], DEN_EPS, None, ALU.add))
            link(dve.reciprocal(den, den))

            def row16(j):
                return ROWS16[:, j, :].unsqueeze(1).to_broadcast([P, TILES, 16])

            def col(v, n=16):
                return v.unsqueeze(2).to_broadcast([P, TILES, n])
            A16 = S16A[:, :, :]
            B16 = S16B[:, :, :]
            link(dve.tensor_tensor(A16.rearrange("p t (h c) -> p t h c", c=F_CH), ACC2[:, :, :, 0:F_CH],
                                   den.unsqueeze(3).to_broadcast([P, TILES, F_HEADS, F_CH]), ALU.mult))
            link(dve.tensor_tensor(A16, A16, row16(2), ALU.add))
            link(dve.tensor_reduce(S1[:, 0, :], A16, AX.X, ALU.add))
            link(dve.tensor_scalar(S1[:, 0, :], S1[:, 0, :], 1.0 / 16, None, ALU.mult))
            link(dve.tensor_tensor(A16, A16, col(S1[:, 0, :]), ALU.subtract))
            link(dve.tensor_tensor(B16, A16, A16, ALU.mult))
            link(dve.tensor_reduce(S1[:, 1, :], B16, AX.X, ALU.add))
            dve.tensor_scalar(VAR[:, :], S1[:, 1, :], 1.0 / 16, LN_EPS, ALU.mult, ALU.add).then_inc(s_var, 1)
            dve.wait_ge(s_sd, 3)
            link(dve.reciprocal(RSTD[:, :], RSTD[:, :]))
            link(dve.tensor_tensor(A16, A16, col(RSTD[:, :]), ALU.mult))
            link(dve.tensor_tensor(A16, A16, row16(3), ALU.mult))
            link(dve.tensor_tensor(A16, A16, row16(4), ALU.add))
            sc = S4[:, 3, :, :]
            link(dve.tensor_reduce(sc, A16.rearrange("p t (h c) -> p t c h", c=F_CH), AX.X, ALU.add))
            link(dve.tensor_scalar(sc, sc, 1.0 / F_HEADS, None, ALU.mult))
            rank = S4[:, 2, :, :]
            link(dve.memset(rank, 0.0))
            for e in range(EXPERTS):
                for o in range(EXPERTS):
                    if o != e:
                        link(dve.tensor_tensor(S1[:, 2, :], sc[:, :, o], sc[:, :, e], ALU.is_ge if o < e else ALU.is_gt))
                        link(dve.tensor_tensor(rank[:, :, e], rank[:, :, e], S1[:, 2, :], ALU.add))
            link(dve.tensor_scalar(rank, rank, 2.0, None, ALU.is_lt))
            link(dve.tensor_reduce(S1[:, 0, :], sc, AX.X, ALU.max))
            dve.tensor_tensor(S4[:, 0, :, :], sc, col(S1[:, 0, :], 4), ALU.subtract).then_inc(s_var, 1)
            dve.wait_ge(s_sd, 4)
            link(dve.tensor_tensor(G4[:, :, :], S4[:, 1, :, :], rank, ALU.mult))
            link(dve.tensor_reduce(S1[:, 1, :], G4[:, :, :], AX.X, ALU.add))
            link(dve.reciprocal(S1[:, 1, :], S1[:, 1, :]))
            link(dve.tensor_tensor(G4[:, :, :], G4[:, :, :], col(S1[:, 1, :], 4), ALU.mult))

            def combine(i, nt):
                if not (isinstance(i, int) and i == 0):
                    dve.wait_ge(s_st, 16 * i)
                for e in range(EXPERTS):
                    if e:
                        dve.wait_ge(s_bias[e - 1], 4 * i + nt)
                    for j in range(nt):
                        t = 4 * i + j
                        dve.scalar_tensor_tensor(OUTS[:, j, :], B2R[:, e, :], G4[:, bass.ds(t, 1), e:e + 1].squeeze(1),
                                                 OUTS[:, j, :] if e else X[:, bass.ds(t, 1), :].squeeze(1),
                                                 ALU.mult, ALU.add).then_inc(s_bias[e], 1)
                for e in range(EXPERTS):
                    dve.wait_ge(s_y, i * EXPERTS + e + 1)
                    dve.wait_ge(s_add[e - 1] if e else s_bias[EXPERTS - 1], 4 * i + nt)
                    for j in range(nt):
                        t = 4 * i + j
                        dve.scalar_tensor_tensor(OUTS[:, j, :], (TR[0], TR[1], GP, OP)[j][:, 0:D],
                                                 G4[:, bass.ds(t, 1), e:e + 1].squeeze(1), OUTS[:, j, :],
                                                 ALU.mult, ALU.add).then_inc(s_add[e], 1)
            dve.wait_ge(s_ew, 16 * 9)
            combine(0, 4)
            with dve.Fori(1, TILES // 4) as i:
                combine(i, 4)
            combine(TILES // 4, 1)


_INS = ['x', 'src', 'dst', 'L0_gnn_W', 'L0_gnn_a_left', 'L0_gnn_a_right', 'L0_ffn_W_gat', 'L0_ffn_att_src',
        'L0_ffn_att_dst', 'L0_ffn_b_gat', 'L0_ffn_ln_gamma', 'L0_ffn_ln_beta', 'L0_ffn_W1', 'L0_ffn_b1',
        'L0_ffn_W2', 'L0_ffn_b2', 'L0_ffn_edge_index']


def kernel(**inputs):
    import numpy as _np
    import concourse.bacc as _bacc
    from concourse import mybir as _mybir
    from concourse.bass_utils import run_bass_kernel_spmd as _run

    nc = _bacc.Bacc("TRN2", target_bir_lowering=False, num_devices=1)
    arrays, args = {}, []
    for name in _INS:
        a = _np.ascontiguousarray(inputs[name])
        arrays[f"in_{name}"] = a
        args.append(nc.dram_tensor(f"in_{name}", a.shape, _mybir.dt.from_np(a.dtype), kind="ExternalInput").ap())
    out = nc.dram_tensor("out_0", (N_NODES, D), _mybir.dt.float32, kind="ExternalOutput").ap()
    build(nc, *args, out)
    r = _run(nc, [arrays], core_ids=[0])
    return r.results[0]["out_0"]
```

```python
import concourse.bass as bass
from concourse import mybir
from contextlib import ExitStack

P = 128
N_NODES, D = 6250, 256
TILES = -(-N_NODES // P)
LAST_ROWS = N_NODES - (TILES - 1) * P
NODES_PAD = TILES * P
SLOT = 256
CHUNKS = SLOT // P
SPI = 8
HALF = SPI // 2
G_HEADS, G_CH = 8, 32
F_HEADS, F_CH = 4, 4
EXPERTS, HID = 4, 512
FB = HID // P
G_EDGES, F_EDGES = 100000, 131072
G_CHUNK_ROWS = -(-G_EDGES // SLOT)
G_ITERS = -(-(G_CHUNK_ROWS + TILES - 1) // SPI)
G_SLOTS = G_ITERS * SPI
G_PAD_ROWS = G_SLOTS - (TILES - 1)
G_PAD = G_PAD_ROWS * SLOT
F_ITERS = (F_EDGES + TILES * (SLOT - 1)) // SLOT // SPI
F_SLOTS = F_ITERS * SPI
assert F_SLOTS >= (F_EDGES + TILES * (SLOT - 1)) // SLOT
ALL_SLOTS = G_SLOTS + F_SLOTS
G_BLOCKS, F_BLOCKS = -(-G_SLOTS // P), -(-F_SLOTS // P)
EPP = F_EDGES // P
SC_ITER = -(-EPP // G_ITERS)
SC_HALF = (SC_ITER - SC_ITER // 2, SC_ITER // 2)
SC_COLS = SC_ITER * G_ITERS
LIST_LEN = F_BLOCKS * P * SLOT
TRASH = LIST_LEN
LIST_ALL = LIST_LEN + SC_COLS * P
SRC_BITS = 13
SRC_SPAN = 1 << SRC_BITS
FAR = 8000
BIG = 2.0 ** 100
SLOPE = 0.2
DEN_EPS = 1e-16
LN_EPS = 1e-5


class Gat:
    def __init__(self, heads, ch, first_iter, iters):
        self.H, self.C = heads, ch
        self.HC = heads * ch
        self.A = heads * (ch + 1)
        self.EL = self.HC
        self.SPL = self.HC + heads
        self.W = self.SPL + (3 * heads + 1) // 2
        self.i0, self.i1 = first_iter, first_iter + iters


GNN = Gat(G_HEADS, G_CH, 0, G_ITERS)
FFN = Gat(F_HEADS, F_CH, G_ITERS, F_ITERS)


def build(nc, x, src, dst, g_w, a_left, a_right, w_gat, att_src, att_dst, b_gat, ln_gamma, ln_beta,
          w1, b1, w2, b2, edge_index, out):
    f32, bf16, i32 = mybir.dt.float32, mybir.dt.bfloat16, mybir.dt.int32
    ALU, ACT, AX = mybir.AluOpType, mybir.ActivationFunctionType, mybir.AxisListType
    ctx = ExitStack()
    with ctx:
        def sb(name, shape, dt=f32):
            return ctx.enter_context(nc.sbuf_tensor(name, shape, dt))

        def pb(name, shape, dt=f32):
            return ctx.enter_context(nc.psum_tensor(name, shape, dt))

        def sem(name):
            return ctx.enter_context(nc.semaphore(name))

        def dram(name, shape, dt):
            return nc.dram_tensor(name, shape, dt, kind="Internal").ap()

        g_table = dram("g_table", (NODES_PAD, GNN.W), f32)
        f_table = dram("f_table", (NODES_PAD, FFN.W), f32)
        src_rows = dram("src_rows", (G_PAD_ROWS, SLOT), i32)
        dst_rows = dram("dst_rows", (G_PAD_ROWS, SLOT), i32)
        f_list = dram("f_list", (LIST_ALL, 1), i32)

        X = sb("X", [P, TILES, D])
        ACC = sb("ACC", [P, TILES, G_HEADS, G_CH + 1])
        EM = sb("EM", [P, TILES, 2 * G_HEADS])
        ACC2 = sb("ACC2", [P, TILES, F_HEADS, F_CH + 1])
        EM2 = sb("EM2", [P, TILES, 2 * F_HEADS])
        TROW = sb("TROW", [1, ALL_SLOTS], i32)
        ROW = sb("ROW", [P, P])
        ROWI = sb("ROWI", [P, P], i32)
        COL = sb("COL", [P, 1])
        COLI = sb("COLI", [P, 1], i32)
        IDF = sb("IDF", [P, P])
        IDB = sb("IDB", [P, P], bf16)
        ONES = sb("ONES", [P, P])
        UPPER = sb("UPPER", [P, P])
        CODE = 3 * F_HEADS + 15
        BIT = 3 * F_HEADS
        NODE_CODE = sb("NODE_CODE", [CODE, F_HEADS, P], bf16)
        NCOL = sb("NCOL", [P, F_HEADS, CODE])
        BITS = sb("BITS", [P, 8], i32)
        NBIT = sb("NBIT", [P, 8], i32)
        DINT = sb("DINT", [P, HALF * CHUNKS], i32)
        EBIT = sb("EBIT", [P, HALF * CHUNKS, 8], i32)
        ECODE = sb("ECODE", [P, 2, HALF, CHUNKS, CODE + 1], bf16)
        IDXB = sb("IDXB", [P, 2, HALF, CHUNKS], i32)
        POSB = sb("POSB", [P, 2, SC_HALF[0]], i32)
        RECB = sb("RECB", [P, 2, SC_HALF[0]], i32)
        DLB = sb("DLB", [P, 2, HALF, CHUNKS])
        TICK = sb("TICK", [P, 4])
        U1 = sb("U1", [P, G_HEADS])
        U2 = sb("U2", [P, G_HEADS])
        U3 = sb("U3", [P, G_HEADS])
        TB = sb("TB", [P, 2, 2 * G_HEADS])
        DLT = sb("DLT", [P, 2, G_HEADS])
        AL = sb("AL", [P, 4, G_HEADS])
        L1 = sb("L1", [P, CHUNKS, G_HEADS])
        L2 = sb("L2", [P, CHUNKS, G_HEADS])
        L3 = sb("L3", [P, CHUNKS, G_HEADS])
        LG = sb("LG", [P, 2, CHUNKS, G_HEADS])
        TMPA = sb("TMPA", [P, GNN.A])
        STAT = sb("STAT", [P, TILES, 6])
        MEAN = sb("MEAN", [P, TILES])
        VAR = sb("VAR", [P, TILES])
        RSTD = sb("RSTD", [P, TILES])
        ELR = sb("ELR", [P, TILES, 2 * G_HEADS])
        TCOLS = sb("TCOLS", [P, TILES * FFN.W])
        ET = TCOLS[:, 0:TILES * (GNN.W - GNN.HC)].rearrange("p (t w) -> p t w", t=TILES)
        FT = TCOLS[:, :].rearrange("p (t w) -> p t w", t=TILES)
        WREG = sb("WREG", [P, 2 * D + 2 * (D + 2 * G_HEADS)])
        WSB = WREG[:, 0:2 * D].rearrange("p (b d) -> p b d", b=2)
        WA = WREG[:, 2 * D:].rearrange("p (b d) -> p b d", b=2)
        S4 = WREG[:, 0:4 * TILES * 4].rearrange("p (a t e) -> p a t e", a=4, t=TILES)
        ACOL = sb("ACOL", [P, 2, 2])
        ADIAG = sb("ADIAG", [P, 2, 2 * G_HEADS])
        WGAT = sb("WGAT", [P, 2, F_HEADS * F_CH])
        HF = sb("HF", [P, TILES, F_HEADS * F_CH])
        ROWS16 = sb("ROWS16", [P, 5, F_HEADS * F_CH])
        B1R = sb("B1R", [EXPERTS * FB, P])
        B1C = sb("B1C", [P, EXPERTS * FB])
        G4 = sb("G4", [P, TILES, EXPERTS])
        S16A = sb("S16A", [P, TILES, 16])
        S16B = sb("S16B", [P, TILES, 16])
        S1 = sb("S1", [P, 4, TILES])
        LI = sb("LI", [P, 2, SLOT], i32)
        LF = sb("LF", [P, 2, SLOT])
        CNT = sb("CNT", [P, TILES])
        CNT2 = sb("CNT2", [P, TILES])
        Q = sb("Q", [P, TILES])
        QI = sb("QI", [P, TILES], i32)
        THR = sb("THR", [P, TILES])
        BASE = sb("BASE", [P, TILES])
        SLOT0 = sb("SLOT0", [P, TILES + 1])
        NSL = sb("NSL", [P, TILES])
        ZERO = sb("ZERO", [P, TILES])
        TCOL = sb("TCOL", [P, G_BLOCKS + F_BLOCKS])
        CCOL = sb("CCOL", [P, G_BLOCKS])
        CIDX = sb("CIDX", [P, G_BLOCKS], i32)
        SCOL = sb("SCOL", [P, 1])
        JUNK = sb("JUNK", [P, 64])

        sizes = [2 * ALL_SLOTS, 2 * ALL_SLOTS, SC_COLS, SC_COLS, SPI * CHUNKS * GNN.W, 4 * SLOT, SLOT, 4 * SLOT, SLOT,
                 2 * CHUNKS * GNN.A]
        LOOP = sb("LOOP", [P, sum(sizes)])
        at = [sum(sizes[:k]) for k in range(len(sizes) + 1)]
        part = [LOOP[:, at[k]:at[k + 1]] for k in range(len(sizes))]
        IDX = part[0].bitcast(i32).rearrange("p (g k) -> p g k", k=CHUNKS)
        DL = part[1].rearrange("p (g k) -> p g k", k=CHUNKS)
        POS = part[2].bitcast(i32)
        REC = part[3].bitcast(i32)
        R = part[4].rearrange("p (s k w) -> p s k w", s=SPI, k=CHUNKS)
        SF = part[5].rearrange("p (s k n) -> p s k n", s=4, k=CHUNKS)
        NE = part[6].bitcast(bf16).rearrange("p (s k n) -> p s k n", s=2, k=CHUNKS)
        ST = part[7].rearrange("p (s k n) -> p s k n", s=4, k=CHUNKS)
        ELT = part[8].bitcast(bf16)[0:CODE].rearrange("p (s k n) -> p s k n", s=2, k=CHUNKS)
        MSG = part[9].rearrange("p (s k a) -> p s k a", s=2, k=CHUNKS)
        HP = HALF * G_HEADS
        DT = S16A[:, :, :].rearrange("p t c -> p (t c)")[0:HP, 0:SLOT]
        NF = S16A[:, :, :].rearrange("p t c -> p (t c)")[0:HP, SLOT:2 * SLOT + 1]
        PEN = S16B[:, :, :].rearrange("p t c -> p (t c)")[0:HP, 0:SLOT + 1]
        SCN = S16B[:, :, :].rearrange("p t c -> p (t c)")[0:HP, SLOT + 1:2 * SLOT + 1]
        LAST = ELR[:, :, :].rearrange("p t c -> p (t c)")[0:HP, 0:SLOT]
        UB = HF[:, :, :].rearrange("p t c -> p (t c)")[:, 0:2 * CHUNKS * HALF * 2 * G_HEADS] \
            .rearrange("p (q k s v) -> p q k s v", q=2, k=CHUNKS, s=HALF)
        EH, DH = (HF[:, :, :].rearrange("p t c -> p (t c)")[:, 256 + 64 * j:320 + 64 * j]
                  .rearrange("p (k s h) -> p k s h", k=CHUNKS, s=HALF) for j in range(2))
        XN = part[5][:, 0:2 * D].rearrange("p (r d) -> p r d", r=2)
        XT = part[5][:, 2 * D:4 * D].rearrange("p (r k n) -> p r k n", r=2, k=2)
        STG = part[9][:, 0:2 * (D + 2 * G_HEADS)].rearrange("p (r d) -> p r d", r=2)
        w_at = [0, EXPERTS * 2 * HID, EXPERTS * FB * D, 2 * FB * 4 * P, 4 * D]
        w_at = [sum(w_at[:k + 1]) for k in range(len(w_at))]
        assert w_at[-1] <= at[-1]
        W1S = LOOP[:, w_at[0]:w_at[1]].rearrange("p (e k n) -> p e k n", e=EXPERTS, k=2)
        W2S = LOOP[:, w_at[1]:w_at[2]].rearrange("p (e f n) -> p e f n", e=EXPERTS, f=FB)
        HH = LOOP[:, w_at[2]:w_at[3]].rearrange("p (q f n) -> p q f n", q=2, f=FB)
        OUTS = LOOP[:, w_at[3]:w_at[4]].rearrange("p (j n) -> p j n", n=D)
        B2R = TCOLS[:, 0:EXPERTS * D].rearrange("p (e n) -> p e n", e=EXPERTS)

        assert 8 * EPP <= (TILES - 1) * D
        xflat = X[:, :, :].rearrange("p t d -> p (t d)")

        def edges_at(k):
            return xflat[:, k * EPP:(k + 1) * EPP]
        fsrc, ftrash = (edges_at(k).bitcast(i32) for k in (0, 1))
        fmask, fval, fscan = ([edges_at(k), edges_at(k + 1)] for k in (2, 4, 6))
        HR, HW = 125, G_EDGES // 125
        gdst = part[4][:, 0:HW].bitcast(i32)
        gdstf = part[4][:, HW:2 * HW]
        gjunk = part[4][:, 2 * HW:3 * HW]
        FILL = part[4][:, 3 * HW:3 * HW + LIST_LEN // P // 2].bitcast(i32)
        FT0 = 3 * HW + LIST_LEN // P // 2
        assert FT0 + EPP <= sizes[4] and EPP <= sizes[7] and EPP <= sizes[2]
        fdst = part[7][:, 0:EPP].bitcast(i32)
        ftile = part[4][:, FT0:FT0 + EPP]
        fjunk = part[2][:, 0:EPP]

        XP = pb("XP", [P, 4, 512])
        TR = [pb(f"TR{r}", [P, 512]) for r in range(2)]
        GP = pb("GP", [P, 512])
        OP = pb("OP", [P, 512])

        x_loaded = sem("x_loaded")
        x_reloaded = sem("x_reloaded")
        proj_w_loaded = sem("proj_w_loaded")
        rows_written = sem("rows_written")
        pads_set = sem("pads_set")
        g_dst_loaded = sem("g_dst_loaded")
        f_dst_loaded = sem("f_dst_loaded")
        f_src_loaded = sem("f_src_loaded")
        fill_set = sem("fill_set")
        list_filled = sem("list_filled")
        f_weights_loaded = sem("f_weights_loaded")
        e_weights_loaded = sem("e_weights_loaded")
        last_tile_zeroed = sem("last_tile_zeroed")
        indices_made = sem("indices_made")
        dve_done = sem("dve_done")
        dve_ready = sem("dve_ready")
        weights_turned = sem("weights_turned")
        copied = sem("copied")
        rows_named = sem("rows_named")
        rows_fetched = sem("rows_fetched")
        list_fetched = sem("list_fetched")
        list_unpacked = sem("list_unpacked")
        list_turned = sem("list_turned")
        lists_ready = sem("lists_ready")
        x_normalized = sem("x_normalized")
        tile_turned = sem("tile_turned")
        tile_copied = sem("tile_copied")
        projected = sem("projected")
        projection_staged = sem("projection_staged")
        projection_kept = sem("projection_kept")
        row_stats = sem("row_stats")
        tiles_counted = sem("tiles_counted")
        counts_summed = sem("counts_summed")
        table_written = [sem(f"table_written{k}") for k in range(2)]
        columns_ready = sem("columns_ready")
        table_ready = sem("table_ready")
        half_staged = [sem(f"half_staged{k}") for k in range(2)]
        scattered = [sem(f"scattered{k}") for k in range(2)]
        row_gathered = [sem(f"row_gathered{k}") for k in range(SPI)]
        tick = sem("tick")
        sel_ready = sem("sel_ready")
        sel16_ready = sem("sel16_ready")
        sel_turned = sem("sel_turned")
        sel_copied = sem("sel_copied")
        codes_copied = sem("codes_copied")
        node_logits = sem("node_logits")
        node_reduced = sem("node_reduced")
        no_edge_term = sem("no_edge_term")
        logit_max = sem("logit_max")
        logit_lrelu = sem("logit_lrelu")
        new_max = sem("new_max")
        dst_logit = sem("dst_logit")
        max_change = sem("max_change")
        max_kept = sem("max_kept")
        rescale_ready = sem("rescale_ready")
        at_edges_ready = sem("at_edges_ready")
        edge_sum = sem("edge_sum")
        edge_lrelu = sem("edge_lrelu")
        edge_shifted = sem("edge_shifted")
        edge_logit = sem("edge_logit")
        edge_weight = sem("edge_weight")
        messages = sem("messages")
        slot_sums = sem("slot_sums")
        sums_rescaled = sem("sums_rescaled")
        sums_added = sem("sums_added")
        hidden_psum = sem("hidden_psum")
        hidden_gelu = sem("hidden_gelu")
        expert_out = sem("expert_out")
        logits_turned = sem("logits_turned")
        dst_compared = [sem(f"dst_compared{k}") for k in range(2)]
        logits_packed = sem("logits_packed")
        dst_rows_copied = sem("dst_rows_copied")
        starts = sem("starts")
        starts_penalty = sem("starts_penalty")
        scanned = sem("scanned")
        run_maxima = sem("run_maxima")
        maxima_turned = sem("maxima_turned")
        maxima_copied = sem("maxima_copied")
        node_maxima = sem("node_maxima")
        out_stored = sem("out_stored")
        variance = sem("variance")
        act_answer = sem("act_answer")
        tile_mask = sem("tile_mask")
        tile_scan = sem("tile_scan")
        tile_places = sem("tile_places")
        places_added = sem("places_added")
        node_codes = sem("node_codes")
        node_codes_turned = sem("node_codes_turned")
        bits_set = sem("bits_set")
        dst_int = sem("dst_int")
        dst_bits = sem("dst_bits")
        dst_codes = sem("dst_codes")
        code_parts = sem("code_parts")
        bias_added = [sem(f"bias_added{k}") for k in range(EXPERTS)]
        output_added = [sem(f"output_added{k}") for k in range(EXPERTS)]

        block = ctx.enter_context(nc.Block())

        def wait(eng, semaphore, value):
            if not (isinstance(value, int) and value < 1):
                eng.wait_ge(semaphore, value)

        def span(first, last):
            return range(-2 if first else 0, SPI + (2 if last else 0))

        def staged(gat, i):
            return 64 * i + 64 if gat is GNN else 64 * G_ITERS + 32 * (i - G_ITERS) + 32

        def has(slot, first, last):
            return not (first and slot < 0) and not (last and slot >= SPI)

        def bank(n, cols):
            return XP[:, n, 0:cols]

        x_full = x[0:(TILES - 1) * P, :].rearrange("(t p) d -> p t d", p=P)

        @block.sync
        def _(sp):
            with nc.allow_non_contiguous_dma("small rows"):
                XL = 8
                for j in range(0, TILES - 1, XL):
                    sp.dma_start(X[:, j:j + XL, :], x_full[:, j:j + XL, :]).then_inc(x_loaded, 16)
                sp.wait_ge(last_tile_zeroed, 1)
                sp.dma_start(X[0:LAST_ROWS, TILES - 1, :], x[(TILES - 1) * P:N_NODES, :]).then_inc(x_loaded, 16)
                sp.dma_start(gdst[0:HR, :], dst.rearrange("(p n) -> p n", p=HR)).then_inc(g_dst_loaded, 16)
                e2 = edge_index.rearrange("a (p n) -> a p n", p=P)
                sp.dma_start(fdst, e2[1]).then_inc(f_dst_loaded, 16)
                sp.dma_start(WSB[:, :, :], g_w.rearrange("(b p) d -> p b d", p=P)).then_inc(proj_w_loaded, 16)
                for b in range(2):
                    for c, a in enumerate((a_left, a_right)):
                        sp.dma_start(ACOL[:, b, c:c + 1],
                                     a.rearrange("h (c one) -> (h c) one", one=1)[b * P:(b + 1) * P, :]).then_inc(proj_w_loaded, 16)
                for rows, a in ((src_rows, src), (dst_rows, dst)):
                    flat = rows.rearrange("a b -> (a b)")
                    sp.dma_start(flat[0:G_EDGES].rearrange("(a b) -> a b", a=16),
                                 a.rearrange("(a b) -> a b", a=16)).then_inc(rows_written, 16)
                sp.wait_ge(pads_set, 2)
                npad = (G_PAD - G_EDGES) // 32
                for k, rows in enumerate((src_rows, dst_rows)):
                    flat = rows.rearrange("a b -> (a b)")
                    sp.dma_start(flat[G_EDGES:G_PAD].rearrange("(a b) -> a b", a=32),
                                 LI[0:32, k, 0:npad]).then_inc(rows_written, 16)
                sp.wait_ge(fill_set, 1)
                for k in range(2):
                    sp.dma_start(f_list[k * LIST_LEN // 2:(k + 1) * LIST_LEN // 2, 0].rearrange("(p n) -> p n", p=P),
                                 FILL).then_inc(list_filled, 16)
                sp.dma_start(WGAT[:, :, :], w_gat.rearrange("(k p) n -> p k n", p=P)).then_inc(f_weights_loaded, 16)
                for j, a in enumerate((att_src.rearrange("h c -> (h c)"), att_dst.rearrange("h c -> (h c)"),
                                       b_gat, ln_gamma, ln_beta)):
                    sp.dma_start(ROWS16[:, j, :], a.partition_broadcast(P)).then_inc(f_weights_loaded, 16)
                sp.dma_start(B1R[:, :], b1.rearrange("e (f p) -> (e f) p", p=P)).then_inc(f_weights_loaded, 16)

                def table_rows(i, r):
                    sp.wait_ge(projection_staged, 2 * i + r + 1)
                    sp.dma_start(g_table[bass.ds(256 * i + P * r, P), 0:D], STG[:, r, 0:D]).then_inc(table_written[r], 16)
                with sp.Fori(0, TILES // 2) as i:
                    for r in range(2):
                        table_rows(i, r)
                table_rows(TILES // 2, 0)
                sp.wait_ge(x_normalized, TILES)
                sp.dma_start(fsrc, e2[0]).then_inc(f_src_loaded, 16)
                sp.wait_ge(columns_ready, 1)
                sp.dma_start(g_table.rearrange("(t p) w -> p t w", p=P)[:, :, D:GNN.W], ET[:, :, :]).then_inc(table_ready, 16)

                def stage(gat, i, h):
                    if gat is GNN:
                        if not (isinstance(i, int) and i == 0):
                            sp.wait_ge(scattered[h], 16 * SC_HALF[h] * i)
                        sp.dma_start(POSB[:, h, 0:SC_HALF[h]], POS[:, bass.ds(SC_ITER * i + h * SC_HALF[0], SC_HALF[h])]).then_inc(half_staged[h], 16)
                        sp.dma_start(RECB[:, h, 0:SC_HALF[h]], REC[:, bass.ds(SC_ITER * i + h * SC_HALF[0], SC_HALF[h])]).then_inc(half_staged[h], 16)
                    if not (isinstance(i, int) and i == 0):
                        for s in range(h * HALF, (h + 1) * HALF):
                            sp.wait_ge(row_gathered[s], 32 * i)
                        sp.wait_ge(dst_compared[h], 32 * i)
                    sp.dma_start(IDXB[:, h, :, :], IDX[:, bass.ds(SPI * i + HALF * h, HALF), :]).then_inc(half_staged[h], 16)
                    sp.dma_start(DLB[:, h, :, :], DL[:, bass.ds(SPI * i + HALF * h, HALF), :]).then_inc(half_staged[h], 16)

                sp.wait_ge(lists_ready, 1)
                for j in range(0, TILES - 1, XL):
                    sp.dma_start(X[:, j:j + XL, :], x_full[:, j:j + XL, :]).then_inc(x_reloaded, 16)
                for gat in (GNN, FFN):
                    if gat is FFN:
                        sp.wait_ge(scattered[0], 16 * SC_HALF[0] * G_ITERS)
                        sp.wait_ge(scattered[1], 16 * SC_HALF[1] * G_ITERS)
                        for b in range(F_BLOCKS):
                            if b:
                                sp.wait_ge(list_unpacked, G_BLOCKS + b)
                            sp.dma_start(LI[:, 0, :], f_list[b * P * SLOT:(b + 1) * P * SLOT, 0]
                                         .rearrange("(p n) -> p n", p=P)).then_inc(list_fetched, 16)
                        sp.wait_ge(columns_ready, 2)
                        sp.dma_start(f_table.rearrange("(t p) w -> p t w", p=P), FT[:, :, :]).then_inc(table_ready, 16)
                        sp.wait_ge(lists_ready, 2)
                    for h in range(2):
                        stage(gat, gat.i0, h)
                    with sp.Fori(gat.i0 + 1, gat.i1) as i:
                        for h in range(2):
                            stage(gat, i, h)

                sp.wait_ge(sums_added, ALL_SLOTS)
                for e in range(EXPERTS):
                    sp.dma_start(W1S[:, e, :, :], w1[e].rearrange("(k p) n -> p k n", p=P)).then_inc(e_weights_loaded, 16)
                    sp.dma_start(W2S[:, e, :, :], w2[e].rearrange("(f p) n -> p f n", p=P)).then_inc(e_weights_loaded, 16)
                sp.dma_start(B2R, b2.partition_broadcast(P)).then_inc(e_weights_loaded, 16)
                with sp.Fori(0, TILES // 4) as i:
                    sp.wait_ge(output_added[EXPERTS - 1], 4 * i + 4)
                    sp.dma_start(out[bass.ds(i * 4 * P, 4 * P), :].rearrange("(j p) d -> p j d", p=P), OUTS).then_inc(out_stored, 16)
                sp.wait_ge(output_added[EXPERTS - 1], TILES)
                sp.dma_start(out[(TILES - 1) * P:N_NODES, :], OUTS[0:LAST_ROWS, 0, :]).then_inc(out_stored, 16)
                sp.wait_ge(out_stored, 16 * (TILES // 4 + 1))

        @block.gpsimd
        def _(pool):
            pool.iota(ROWI[:, :], pattern=[[1, P]], base=0, channel_multiplier=0).then_inc(indices_made, 1)
            pool.iota(COLI[:, :], pattern=[[0, 1]], base=0, channel_multiplier=1).then_inc(indices_made, 1)
            pool.iota(POS[:, EPP:SC_COLS], pattern=[[1, SC_COLS - EPP]], base=TRASH + F_EDGES,
                      channel_multiplier=SC_COLS - EPP).then_inc(indices_made, 1)
            pool.memset(REC[:, EPP:SC_COLS], 0).then_inc(indices_made, 1)
            pool.memset(X[:, TILES - 1, :], 0.0).then_inc(last_tile_zeroed, 1)
            pool.memset(TICK[:, :], 0.0).then_inc(tick, 1)
            for b in range(8):
                pool.memset(BITS[:, b:b + 1], 1 << b).then_inc(bits_set, 1)
            pool.memset(LI[:, 0, 0:SLOT], 0).then_inc(pads_set, 1)
            pool.memset(LI[:, 1, 0:SLOT], FAR).then_inc(pads_set, 1)
            pool.memset(FILL, P * SRC_SPAN).then_inc(fill_set, 1)
            pool.wait_ge(rows_written, 64)
            pool.wait_ge(rows_named, 1)
            for b in range(G_BLOCKS):
                if b:
                    pool.wait_ge(list_unpacked, b)
                for k, rows in enumerate((src_rows, dst_rows)):
                    pool.indirect_dma_start(out=LI[:, k, :], out_offset=None, in_=rows,
                                            in_offset=bass.IndirectOffsetOnAxis(ap=CIDX[:, b:b + 1], axis=0)).then_inc(rows_fetched, 16)

            def half(gat, i, h):
                table = g_table if gat is GNN else f_table
                for pair in range(2):
                    first = pair * HALF // 2
                    pool.wait_ge(tick, 4 * i + 2 * h + pair + 1)
                    if pair == 0:
                        pool.wait_ge(half_staged[h], staged(gat, i))
                    if not (isinstance(i, int) and i == gat.i0):
                        pool.wait_ge(messages, SPI * (i - 1) + HALF * h + first + HALF // 2)
                    pool.tensor_tensor(TICK[:, 0:1], TICK[:, 1:2], TICK[:, 2:3], ALU.add).then_inc(tick, 1)
                    for s in range(first, first + HALF // 2):
                        for k in range(CHUNKS):
                            pool.indirect_dma_start(out=R[:, h * HALF + s, k, 0:gat.W], out_offset=None, in_=table,
                                                    in_offset=bass.IndirectOffsetOnAxis(ap=IDXB[:, h, s, k:k + 1], axis=0)
                                                    ).then_inc(row_gathered[h * HALF + s], 16)
                    for c in range(pair * (SC_HALF[0] // 2), (SC_HALF[h] if pair else SC_HALF[0] // 2) if gat is GNN else 0):
                        pool.indirect_dma_start(out=f_list, out_offset=bass.IndirectOffsetOnAxis(ap=POSB[:, h, c:c + 1], axis=0),
                                                in_=RECB[:, h, c:c + 1], in_offset=None).then_inc(scattered[h], 16)

            pool.wait_ge(x_normalized, TILES)
            pool.iota(ftrash, pattern=[[1, EPP]], base=TRASH + 1, channel_multiplier=EPP).then_inc(indices_made, 1)
            pool.wait_ge(list_filled, 32)
            for k, gat in enumerate((GNN, FFN)):
                if gat is GNN:
                    pool.wait_ge(table_written[0], 16 * (TILES // 2 + 1))
                    pool.wait_ge(table_written[1], 16 * (TILES // 2))
                pool.wait_ge(table_ready, 16 * (k + 1))
                for h in range(2):
                    half(gat, gat.i0, h)
                with pool.Fori(gat.i0 + 1, gat.i1) as i:
                    for h in range(2):
                        half(gat, i, h)

        @block.scalar
        def _(act):
            def list_copies(first, blocks):
                for b in range(blocks):
                    n = first + b
                    g0 = (0 if first == 0 else G_SLOTS) + P * b
                    w = min(P, (G_SLOTS if first == 0 else ALL_SLOTS) - g0)
                    act.wait_ge(list_turned, n + 1)
                    for k in range(CHUNKS):
                        act.activation(IDX[:, g0:g0 + w, k], TR[0][:, k * P:k * P + w], ACT.Copy)
                        act.activation(DL[:, g0:g0 + w, k], TR[1][:, k * P:k * P + w], ACT.Copy)
                    act.activation(TROW[0:1, g0:g0 + w], GP[0:1, 0:w], ACT.Copy).then_inc(copied, 1)

            def rstd(k):
                act.wait_ge(variance, k + 1)
                act.activation(RSTD[:, :], VAR[:, :], ACT.Sqrt).then_inc(act_answer, 1)

            def copy_turned(phase, t, r):
                tau = (TILES if phase else 0) + t
                act.wait_ge(tile_turned, tau + 1)
                wait(act, projected, tau - 1)
                if phase == 1:
                    act.wait_ge(projection_kept, tau - 1)
                act.activation(XT[:, r, :, :], TR[r][:, 0:2 * P].rearrange("p (k n) -> p k n", k=2), ACT.Copy).then_inc(tile_copied, 1)

            def stage_out(phase, i, r):
                t = 2 * i + r
                if phase == 0:
                    act.wait_ge(projected, t + 1)
                    wait(act, table_written[r], 16 * i)
                    wait(act, projection_kept, t - 1)
                    act.activation(STG[:, r, :], (GP, OP)[r][:, 0:D + 2 * G_HEADS], ACT.Copy).then_inc(projection_staged, 1)

            def projection(phase):
                def two(i):
                    copy_turned(phase, 2 * i + 1, 1)
                    stage_out(phase, i, 0)
                    copy_turned(phase, 2 * i + 2, 0)
                    stage_out(phase, i, 1)
                copy_turned(phase, 0, 0)
                two(0)
                with act.Fori(1, TILES // 2) as i:
                    two(i)
                stage_out(phase, TILES // 2, 0)

            def steps(gat, it, first, last):
                H, C, n0 = gat.H, gat.C, it * SPI
                for s in span(first, last):
                    g = n0 + s
                    if gat is GNN and s % HALF == HALF - 1 and has(s + 1, first, last):
                        n = 2 * it + (s + 1) // HALF
                        act.wait_ge(logits_turned, n + 1)
                        wait(act, starts, n)
                        act.activation(DT, XP[0:HP, 0, SLOT:2 * SLOT], ACT.Copy).then_inc(dst_rows_copied, 1)
                    if has(s - 1, first, last):
                        act.wait_ge(edge_logit, g)
                        wait(act, slot_sums, g - 2)
                        act.activation(MSG[:, (s - 1) % 2, :, 0:gat.A].rearrange("p k (h c) -> p k h c", c=C + 1)[:, :, :, C],
                                       LG[:, (s - 1) % 2, :, 0:H], ACT.Exp).then_inc(edge_weight, 1)
                    if gat is GNN and s % HALF == HALF - 2 and has(s + 2, first, last):
                        n, h = 2 * it + (s + 2) // HALF, (s + 2) // HALF % 2
                        wait(act, logits_turned, n)
                        for sl in range(h * HALF, h * HALF + HALF):
                            act.wait_ge(row_gathered[sl], it * 32 + 32 * (1 + (s + 2) // SPI))
                        act.activation(EH, R[:, h * HALF:(h + 1) * HALF, :, gat.EL:gat.EL + H].rearrange("p s k h -> p k s h"),
                                       ACT.Copy)
                        act.wait_ge(half_staged[h], staged(gat, it + (s + 2) // SPI))
                        act.activation(DH, DLB[:, h, :, :].rearrange("p s k -> p k s").unsqueeze(3).to_broadcast([P, CHUNKS, HALF, H]),
                                       ACT.Copy).then_inc(logits_packed, 1)
                    if gat is GNN and s % HALF == HALF - 1 and has(s + 1, first, last):
                        n = 2 * it + (s + 1) // HALF
                        act.wait_ge(maxima_turned, n + 1)
                        wait(act, node_maxima, 4 * (n - 1))
                        act.activation(UB[:, (s + 1) // HALF % 2, :, :, :],
                                       XP[:, 1, 0:P].rearrange("p (k s v) -> p k s v", k=CHUNKS, s=HALF),
                                       ACT.Copy).then_inc(maxima_copied, 1)
                    if has(s + 2, first, last):
                        q = s % 2
                        if gat is FFN:
                            act.wait_ge(row_gathered[(s + 2) % SPI], it * 32 + 32 * (1 + (s + 2) // SPI))
                            act.activation(ECODE[:, (s + 2) // HALF % 2, (s + 2) % HALF, :, 0:3 * H],
                                           R[:, (s + 2) % SPI, :, gat.SPL:gat.SPL + 3 * H // 2].bitcast(bf16), ACT.Copy).then_inc(code_parts, 1)
                            act.wait_ge(sel_ready, g + 3)
                            act.activation(NE[:, q, :, :], SF[:, (s + 2) % 4, :, :], ACT.Copy).then_inc(sel16_ready, 1)
                        act.wait_ge(sel_turned, g + 3)
                        if gat is FFN:
                            if not (first and s < 0):
                                act.wait_ge(node_logits, g + 1 - G_SLOTS)
                            act.activation(ELT[0:CODE, q, :, :],
                                           TR[q][0:CODE, 256:256 + P].bitcast(bf16).rearrange("p (k n) -> p k n", k=CHUNKS),
                                           ACT.Copy).then_inc(codes_copied, 1)
                        wait(act, at_edges_ready, g - 1)
                        if gat is GNN:
                            act.activation(ST[:, (s + 2) % 4, :, :], TR[q][:, 0:2 * P].rearrange("p (k n) -> p k n", k=CHUNKS),
                                           ACT.Copy).then_inc(sel_copied, 1)
                        else:
                            act.activation(ST[:, (s + 2) % 4, :, :], TR[q][:, 0:P].bitcast(bf16).rearrange("p (k n) -> p k n", k=CHUNKS),
                                           ACT.Copy).then_inc(sel_copied, 1)
                    if has(s, first, last):
                        act.wait_ge(max_change, g + 1)
                        wait(act, sums_added, g - 3)
                        act.activation(AL[:, s % 4, 0:H], DLT[:, s % 2, 0:H], ACT.Exp).then_inc(rescale_ready, 1)
            act.wait_ge(weights_turned, 1)
            for b in range(2):
                act.activation(WA[:, b, 0:D], bank(b, D), ACT.Copy)
            for b in range(2):
                act.activation(WA[:, b, D:D + 16], XP[:, b, D:D + 16], ACT.Copy).then_inc(copied, 1)
            rstd(0)
            projection(0)
            list_copies(0, G_BLOCKS)
            steps(GNN, 0, True, False)
            with act.Fori(1, G_ITERS - 1) as i:
                steps(GNN, i, False, False)
            steps(GNN, G_ITERS - 1, False, True)
            list_copies(G_BLOCKS, F_BLOCKS)
            rstd(1)
            projection(1)
            steps(FFN, FFN.i0, True, False)
            with act.Fori(FFN.i0 + 1, FFN.i1 - 1) as i:
                steps(FFN, i, False, False)
            steps(FFN, FFN.i1 - 1, False, True)
            rstd(2)
            act.wait_ge(variance, 4)
            act.activation(S4[:, 1, :, :], S4[:, 0, :, :], ACT.Exp).then_inc(act_answer, 1)
            act.wait_ge(weights_turned, 2)
            act.activation(B1C[:, :], GP[:, 0:EXPERTS * FB], ACT.Copy).then_inc(copied, 1)
            act.wait_ge(copied, 2 + G_BLOCKS + F_BLOCKS + 1)

            def hidden(i, cols):
                for e in range(EXPERTS):
                    for f in range(FB):
                        m = (i * EXPERTS + e) * FB + f
                        act.wait_ge(hidden_psum, m + 1)
                        if f == 0:
                            wait(act, expert_out, i * EXPERTS + e - 1)
                        act.activation(HH[:, e % 2, f, 0:cols], XP[:, f, 0:cols], ACT.Gelu,
                                       bias=B1C[:, e * FB + f:e * FB + f + 1]).then_inc(hidden_gelu, 1)
            hidden(0, 512)
            with act.Fori(1, TILES // 4) as i:
                hidden(i, 512)
            hidden(TILES // 4, P)

        @block.tensor
        def _(pe):
            pe.wait_ge(proj_w_loaded, 80)
            pe.wait_ge(dve_ready, 1)
            for kb in range(2):
                for ob in range(2):
                    pe.transpose(XP[:, kb, ob * P:(ob + 1) * P], WSB[:, ob, kb * P:(kb + 1) * P], IDF[:, :])
                for ob in range(2):
                    last = pe.matmul(XP[:, kb, D:D + 16], WSB[:, ob, kb * P:(kb + 1) * P], ADIAG[:, ob, :],
                                     start=(ob == 0), stop=(ob == 1), skip_group_check=True)
            last.then_inc(weights_turned, 1)
            pe.wait_ge(node_codes, 1)
            for h in range(F_HEADS):
                last = pe.transpose(TR[0][0:CODE, h * P:(h + 1) * P], NCOL[:, h, :], IDF[:, :])
            last.then_inc(node_codes_turned, 1)

            def lists(first, blocks):
                for b in range(blocks):
                    n = first + b
                    pe.wait_ge(list_unpacked, n + 1)
                    if n:
                        pe.wait_ge(copied, 2 + n)
                    for k in range(CHUNKS):
                        pe.transpose(TR[0][:, k * P:(k + 1) * P], LF[:, 0, k * P:(k + 1) * P], IDF[:, :])
                        pe.transpose(TR[1][:, k * P:(k + 1) * P], LF[:, 1, k * P:(k + 1) * P], IDF[:, :])
                    pe.transpose(GP[0:1, 0:P], TCOL[:, n:n + 1], IDF[:, :]).then_inc(list_turned, 1)

            def turn(phase, t, r):
                tau = (TILES if phase else 0) + t
                pe.wait_ge(x_normalized, tau + 1)
                wait(pe, tile_copied, tau - 1)
                for k in range(2):
                    last = pe.transpose(TR[r][:, k * P:(k + 1) * P], XN[:, r, k * P:(k + 1) * P], IDF[:, :])
                last.then_inc(tile_turned, 1)

            def product(phase, t, r):
                tau = (TILES if phase else 0) + t
                pe.wait_ge(tile_copied, tau + 1)
                wait(pe, projection_staged if phase == 0 else projection_kept, tau - 1)
                w = WA if phase == 0 else WGAT
                cols = D + 16 if phase == 0 else 16
                for k in range(2):
                    last = pe.matmul((GP, OP)[r][:, 0:cols], XT[:, r, k, :], w[:, k, :], start=(k == 0), stop=(k == 1))
                last.then_inc(projected, 1)

            def projection(phase):
                def two(i):
                    turn(phase, 2 * i + 1, 1)
                    product(phase, 2 * i, 0)
                    turn(phase, 2 * i + 2, 0)
                    product(phase, 2 * i + 1, 1)
                turn(phase, 0, 0)
                two(0)
                with pe.Fori(1, TILES // 2) as i:
                    two(i)
                product(phase, TILES - 1, 0)

            def steps(gat, it, first, last_):
                H, C, n0 = gat.H, gat.C, it * SPI

                def selection_t(s):
                    g, q = n0 + s, s % 2
                    pe.wait_ge(sel_ready, g + 1)
                    if s % HALF == HALF - 1:
                        pe.sem_inc(dst_compared[s // HALF % 2], 32)
                    wait(pe, sel_copied, g - 1)
                    if gat is FFN:
                        if not (first and s < 2):
                            pe.wait_ge(codes_copied, g - 1 - G_SLOTS)
                        pe.wait_ge(code_parts, g + 1 - G_SLOTS)
                        pe.wait_ge(dst_codes, 4 * (it - G_ITERS) + 2 * (s // HALF) + 2)
                        for k in range(CHUNKS):
                            pe.transpose(TR[q][0:CODE, 256 + k * 64:256 + (k + 1) * 64].bitcast(bf16),
                                         ECODE[:, s // HALF % 2, s % HALF, k, 0:CODE], IDB[:, :])
                        pe.wait_ge(sel16_ready, g + 1 - G_SLOTS)
                    for k in range(CHUNKS):
                        if gat is GNN:
                            last = pe.transpose(TR[q][:, k * P:(k + 1) * P], SF[:, s % 4, k, :], IDF[:, :])
                        else:
                            last = pe.transpose(TR[q][:, k * 64:(k + 1) * 64].bitcast(bf16), NE[:, q, k, :], IDB[:, :])
                    last.then_inc(sel_turned, 1)

                def masked_logits(s):
                    g, q = n0 + s, s % 2
                    pe.wait_ge(codes_copied, g + 1 - G_SLOTS)
                    if not (first and s < 2):
                        pe.wait_ge(node_reduced, g - 1 - G_SLOTS)
                    for k in range(CHUNKS):
                        o = XP[:, 2 * q + k, :].rearrange("p (h n) -> p h n", h=H)
                        for h in range(H):
                            last = pe.matmul(o[:, h, :], NODE_CODE[:, h, :], ELT[:, q, k, :],
                                             start=True, stop=True, skip_group_check=True)
                    last.then_inc(node_logits, 1)

                def rows_of_logits(s):
                    n, h = 2 * it + s // HALF, s // HALF % 2
                    pe.wait_ge(logits_packed, n + 1)
                    wait(pe, scanned, n)
                    wait(pe, dst_rows_copied, n)
                    for k in range(CHUNKS):
                        pe.transpose(XP[0:HP, 0, k * P:(k + 1) * P], EH[:, k, :, :].rearrange("p s h -> p (s h)"), IDF[:, :])
                    for k in range(CHUNKS):
                        last = pe.transpose(XP[0:HP, 0, SLOT + k * P:SLOT + (k + 1) * P],
                                            DH[:, k, :, :].rearrange("p s h -> p (s h)"), IDF[:, :])
                    last.then_inc(logits_turned, 1)

                def maxima_back(s):
                    n = 2 * it + s // HALF
                    pe.wait_ge(run_maxima, n + 1)
                    wait(pe, maxima_copied, n)
                    for k in range(CHUNKS):
                        o = XP[:, 1, k * 64:(k + 1) * 64].rearrange("p (s v) -> p s v", s=HALF)
                        pe.matmul(o[:, :, 0:H], LAST[:, k * P:(k + 1) * P], IDF[0:HP, 0:HP], start=True, stop=True, skip_group_check=True)
                        last = pe.matmul(o[:, :, H:2 * H], PEN[:, 1 + k * P:1 + (k + 1) * P], IDF[0:HP, 0:HP], start=True, stop=True, skip_group_check=True)
                    last.then_inc(maxima_turned, 1)

                def maxima(s):
                    g = n0 + s
                    pe.wait_ge(maxima_copied, 2 * it + s // HALF + 1)
                    pe.wait_ge(sel_ready, g + 1)
                    wait(pe, logit_max, g - 1)
                    for k in range(CHUNKS):
                        last = pe.matmul(XP[:, 2 + s % 2, 0:2 * H], SF[:, s % 4, k, :], UB[:, s // HALF % 2, k, s % HALF, :],
                                         start=(k == 0), stop=(k == CHUNKS - 1))
                    last.then_inc(node_maxima, 1)

                def at_edges(s):
                    g, q = n0 + s, s % 2
                    pe.wait_ge(new_max, g + 1)
                    pe.wait_ge(dst_logit, g + 1)
                    pe.wait_ge(sel_copied, g + 1)
                    wait(pe, edge_shifted, g)
                    for k in range(CHUNKS):
                        last = pe.matmul(GP[:, k * 2 * H:(k + 1) * 2 * H], ST[:, s % 4, k, :], TB[:, q, 0:2 * H],
                                         start=True, stop=True, skip_group_check=True)
                    last.then_inc(at_edges_ready, 1)

                def sums(s):
                    g = n0 + s
                    pe.wait_ge(messages, g + 1)
                    wait(pe, sums_added, g)
                    for k in range(CHUNKS):
                        last = pe.matmul(OP[:, 0:gat.A], SF[:, s % 4, k, :], MSG[:, s % 2, k, 0:gat.A],
                                         start=(k == 0), stop=(k == CHUNKS - 1))
                    last.then_inc(slot_sums, 1)

                for s in span(first, last_):
                    if gat is FFN and has(s + 1, first, last_):
                        masked_logits(s + 1)
                    if has(s, first, last_):
                        at_edges(s)
                    if gat is GNN and s % HALF == HALF - 1 and has(s + 1, first, last_):
                        maxima_back(s + 1)
                    if has(s + 2, first, last_) and s % HALF == HALF - 1:
                        selection_t(s + 2)
                    if gat is GNN and has(s + 1, first, last_):
                        maxima(s + 1)
                    if has(s + 2, first, last_) and s % HALF != HALF - 1:
                        selection_t(s + 2)
                    if gat is GNN and s % HALF == HALF - 2 and has(s + 2, first, last_):
                        rows_of_logits(s + 2)
                    if has(s - 1, first, last_):
                        sums(s - 1)

            projection(0)
            pe.wait_ge(dve_ready, 2)
            pe.matmul(XP[:, 1, 0:TILES], ONES[0:HR, :], CNT[0:HR, :], start=True, stop=True)
            pe.matmul(XP[:, 2, 0:TILES], ONES[:, :], CNT2[:, :], start=True, stop=True)
            pe.matmul(XP[:, 3, 0:TILES], UPPER[:, :], CNT2[:, :], start=True, stop=True).then_inc(counts_summed, 1)
            lists(0, G_BLOCKS)

            def add_places(t, r, first=False, last_=False):
                pe.wait_ge(tile_places, t + 1)
                for k in range(2):
                    last = pe.matmul(XP[:, k, :], IDF[:, :], fval[r][:, k * 512:(k + 1) * 512], start=first, stop=last_)
                last.then_inc(places_added, 1)
            pe.wait_ge(list_unpacked, G_BLOCKS)
            add_places(0, 0, first=True)
            with pe.Fori(0, TILES // 2 - 1) as i:
                add_places(2 * i + 1, 1)
                add_places(2 * i + 2, 0)
            add_places(TILES - 2, 1)
            add_places(TILES - 1, 0, last_=True)
            steps(GNN, 0, True, False)
            with pe.Fori(1, G_ITERS - 1) as i:
                steps(GNN, i, False, False)
            steps(GNN, G_ITERS - 1, False, True)
            lists(G_BLOCKS, F_BLOCKS)
            projection(1)
            steps(FFN, FFN.i0, True, False)
            with pe.Fori(FFN.i0 + 1, FFN.i1 - 1) as i:
                steps(FFN, i, False, False)
            steps(FFN, FFN.i1 - 1, False, True)

            pe.wait_ge(f_weights_loaded, 16 * 7)
            pe.wait_ge(sums_added, ALL_SLOTS)
            pe.transpose(GP[:, 0:EXPERTS * FB], B1R[:, :], IDF[0:16, 0:16]).then_inc(weights_turned, 1)
            pe.wait_ge(e_weights_loaded, 16 * 9)
            XTA = ACC[:, :, :, :].rearrange("p t h c -> p (t h c)")[:, 0:2 * NODES_PAD].rearrange("p (k n) -> p k n", k=2)

            def up(i, e, cols):
                for f in range(FB):
                    wait(pe, hidden_gelu, (i * EXPERTS + e - 1) * FB + f + 1)
                    for k in range(2):
                        last = pe.matmul(XP[:, f, 0:cols], W1S[:, e, k, f * P:(f + 1) * P],
                                         XTA[:, k, bass.ds(i * 4 * P, cols)], start=(k == 0), stop=(k == 1))
                    last.then_inc(hidden_psum, 1)

            def down(i, e, cols):
                pe.wait_ge(hidden_gelu, (i * EXPERTS + e + 1) * FB)
                wait(pe, output_added[e - 1 if e else EXPERTS - 1], 4 * i + (cols // P if e else 0))
                for j in range(cols // P):
                    for f in range(FB):
                        last = pe.matmul((TR[0], TR[1], GP, OP)[j][:, 0:D], HH[:, e % 2, f, j * P:(j + 1) * P], W2S[:, e, f, :],
                                         start=(f == 0), stop=(f == FB - 1))
                last.then_inc(expert_out, 1)

            def block_of_nodes(i, cols, next_cols):
                for e in range(EXPERTS):
                    if e < EXPERTS - 1:
                        up(i, e + 1, cols)
                    elif next_cols:
                        up(i + 1, 0, next_cols)
                    down(i, e, cols)
            pe.wait_ge(copied, 2 + G_BLOCKS + F_BLOCKS + 1)
            up(0, 0, 4 * P)
            block_of_nodes(0, 4 * P, 4 * P)
            with pe.Fori(1, TILES // 4 - 1) as i:
                block_of_nodes(i, 4 * P, 4 * P)
            block_of_nodes(TILES // 4 - 1, 4 * P, (TILES - TILES // 4 * 4) * P)
            block_of_nodes(TILES // 4, (TILES - TILES // 4 * 4) * P, 0)

        @block.vector
        def _(dve):
            chain = [0]

            def link(ins):
                chain[0] += 1
                ins.then_inc(dve_done, 1)
                dve.wait_ge(dve_done, chain[0])

            def layer_stats(k):
                with dve.Fori(0, TILES) as t:
                    dve.bn_stats(STAT[:, t, :], X[:, t, :]).then_inc(row_stats, 1)
                dve.wait_ge(row_stats, TILES * (k + 1))
                link(dve.tensor_tensor(MEAN[:, :], STAT[:, :, 1], STAT[:, :, 4], ALU.add))
                link(dve.tensor_scalar(MEAN[:, :], MEAN[:, :], 0.5, None, ALU.mult))
                link(dve.tensor_tensor(VAR[:, :], STAT[:, :, 1], STAT[:, :, 4], ALU.subtract))
                link(dve.tensor_tensor(VAR[:, :], VAR[:, :], VAR[:, :], ALU.mult))
                link(dve.tensor_scalar(VAR[:, :], VAR[:, :], 0.25, LN_EPS, ALU.mult, ALU.add))
                link(dve.tensor_tensor(RSTD[:, :], STAT[:, :, 2], STAT[:, :, 5], ALU.add))
                link(dve.tensor_scalar(RSTD[:, :], RSTD[:, :], 1.0 / D, None, ALU.mult))
                link(dve.tensor_tensor(VAR[:, :], VAR[:, :], RSTD[:, :], ALU.add))
                dve.sem_inc(variance, 1)
                dve.wait_ge(act_answer, k + 1)
                link(dve.reciprocal(RSTD[:, :], RSTD[:, :]))

            def normalize(phase, t, r):
                tau = (TILES if phase else 0) + t
                wait(dve, tile_turned, tau - 1)
                dve.tensor_scalar(XN[:, r, :], X[:, t, :] if isinstance(t, int) else X[:, bass.ds(t, 1), :].squeeze(1),
                                  MEAN[:, bass.ds(t, 1)], RSTD[:, bass.ds(t, 1)], ALU.subtract, ALU.mult).then_inc(x_normalized, 1)

            def project_out(phase, i, r):
                t = 2 * i + r
                tau = (TILES if phase else 0) + t
                ps = (GP, OP)[r]
                if phase == 0:
                    dve.wait_ge(projection_staged, tau + 1)
                    dve.tensor_scalar(ACC[:, bass.ds(t, 1), :, 0:G_CH].squeeze(1),
                                      STG[:, r, 0:D].rearrange("p (h c) -> p h c", h=G_HEADS), 1.0, None, ALU.mult)
                    dve.tensor_scalar(ELR[:, bass.ds(t, 1), :].squeeze(1), STG[:, r, D:D + 2 * G_HEADS], 1.0, None, ALU.mult).then_inc(projection_kept, 1)
                else:
                    dve.wait_ge(projected, tau + 1)
                    dve.tensor_scalar(XTA[:, :, bass.ds(t * P, P)], XT[:, r, :, :], 1.0, None, ALU.mult)
                    dve.tensor_scalar(HF[:, bass.ds(t, 1), :].squeeze(1), ps[:, 0:16], 1.0, None, ALU.mult).then_inc(projection_kept, 1)

            def count(t):
                wait(dve, tiles_counted, 2 * t - 1)
                dve.tensor_scalar(gjunk[0:HR, :], gdstf[0:HR, :], THR[0:HR, bass.ds(t, 1)], None, ALU.is_lt, ALU.add,
                                  accum_out=CNT[0:HR, bass.ds(t, 1)]).then_inc(tiles_counted, 1)
                wait(dve, tiles_counted, 2 * t)
                dve.tensor_scalar(fjunk, ftile, ROW[:, bass.ds(t, 1)], None, ALU.is_equal, ALU.add,
                                  accum_out=CNT2[:, bass.ds(t, 1)]).then_inc(tiles_counted, 1)

            def projection(phase):
                def tile(i, r, ahead=True):
                    if phase == 0:
                        count(2 * i + r)
                    project_out(phase, i, r)
                    if ahead:
                        normalize(phase, 2 * i + r + 2, r)
                for r in range(2):
                    normalize(phase, r, r)
                for r in range(2):
                    tile(0, r)
                with dve.Fori(1, TILES // 2 - 1) as i:
                    for r in range(2):
                        tile(i, r)
                tile(TILES // 2 - 1, 0)
                tile(TILES // 2 - 1, 1, ahead=False)
                tile(TILES // 2, 0, ahead=False)
                dve.wait_ge(projection_kept, TILES * (phase + 1))
                if phase == 0:
                    dve.wait_ge(tiles_counted, 2 * TILES)

            def logits(el, er, et, em, H):
                spl = et[:, :, H:H + (3 * H + 1) // 2].bitcast(bf16)
                t1, t2 = S16A[:, :, 0:H], S16B[:, :, 0:H]
                dve.tensor_copy(et[:, :, 0:H], el)
                link(dve.tensor_copy(spl[:, :, 0:H], el))
                link(dve.tensor_tensor(t1, el, spl[:, :, 0:H], ALU.subtract))
                link(dve.tensor_copy(spl[:, :, H:2 * H], t1))
                link(dve.tensor_tensor(t2, t1, spl[:, :, H:2 * H], ALU.subtract))
                link(dve.tensor_copy(spl[:, :, 2 * H:3 * H], t2))
                dve.tensor_copy(em[:, :, 0:H], er)
                link(dve.tensor_tensor(t1, el, er, ALU.add))
                link(dve.scalar_tensor_tensor(em[:, :, H:2 * H], t1, SLOPE, t1, ALU.mult, ALU.max))

            def slot_tiles(first, blocks, qcols):
                for b in range(blocks):
                    link(dve.tensor_scalar(SCOL[:, :], COL[:, :], float(P * b), None, ALU.add))
                    link(dve.tensor_scalar(JUNK[:, 0:TILES - 1], qcols, SCOL[:, 0:1], None, ALU.is_le, ALU.add,
                                           accum_out=TCOL[:, first + b:first + b + 1]))
                    if first == 0:
                        link(dve.tensor_tensor(CCOL[:, b:b + 1], SCOL[:, :], TCOL[:, b:b + 1], ALU.subtract))
                        link(dve.tensor_scalar(CIDX[:, b:b + 1], CCOL[:, b:b + 1], float(G_PAD_ROWS - 1), None, ALU.min))

            XTA = ACC[:, :, :, :].rearrange("p t h c -> p (t h c)")[:, 0:2 * NODES_PAD].rearrange("p (k n) -> p k n", k=2)

            dve.wait_ge(indices_made, 4)
            dve.memset(ONES[:, :], 1.0)
            dve.memset(CNT[:, :], 0.0)
            dve.memset(ZERO[:, :], 0.0)
            dve.memset(ACC[:, :, :, G_CH:G_CH + 1], 1.0)
            dve.memset(ACC2[:, :, :, F_CH:F_CH + 1], 1.0)
            dve.tensor_copy(COL[:, :], COLI[:, :])
            link(dve.tensor_copy(ROW[:, :], ROWI[:, :]))
            link(dve.tensor_scalar(IDF[:, :], ROW[:, :], COL[:, 0:1], None, ALU.is_equal))
            dve.tensor_copy(IDB[:, :], IDF[:, :])
            dve.tensor_scalar(UPPER[:, :], ROW[:, :], COL[:, 0:1], None, ALU.is_gt)
            dve.tensor_scalar(THR[:, :], ROW[:, 0:TILES], float(P), None, ALU.mult)
            dve.wait_ge(bits_set, 8)
            link(dve.memset(NCOL[:, :, :], 0.0))
            for h in range(F_HEADS):
                dve.memset(NCOL[:, h, 0:BIT].rearrange("p (j h) -> p j h", h=F_HEADS)[:, :, h], 1.0)
            dve.memset(NCOL[:, :, BIT + 7:BIT + 8], -BIG)
            link(dve.tensor_tensor(NBIT[:, :], COLI[:, 0:1].to_broadcast([P, 8]), BITS[:, :], ALU.bitwise_and))
            node_bits = NBIT[:, 0:7].unsqueeze(1).to_broadcast([P, F_HEADS, 7])
            dve.tensor_scalar(NCOL[:, :, BIT:BIT + 7], node_bits, 0.0, -BIG, ALU.is_equal, ALU.mult)
            link(dve.tensor_scalar(NCOL[:, :, BIT + 8:BIT + 15], node_bits, 0.0, -BIG, ALU.is_gt, ALU.mult))
            dve.sem_inc(node_codes, 1)
            dve.wait_ge(proj_w_loaded, 80)
            dve.memset(ADIAG[:, :, :], 0.0)
            HPB = P // G_CH
            link(dve.tensor_reduce(JUNK[:, 0:HPB], IDF[:, :].rearrange("p (h c) -> p h c", c=G_CH), AX.X, ALU.add))
            for b in range(2):
                for c in range(2):
                    o = c * G_HEADS + b * HPB
                    link(dve.tensor_scalar(ADIAG[:, b, o:o + HPB], JUNK[:, 0:HPB], ACOL[:, b, c:c + 1], None, ALU.mult))
            dve.sem_inc(dve_ready, 1)

            dve.wait_ge(node_codes_turned, 1)
            dve.tensor_copy(NODE_CODE[:, :, :], TR[0][0:CODE, :].rearrange("p (h n) -> p h n", h=F_HEADS))
            dve.wait_ge(g_dst_loaded, 16)
            dve.tensor_copy(gdstf[0:HR, :], gdst[0:HR, :])
            dve.wait_ge(f_dst_loaded, 16)
            link(dve.tensor_scalar(REC[:, 0:EPP], fdst, 7, None, ALU.arith_shift_right))
            link(dve.tensor_copy(ftile, REC[:, 0:EPP]))

            dve.wait_ge(x_loaded, 16 * (-(-(TILES - 1) // 8) + 1))
            layer_stats(0)
            projection(0)
            dve.sem_inc(dve_ready, 1)
            logits(ELR[:, :, 0:8], ELR[:, :, 8:16], ET, EM, G_HEADS)
            dve.sem_inc(columns_ready, 1)

            dve.wait_ge(counts_summed, 1)
            link(dve.tensor_copy(QI[:, :], XP[:, 1, 0:TILES]))
            link(dve.tensor_scalar(QI[:, :], QI[:, :], 8, None, ALU.arith_shift_right))
            link(dve.tensor_copy(Q[:, :], QI[:, :]))
            link(dve.tensor_tensor(Q[:, :], Q[:, :], ROW[:, 0:TILES], ALU.add))
            slot_tiles(0, G_BLOCKS, Q[:, 1:TILES])
            dve.sem_inc(rows_named, 1)
            for b in range(G_BLOCKS):
                dve.wait_ge(rows_fetched, 32 * (b + 1))
                if b:
                    dve.wait_ge(list_turned, b)
                link(dve.tensor_scalar(SCOL[:, :], TCOL[:, b:b + 1], float(P), None, ALU.mult))
                dve.tensor_copy(LF[:, 0, :], LI[:, 0, :])
                link(dve.tensor_copy(LF[:, 1, :], LI[:, 1, :]))
                dve.tensor_scalar(LF[:, 1, :], LF[:, 1, :], SCOL[:, 0:1], None, ALU.subtract).then_inc(list_unpacked, 1)

            dve.wait_ge(f_src_loaded, 16)
            dve.wait_ge(indices_made, 5)
            link(dve.tensor_scalar(REC[:, 0:EPP], fdst, P - 1, None, ALU.bitwise_and))
            link(dve.tensor_copy(fval[0], REC[:, 0:EPP]))
            link(dve.tensor_copy(fscan[0], fsrc))
            link(dve.tensor_scalar(fscan[0], fscan[0], float(N_NODES - 1), None, ALU.min))
            link(dve.scalar_tensor_tensor(REC[:, 0:EPP], fval[0], float(SRC_SPAN), fscan[0], ALU.mult, ALU.add))
            link(dve.tensor_scalar(NSL[:, :], XP[:, 2, 0:TILES], float(SLOT - 1), None, ALU.add))
            link(dve.tensor_copy(QI[:, :], NSL[:, :]))
            link(dve.tensor_scalar(QI[:, :], QI[:, :], 8, None, ALU.arith_shift_right))
            link(dve.tensor_copy(NSL[:, :], QI[:, :]))
            link(dve.memset(ZERO[:, :], 0.0))
            link(dve.memset(SLOT0[:, 0:1], 0.0))
            link(dve.tensor_tensor_scan(SLOT0[:, 1:TILES + 1], NSL[:, :], ZERO[:, :], 0.0, ALU.add, ALU.add))
            link(dve.scalar_tensor_tensor(BASE[:, :], SLOT0[:, 0:TILES], float(SLOT), XP[:, 3, 0:TILES], ALU.mult, ALU.add))

            def mask(t, r):
                dve.tensor_scalar(fmask[r], ftile, ROW[:, bass.ds(t, 1)], None, ALU.is_equal).then_inc(tile_mask, 1)

            def place(t, r, more=True):
                dve.wait_ge(tile_mask, t + 1)
                wait(dve, tile_places, t - 1)
                dve.tensor_tensor_scan(fscan[r], fmask[r], ZERO[:, 0:1].to_broadcast([P, EPP]), BASE[:, bass.ds(t, 1)],
                                       ALU.add, ALU.add).then_inc(tile_scan, 1)
                if more:
                    mask(t + 1, 1 - r)
                dve.wait_ge(tile_scan, t + 1)
                wait(dve, places_added, t - 1)
                dve.scalar_tensor_tensor(fval[r], ftile, ROW[:, bass.ds(t, 1)], fscan[r], ALU.is_equal, ALU.mult).then_inc(tile_places, 1)
            mask(0, 0)
            place(0, 0)
            place(1, 1)
            with dve.Fori(1, TILES // 2) as i:
                for r in range(2):
                    place(2 * i + r, r)
            place(TILES - 1, 0, more=False)
            dve.wait_ge(places_added, TILES)
            places = XP[:, 0:2, :].rearrange("p k n -> p (k n)")
            link(dve.scalar_tensor_tensor(fval[0], places, 0.0, ftrash, ALU.is_equal, ALU.mult))
            link(dve.tensor_tensor(fval[1], places, fval[0], ALU.add))
            link(dve.tensor_scalar(POS[:, 0:EPP], fval[1], -1.0, None, ALU.add))
            slot_tiles(G_BLOCKS, F_BLOCKS, SLOT0[:, 1:TILES])
            dve.wait_ge(copied, 2 + G_BLOCKS)
            dve.sem_inc(lists_ready, 1)

            def tile_of(slot):
                return dve.value_load(TROW[0:1, bass.ds(slot, 1)], min_val=0, max_val=TILES - 1)

            last_tiles = {j: dve.alloc_register(f"last_tile{-j}") for j in (-2, -1)}

            def steps(gat, it, first, last_):
                H, C, n0 = gat.H, gat.C, it * SPI
                acc, em = (ACC, EM) if gat is GNN else (ACC2, EM2)
                tiles = {}
                if not first:
                    tiles.update({j: dve.snap(last_tiles[j], min_val=0, max_val=TILES - 1) for j in (-2, -1)})

                def load_tile(s):
                    if s < SPI - 2:
                        tiles[s] = tile_of(n0 + s)
                    else:
                        dve.reg_load(last_tiles[s - SPI], TROW[0:1, bass.ds(n0 + s, 1)])
                        tiles[s] = dve.snap(last_tiles[s - SPI], min_val=0, max_val=TILES - 1)
                if gat is GNN:
                    load_tile(0)

                def er(s):
                    return em[:, bass.ds(tiles[s], 1), 0:H].squeeze(1)

                def top(s):
                    return em[:, bass.ds(tiles[s], 1), H:2 * H].squeeze(1)

                def sums_of(s):
                    return acc[:, bass.ds(tiles[s], 1), :, :].squeeze(1)

                tmp = TMPA[:, 0:gat.A].rearrange("p (h c) -> p h c", c=C + 1)
                gp = GP[:, 0:CHUNKS * 2 * H].rearrange("p (k n) -> p k n", k=CHUNKS)
                base = 0 if gat is GNN else G_SLOTS

                def scan(s, stage):
                    n = 2 * it + (s + 1) // HALF
                    if gat is FFN or s % HALF != HALF - 1 or not has(s + 1, first, last_):
                        return
                    if stage == 0:
                        dve.wait_ge(dst_rows_copied, n + 1)
                        wait(dve, maxima_turned, n)
                        dve.tensor_tensor(NF[:, 1:SLOT], DT[:, 1:SLOT], DT[:, 0:SLOT - 1], ALU.not_equal).then_inc(starts, 1)
                    elif stage == 1:
                        dve.wait_ge(starts, n + 1)
                        dve.tensor_scalar(PEN, NF, -BIG, None, ALU.mult).then_inc(starts_penalty, 1)
                    elif stage == 2:
                        dve.wait_ge(starts_penalty, n + 1)
                        dve.tensor_tensor_scan(SCN, PEN[:, 0:SLOT], XP[0:HP, 0, 0:SLOT], -BIG, ALU.add, ALU.max).then_inc(scanned, 1)
                    else:
                        dve.wait_ge(scanned, n + 1)
                        dve.tensor_tensor(LAST, SCN, NF[:, 1:SLOT + 1], ALU.mult).then_inc(run_maxima, 1)

                def codes(s, stage):
                    n, h = 2 * (it - G_ITERS) + (s + 2) // HALF, (s + 2) // HALF % 2
                    if gat is GNN or (s + 2) % HALF or not has(s + 2, first, last_):
                        return
                    code = ECODE[:, h, :, :, :].rearrange("p s k c -> p (s k) c")
                    if stage == 0:
                        dve.wait_ge(half_staged[h], staged(gat, it + (s + 2) // SPI))
                        wait(dve, dst_bits, n)
                        dve.tensor_scalar(DINT[:, :], DLB[:, h, :, :].rearrange("p s k -> p (s k)"), 1.0, None, ALU.mult).then_inc(dst_int, 1)
                    elif stage == 1:
                        dve.wait_ge(dst_int, n + 1)
                        wait(dve, dst_codes, 2 * n)
                        dve.tensor_tensor(EBIT[:, :, :], DINT[:, :].unsqueeze(2).to_broadcast([P, HALF * CHUNKS, 8]),
                                          BITS[:, :].unsqueeze(1).to_broadcast([P, HALF * CHUNKS, 8]), ALU.bitwise_and).then_inc(dst_bits, 1)
                    elif stage == 2:
                        dve.wait_ge(dst_bits, n + 1)
                        dve.wait_ge(sel_turned, n0 + s - 2)
                        dve.tensor_scalar(code[:, :, BIT:BIT + 8], EBIT[:, :, :], 0.0, None, ALU.is_gt).then_inc(dst_codes, 1)
                        dve.tensor_scalar(code[:, :, BIT + 8:BIT + 15], EBIT[:, :, 0:7], 0.0, None, ALU.is_equal).then_inc(dst_codes, 1)

                def node_maximum(s, stage):
                    g, q = n0 + s, s % 2
                    if stage == 0:
                        dve.wait_ge(node_maxima, g + 1)
                        wait(dve, logit_max, g)
                        dve.scalar_tensor_tensor(U1[:, 0:H], XP[:, 2 + q, H:2 * H], BIG, er(s),
                                                 ALU.add, ALU.subtract).then_inc(no_edge_term, 1)
                    elif stage == 1 and gat is GNN:
                        dve.wait_ge(no_edge_term, g + 1)
                        dve.tensor_tensor(U2[:, 0:H], XP[:, 2 + q, 0:H], U1[:, 0:H], ALU.subtract).then_inc(logit_max, 1)
                    elif stage == 1:
                        dve.wait_ge(node_reduced, g + 1 - base)
                        dve.tensor_tensor(U2[:, 0:H], er(s), U1[:, 0:H], ALU.add).then_inc(logit_max, 1)
                    elif stage == 2:
                        dve.wait_ge(logit_max, g + 1)
                        dve.scalar_tensor_tensor(U3[:, 0:H], U2[:, 0:H], SLOPE, U2[:, 0:H], ALU.mult, ALU.max).then_inc(logit_lrelu, 1)
                    else:
                        dve.wait_ge(logit_lrelu, g + 1)
                        wait(dve, max_kept, g)
                        dve.tensor_tensor(TB[:, q, H:2 * H], U3[:, 0:H], top(s), ALU.max).then_inc(new_max, 1)

                for s in span(first, last_):
                    g, q = n0 + s, s % 2
                    has_a, has_b = has(s + 2, first, last_), has(s, first, last_)
                    has_c, has_e = has(s - 1, first, last_), has(s - 2, first, last_)
                    r = (s - 1) % 2
                    if has_b and gat is FFN:
                        dve.wait_ge(node_logits, g + 1 - base)
                        dve.tensor_reduce(U1[:, 0:H], XP[:, 2 * q:2 * q + CHUNKS, :].rearrange("p k (h n) -> p h k n", h=H),
                                          AX.XY, ALU.max).then_inc(node_reduced, 1)
                    if gat is FFN:
                        if 0 <= s < SPI:
                            load_tile(s)
                    if has_b:
                        dve.tensor_scalar(TB[:, q, 0:H], er(s), 1.0, None, ALU.mult).then_inc(dst_logit, 1)
                    if has_e:
                        dve.wait_ge(rescale_ready, g - 1)
                        wait(dve, sums_added, g - 2)
                        dve.tensor_tensor(tmp, sums_of(s - 2), AL[:, (s - 2) % 4, 0:H].unsqueeze(2).to_broadcast([P, H, C + 1]),
                                          ALU.mult).then_inc(sums_rescaled, 1)
                    if has_c:
                        dve.wait_ge(at_edges_ready, g)
                        dve.tensor_tensor(L1[:, :, 0:H], R[:, (s - 1) % SPI, :, gat.EL:gat.EL + H], gp[:, :, 0:H],
                                          ALU.add).then_inc(edge_sum, 1)
                    if has_b:
                        node_maximum(s, 0 if gat is GNN else 1)
                    if has_c:
                        dve.wait_ge(edge_sum, g)
                        dve.scalar_tensor_tensor(L2[:, :, 0:H], L1[:, :, 0:H], SLOPE, L1[:, :, 0:H], ALU.mult, ALU.max).then_inc(edge_lrelu, 1)
                    if has_b:
                        node_maximum(s, 1 if gat is GNN else 2)
                    scan(s, 0)
                    codes(s, 0)
                    if has_c:
                        dve.wait_ge(edge_lrelu, g)
                        dve.tensor_tensor(L3[:, :, 0:H], L2[:, :, 0:H], gp[:, :, H:2 * H], ALU.subtract).then_inc(edge_shifted, 1)
                    if has_b:
                        node_maximum(s, 2 if gat is GNN else 3)
                    if has_c:
                        dve.wait_ge(edge_shifted, g)
                        dve.tensor_scalar(LG[:, r, :, 0:H], L3[:, :, 0:H], 0.0, None, ALU.min).then_inc(edge_logit, 1)
                    if has_b and gat is GNN:
                        node_maximum(s, 3)
                    scan(s, 1)
                    codes(s, 1)
                    if has_b:
                        dve.wait_ge(new_max, g + 1)
                        dve.tensor_tensor(DLT[:, q, 0:H], top(s), TB[:, q, H:2 * H], ALU.subtract).then_inc(max_change, 1)
                    scan(s, 2)
                    codes(s, 2)
                    if has_a:
                        if (s + 2) % HALF == 0:
                            dve.wait_ge(half_staged[(s + 2) // HALF % 2], staged(gat, it + (s + 2) // SPI))
                        wait(dve, slot_sums, g - 1)
                        dve.tensor_tensor(SF[:, (s + 2) % 4, :, :], ROW[:, :].unsqueeze(1).to_broadcast([P, CHUNKS, P]),
                                          DLB[:, (s + 2) // HALF % 2, (s + 2) % HALF, :].unsqueeze(2).to_broadcast([P, CHUNKS, P]),
                                          ALU.is_equal).then_inc(sel_ready, 1)
                    scan(s, 3)
                    if has_e:
                        dve.wait_ge(sums_rescaled, g - 1)
                        dve.wait_ge(slot_sums, g - 1)
                        dve.tensor_tensor(sums_of(s - 2), tmp, OP[:, 0:gat.A].rearrange("p (h c) -> p h c", c=C + 1),
                                          ALU.add).then_inc(sums_added, 1)
                    if has_c:
                        m = MSG[:, r, :, 0:gat.A].rearrange("p k (h c) -> p k h c", c=C + 1)
                        dve.wait_ge(edge_weight, g)
                        dve.tensor_tensor(m[:, :, :, 0:C], R[:, (s - 1) % SPI, :, 0:gat.HC].rearrange("p k (h c) -> p k h c", c=C),
                                          m[:, :, :, C:C + 1].to_broadcast([P, CHUNKS, H, C]), ALU.mult).then_inc(messages, 1)
                    if has_b:
                        dve.wait_ge(max_change, g + 1)
                        dve.tensor_scalar(top(s), TB[:, q, H:2 * H], 1.0, None, ALU.mult).then_inc(max_kept, 1)
                    if gat is GNN and 0 <= s < SPI - 1:
                        load_tile(s + 1)

            def loop(gat):
                steps(gat, gat.i0, True, False)
                with dve.Fori(gat.i0 + 1, gat.i1 - 1) as i:
                    steps(gat, i, False, False)
                steps(gat, gat.i1 - 1, False, True)

            dve.memset(NF[:, 0:1], 1.0)
            link(dve.memset(NF[:, SLOT:SLOT + 1], 1.0))
            loop(GNN)

            dve.wait_ge(x_reloaded, 16 * (TILES - 1) // 8)
            dve.wait_ge(sums_added, G_SLOTS)
            den = ELR[:, :, 0:8]
            link(dve.tensor_scalar(den, ACC[:, :, :, G_CH], DEN_EPS, None, ALU.add))
            link(dve.reciprocal(den, den))
            accv = ACC[:, :, :, 0:G_CH]
            link(dve.tensor_tensor(accv, accv, den.unsqueeze(3).to_broadcast([P, TILES, G_HEADS, G_CH]), ALU.mult))
            link(dve.tensor_tensor(X[:, :, :].rearrange("p t (h c) -> p t h c", h=G_HEADS), accv,
                                   X[:, :, :].rearrange("p t (h c) -> p t h c", h=G_HEADS), ALU.add))
            for b in range(F_BLOCKS):
                n = G_BLOCKS + b
                dve.wait_ge(list_fetched, 16 * (b + 1))
                if b:
                    dve.wait_ge(list_turned, n)
                link(dve.tensor_scalar(LI[:, 1, :], LI[:, 0, :], SRC_BITS, None, ALU.arith_shift_right))
                link(dve.tensor_copy(LF[:, 1, :], LI[:, 1, :]))
                link(dve.tensor_scalar(LI[:, 1, :], LI[:, 0, :], SRC_SPAN - 1, None, ALU.bitwise_and))
                dve.tensor_copy(LF[:, 0, :], LI[:, 1, :]).then_inc(list_unpacked, 1)
            dve.wait_ge(copied, 2 + G_BLOCKS + F_BLOCKS)
            dve.sem_inc(lists_ready, 1)

            layer_stats(1)
            dve.wait_ge(f_weights_loaded, 16 * 7)
            projection(1)
            h44 = HF[:, :, :].rearrange("p t (h c) -> p t h c", c=F_CH)
            for j, o in ((0, 0), (1, 4)):
                link(dve.tensor_tensor(S16A[:, :, :], HF[:, :, :], ROWS16[:, j, :].unsqueeze(1).to_broadcast([P, TILES, 16]), ALU.mult))
                link(dve.tensor_reduce(ELR[:, :, o:o + 4], S16A[:, :, :].rearrange("p t (h c) -> p t h c", c=F_CH), AX.X, ALU.add))
            dve.tensor_copy(ACC2[:, :, :, 0:F_CH], h44)
            dve.tensor_copy(FT[:, :, 0:16], HF[:, :, :])
            logits(ELR[:, :, 0:4], ELR[:, :, 4:8], FT[:, :, 16:FFN.W], EM2, F_HEADS)
            dve.sem_inc(columns_ready, 1)
            loop(FFN)

            dve.wait_ge(sums_added, ALL_SLOTS)
            den = ELR[:, :, 0:4]
            link(dve.tensor_scalar(den, ACC2[:, :, :, F_CH], DEN_EPS, None, ALU.add))
            link(dve.reciprocal(den, den))

            def row16(j):
                return ROWS16[:, j, :].unsqueeze(1).to_broadcast([P, TILES, 16])

            def col(v, n=16):
                return v.unsqueeze(2).to_broadcast([P, TILES, n])
            A16 = S16A[:, :, :]
            B16 = S16B[:, :, :]
            link(dve.tensor_tensor(A16.rearrange("p t (h c) -> p t h c", c=F_CH), ACC2[:, :, :, 0:F_CH],
                                   den.unsqueeze(3).to_broadcast([P, TILES, F_HEADS, F_CH]), ALU.mult))
            link(dve.tensor_tensor(A16, A16, row16(2), ALU.add))
            link(dve.tensor_reduce(S1[:, 0, :], A16, AX.X, ALU.add))
            link(dve.tensor_scalar(S1[:, 0, :], S1[:, 0, :], 1.0 / 16, None, ALU.mult))
            link(dve.tensor_tensor(A16, A16, col(S1[:, 0, :]), ALU.subtract))
            link(dve.tensor_tensor(B16, A16, A16, ALU.mult))
            link(dve.tensor_reduce(S1[:, 1, :], B16, AX.X, ALU.add))
            dve.tensor_scalar(VAR[:, :], S1[:, 1, :], 1.0 / 16, LN_EPS, ALU.mult, ALU.add).then_inc(variance, 1)
            dve.wait_ge(act_answer, 3)
            link(dve.reciprocal(RSTD[:, :], RSTD[:, :]))
            link(dve.tensor_tensor(A16, A16, col(RSTD[:, :]), ALU.mult))
            link(dve.tensor_tensor(A16, A16, row16(3), ALU.mult))
            link(dve.tensor_tensor(A16, A16, row16(4), ALU.add))
            sc = S4[:, 3, :, :]
            link(dve.tensor_reduce(sc, A16.rearrange("p t (h c) -> p t c h", c=F_CH), AX.X, ALU.add))
            link(dve.tensor_scalar(sc, sc, 1.0 / F_HEADS, None, ALU.mult))
            rank = S4[:, 2, :, :]
            link(dve.memset(rank, 0.0))
            for e in range(EXPERTS):
                for o in range(EXPERTS):
                    if o != e:
                        link(dve.tensor_tensor(S1[:, 2, :], sc[:, :, o], sc[:, :, e], ALU.is_ge if o < e else ALU.is_gt))
                        link(dve.tensor_tensor(rank[:, :, e], rank[:, :, e], S1[:, 2, :], ALU.add))
            link(dve.tensor_scalar(rank, rank, 2.0, None, ALU.is_lt))
            link(dve.tensor_reduce(S1[:, 0, :], sc, AX.X, ALU.max))
            dve.tensor_tensor(S4[:, 0, :, :], sc, col(S1[:, 0, :], 4), ALU.subtract).then_inc(variance, 1)
            dve.wait_ge(act_answer, 4)
            link(dve.tensor_tensor(G4[:, :, :], S4[:, 1, :, :], rank, ALU.mult))
            link(dve.tensor_reduce(S1[:, 1, :], G4[:, :, :], AX.X, ALU.add))
            link(dve.reciprocal(S1[:, 1, :], S1[:, 1, :]))
            link(dve.tensor_tensor(G4[:, :, :], G4[:, :, :], col(S1[:, 1, :], 4), ALU.mult))

            def combine(i, nt):
                if not (isinstance(i, int) and i == 0):
                    dve.wait_ge(out_stored, 16 * i)
                for e in range(EXPERTS):
                    if e:
                        dve.wait_ge(bias_added[e - 1], 4 * i + nt)
                    for j in range(nt):
                        t = 4 * i + j
                        dve.scalar_tensor_tensor(OUTS[:, j, :], B2R[:, e, :], G4[:, bass.ds(t, 1), e:e + 1].squeeze(1),
                                                 OUTS[:, j, :] if e else X[:, bass.ds(t, 1), :].squeeze(1),
                                                 ALU.mult, ALU.add).then_inc(bias_added[e], 1)
                for e in range(EXPERTS):
                    dve.wait_ge(expert_out, i * EXPERTS + e + 1)
                    dve.wait_ge(output_added[e - 1] if e else bias_added[EXPERTS - 1], 4 * i + nt)
                    for j in range(nt):
                        t = 4 * i + j
                        dve.scalar_tensor_tensor(OUTS[:, j, :], (TR[0], TR[1], GP, OP)[j][:, 0:D],
                                                 G4[:, bass.ds(t, 1), e:e + 1].squeeze(1), OUTS[:, j, :],
                                                 ALU.mult, ALU.add).then_inc(output_added[e], 1)
            dve.wait_ge(e_weights_loaded, 16 * 9)
            combine(0, 4)
            with dve.Fori(1, TILES // 4) as i:
                combine(i, 4)
            combine(TILES // 4, 1)


_INS = ['x', 'src', 'dst', 'L0_gnn_W', 'L0_gnn_a_left', 'L0_gnn_a_right', 'L0_ffn_W_gat', 'L0_ffn_att_src',
        'L0_ffn_att_dst', 'L0_ffn_b_gat', 'L0_ffn_ln_gamma', 'L0_ffn_ln_beta', 'L0_ffn_W1', 'L0_ffn_b1',
        'L0_ffn_W2', 'L0_ffn_b2', 'L0_ffn_edge_index']


def kernel(**inputs):
    import numpy as _np
    import concourse.bacc as _bacc
    from concourse import mybir as _mybir
    from concourse.bass_utils import run_bass_kernel_spmd as _run

    nc = _bacc.Bacc("TRN2", target_bir_lowering=False, num_devices=1)
    arrays, args = {}, []
    for name in _INS:
        a = _np.ascontiguousarray(inputs[name])
        arrays[f"in_{name}"] = a
        args.append(nc.dram_tensor(f"in_{name}", a.shape, _mybir.dt.from_np(a.dtype), kind="ExternalInput").ap())
    out = nc.dram_tensor("out_0", (N_NODES, D), _mybir.dt.float32, kind="ExternalOutput").ap()
    build(nc, *args, out)
    r = _run(nc, [arrays], core_ids=[0])
    return r.results[0]["out_0"]
```
